# Optimizing a Trainium2 kernel written in Bass

```python
import numpy as np
import jax
import jax.numpy as jnp

def _softmax(x, axis=-1):
    return jax.nn.softmax(x, axis=axis)

def _gelu(x):
    return jax.nn.gelu(x, approximate=True)

def _silu(x):
    return jax.nn.silu(x)

def _sigmoid(x):
    return jax.nn.sigmoid(x)

def _layernorm(x, axis=-1, eps=1e-05):
    m = jnp.mean(x, axis=axis, keepdims=True)
    v = jnp.var(x, axis=axis, keepdims=True)
    return (x - m) / jnp.sqrt(v + eps)

def _scatter_add(tgt, idx, src, axis=0):
    return tgt.at[idx].add(src)

def _segment_sum(src, seg, n):
    return jax.ops.segment_sum(src, seg, n)
kernel_name = 'mk_gnn_resnorm_d4_gnn_r32_108233'

def setup_inputs(seed: int=0):
    np.random.seed(seed)
    _w = jnp.asarray

    def _rec_inputs():
        import jax
        import jax.numpy as jnp
        _gk = jax.random.key(seed)
        x = -0.0003713 + 1 * jax.random.normal(jax.random.fold_in(_gk, 1), (3125, 128), jnp.float32)
        src = jax.random.randint(jax.random.fold_in(_gk, 2), (100000,), 0, 3125, jnp.int32)
        dst = jax.random.randint(jax.random.fold_in(_gk, 3), (100000,), 0, 3125, jnp.int32)
        _o = jnp.argsort(dst, stable=True)
        src = src[_o]
        dst = dst[_o]
        edge_type_8 = jax.random.randint(jax.random.fold_in(_gk, 13), (100000,), 0, 8, jnp.int32)
        edge_weight = jax.random.uniform(jax.random.fold_in(_gk, 14), (100000,), jnp.float32, 0.0, 1)
        return (x, src, dst, edge_type_8, edge_weight)
    x, src, dst, edge_type_8, edge_weight = _rec_inputs()

    def _L0_gnn_setup():
        import jax, jax.numpy as jnp
        import numpy as np
        N_NODES = 3125
        key = jax.random.key(seed)
        k1, k2, k3, k4, k5, k6 = jax.random.split(key, 6)
        N, E, F_IN, F_OUT = (N_NODES, 50000, 128, 128)
        stdv = 1.0 / np.sqrt(F_OUT)
        return {'input_features': jax.random.normal(k1, (N, F_IN), dtype=jnp.float32), 'edge_row': jnp.sort(jax.random.randint(k2, (E,), 0, N, dtype=jnp.int32)), 'edge_col': jax.random.randint(k3, (E,), 0, N, dtype=jnp.int32), 'edge_val': jax.random.uniform(k4, (E,), dtype=jnp.float32), 'weight': jax.random.uniform(k5, (F_IN, F_OUT), minval=-stdv, maxval=stdv, dtype=jnp.float32), 'bias': jax.random.uniform(k6, (F_OUT,), minval=-stdv, maxval=stdv, dtype=jnp.float32)}
    _L0_gnn_all = _L0_gnn_setup()
    _L0_gnn_in = {k: v for k, v in _L0_gnn_all.items() if k in ('weight', 'bias')}
    del _L0_gnn_all

    def _L1_gnn_setup():
        import jax, jax.numpy as jnp
        import numpy as np
        LN_EPS = 1e-05
        key = jax.random.key(seed)
        k1, k2, k3, k4, k5 = jax.random.split(key, 5)
        N, E, D, R = (3125, 18750, 128, 8)
        entity_emb = jax.random.normal(k1, (N, D), dtype=jnp.float32)
        edge_index = jax.random.randint(k2, (2, E), 0, N)
        edge_type = jax.random.randint(k3, (E,), 0, R)
        W = jax.random.normal(k4, (R, D, D), dtype=jnp.float32) * (1.0 / np.sqrt(D))
        b = jax.random.normal(k5, (R, D), dtype=jnp.float32) * 0.01
        gamma = jnp.ones((D,), dtype=jnp.float32)
        beta = jnp.zeros((D,), dtype=jnp.float32)
        return {'entity_emb': entity_emb, 'edge_index': edge_index, 'edge_type': edge_type, 'W': W, 'b': b, 'gamma': gamma, 'beta': beta}
    _L1_gnn_all = _L1_gnn_setup()
    _L1_gnn_in = {k: v for k, v in _L1_gnn_all.items() if k in ('W', 'b', 'gamma', 'beta')}
    del _L1_gnn_all

    def _L2_gnn_setup():
        import jax, jax.numpy as jnp
        import numpy as np

        def _mean_agg(h, src, dst, num_nodes):
            sums = jax.ops.segment_sum(h[src], dst, num_segments=num_nodes)
            deg = jax.ops.segment_sum(jnp.ones_like(dst, dtype=h.dtype), dst, num_segments=num_nodes)
            return sums / jnp.maximum(deg, 1.0)[:, None]

        def _sage_conv(h, src, dst, W_self, W_neigh, b):
            h_neigh = _mean_agg(h, src, dst, h.shape[0])
            return h @ W_self + h_neigh @ W_neigh + b
        key = jax.random.key(seed)
        ks = jax.random.split(key, 10)
        N, E, D, H = (50000, 25000, 128, 128)
        x = jax.random.normal(ks[0], (N, D), dtype=jnp.float32)
        src = jax.random.randint(ks[1], (E,), 0, N)
        dst = jax.random.randint(ks[2], (E,), 0, N)
        s = 1.0 / np.sqrt(D)
        Wself1 = jax.random.uniform(ks[3], (D, H), jnp.float32, -s, s)
        Wneigh1 = jax.random.uniform(ks[4], (D, H), jnp.float32, -s, s)
        b1 = jnp.zeros((H,), jnp.float32)
        s2 = 1.0 / np.sqrt(H)
        Wself2 = jax.random.uniform(ks[5], (H, H), jnp.float32, -s2, s2)
        Wneigh2 = jax.random.uniform(ks[6], (H, H), jnp.float32, -s2, s2)
        b2 = jnp.zeros((H,), jnp.float32)
        return {'x': x, 'src': src, 'dst': dst, 'Wself1': Wself1, 'Wneigh1': Wneigh1, 'b1': b1, 'Wself2': Wself2, 'Wneigh2': Wneigh2, 'b2': b2}
    _L2_gnn_all = _L2_gnn_setup()
    _L2_gnn_in = {k: v for k, v in _L2_gnn_all.items() if k in ('Wself1', 'Wneigh1', 'b1', 'Wself2', 'Wneigh2', 'b2')}
    del _L2_gnn_all

    def _L3_gnn_setup():
        import jax, jax.numpy as jnp
        import numpy as np
        N, F_IN, F_OUT, H, E = (50000, 128, 32, 4, 50000)
        key = jax.random.key(seed)
        ks = jax.random.split(key, 8)
        features = jax.random.normal(ks[0], (N, F_IN), dtype=jnp.float32)
        edge_src = jax.random.randint(ks[1], (E,), 0, N, dtype=jnp.int32)
        edge_dst = jax.random.randint(ks[2], (E,), 0, N, dtype=jnp.int32)
        W_w = jax.random.normal(ks[3], (F_IN, F_OUT * H), dtype=jnp.float32) * 0.05
        W_b = jax.random.normal(ks[4], (F_OUT * H,), dtype=jnp.float32) * 0.05
        a_w = jax.random.normal(ks[5], (H, 2 * F_OUT), dtype=jnp.float32) * 0.05
        a_b = jax.random.normal(ks[6], (H,), dtype=jnp.float32) * 0.05
        return {'features': features, 'edge_src': edge_src, 'edge_dst': edge_dst, 'W_w': W_w, 'W_b': W_b, 'a_w': a_w, 'a_b': a_b}
    _L3_gnn_all = _L3_gnn_setup()
    _L3_gnn_in = {k: v for k, v in _L3_gnn_all.items() if k in ('W_w', 'W_b', 'a_w', 'a_b')}
    del _L3_gnn_all
    return {'x': x, 'src': src, 'dst': dst, 'edge_type_8': edge_type_8, 'edge_weight': edge_weight, 'L0_gnn_weight': _L0_gnn_in['weight'], 'L0_gnn_bias': _L0_gnn_in['bias'], 'L1_gnn_W': _L1_gnn_in['W'], 'L1_gnn_b': _L1_gnn_in['b'], 'L1_gnn_gamma': _L1_gnn_in['gamma'], 'L1_gnn_beta': _L1_gnn_in['beta'], 'L2_gnn_Wself1': _L2_gnn_in['Wself1'], 'L2_gnn_Wneigh1': _L2_gnn_in['Wneigh1'], 'L2_gnn_b1': _L2_gnn_in['b1'], 'L2_gnn_Wself2': _L2_gnn_in['Wself2'], 'L2_gnn_Wneigh2': _L2_gnn_in['Wneigh2'], 'L2_gnn_b2': _L2_gnn_in['b2'], 'L3_gnn_W_w': _L3_gnn_in['W_w'], 'L3_gnn_W_b': _L3_gnn_in['W_b'], 'L3_gnn_a_w': _L3_gnn_in['a_w'], 'L3_gnn_a_b': _L3_gnn_in['a_b']}

def reference(x, src, dst, edge_type_8, edge_weight, L0_gnn_weight, L0_gnn_bias, L1_gnn_W, L1_gnn_b, L1_gnn_gamma, L1_gnn_beta, L2_gnn_Wself1, L2_gnn_Wneigh1, L2_gnn_b1, L2_gnn_Wself2, L2_gnn_Wneigh2, L2_gnn_b2, L3_gnn_W_w, L3_gnn_W_b, L3_gnn_a_w, L3_gnn_a_b):
    import jax
    import jax.numpy as jnp

    def _L0_gnn_ref(input_features, edge_row, edge_col, edge_val, weight, bias):
        import jax, jax.numpy as jnp
        import numpy as np
        N_NODES = 3125
        support = jnp.matmul(input_features, weight)
        msgs = edge_val[:, None] * support[edge_col]
        output = jax.ops.segment_sum(msgs, edge_row, num_segments=N_NODES)
        return output + bias

    def _L1_gnn_ref(entity_emb, edge_index, edge_type, W, b, gamma, beta):
        import jax, jax.numpy as jnp
        import numpy as np
        LN_EPS = 1e-05
        src = edge_index[0]
        dst = edge_index[1]
        H = jnp.einsum('nd,rhd->nrh', entity_emb, W)
        msg = H[src, edge_type] + b[edge_type]
        out = jnp.zeros_like(entity_emb).at[dst].add(msg)
        x = out + entity_emb
        mu = jnp.mean(x, axis=-1, keepdims=True)
        var = jnp.mean(jnp.square(x - mu), axis=-1, keepdims=True)
        return (x - mu) * jax.lax.rsqrt(var + LN_EPS) * gamma + beta

    def _L2_gnn_ref(x, src, dst, Wself1, Wneigh1, b1, Wself2, Wneigh2, b2):
        import jax, jax.numpy as jnp
        import numpy as np

        def _mean_agg(h, src, dst, num_nodes):
            sums = jax.ops.segment_sum(h[src], dst, num_segments=num_nodes)
            deg = jax.ops.segment_sum(jnp.ones_like(dst, dtype=h.dtype), dst, num_segments=num_nodes)
            return sums / jnp.maximum(deg, 1.0)[:, None]

        def _sage_conv(h, src, dst, W_self, W_neigh, b):
            h_neigh = _mean_agg(h, src, dst, h.shape[0])
            return h @ W_self + h_neigh @ W_neigh + b
        h = _sage_conv(x, src, dst, Wself1, Wneigh1, b1)
        h = jax.nn.relu(h)
        h = _sage_conv(h, src, dst, Wself2, Wneigh2, b2)
        return h

    def _L3_gnn_ref(features, edge_src, edge_dst, W_w, W_b, a_w, a_b):
        import jax, jax.numpy as jnp
        import numpy as np
        N, F_IN, F_OUT, H, E = (50000, 128, 32, 4, 50000)
        n = features.shape[0]
        h = a_w.shape[0]
        f_out = a_w.shape[1] // 2
        self_idx = jnp.arange(n, dtype=edge_src.dtype)
        src = jnp.concatenate([edge_src, self_idx])
        dst = jnp.concatenate([edge_dst, self_idx])
        key = (features @ W_w + W_b).reshape(n, h, f_out)
        a_dst = a_w[:, :f_out]
        a_src = a_w[:, f_out:]
        s_dst = jnp.einsum('nhf,hf->nh', key, a_dst)
        s_src = jnp.einsum('nhf,hf->nh', key, a_src)
        e = jax.nn.leaky_relu(s_dst[dst] + s_src[src] + a_b, negative_slope=0.2)
        m = jax.ops.segment_max(e, dst, num_segments=n)
        e_exp = jnp.exp(e - m[dst])
        denom = jax.ops.segment_sum(e_exp, dst, num_segments=n)
        alpha = e_exp / denom[dst]
        out = jax.ops.segment_sum(alpha[:, :, None] * key[src], dst, num_segments=n)
        return out.reshape(n, h * f_out)
    edge_index = jnp.stack([src, dst])
    x = _layernorm(x + _L0_gnn_ref(x, src, dst, edge_weight, L0_gnn_weight, L0_gnn_bias), axis=-1)
    x = _layernorm(x + _L1_gnn_ref(x, edge_index, edge_type_8, L1_gnn_W, L1_gnn_b, L1_gnn_gamma, L1_gnn_beta), axis=-1)
    x = _layernorm(x + _L2_gnn_ref(x, src, dst, L2_gnn_Wself1, L2_gnn_Wneigh1, L2_gnn_b1, L2_gnn_Wself2, L2_gnn_Wneigh2, L2_gnn_b2), axis=-1)
    x = _layernorm(x + _L3_gnn_ref(x, src, dst, L3_gnn_W_w, L3_gnn_W_b, L3_gnn_a_w, L3_gnn_a_b), axis=-1)
    return x

_drawn_inputs = setup_inputs


def setup_inputs(seed=0):
    import zlib

    import numpy as np

    out = dict(_drawn_inputs(seed))
    spreads = {'L1_gnn_gamma': (1.0, 0.2),
     'L1_gnn_beta': (0.0, 0.1),
     'L2_gnn_b1': (0.0, 0.1),
     'L2_gnn_b2': (0.0, 0.1)}
    factors = {'L1_gnn_b': 3.707, 'L3_gnn_a_w': 2.986, 'L3_gnn_a_b': 38.871}
    for name, (base, spread) in spreads.items():
        noise = np.random.default_rng([zlib.crc32(name.encode()), seed]).standard_normal(out[name].shape)
        drawn = base * np.exp(spread * noise) if base else spread * noise
        out[name] = jnp.asarray(drawn.astype(out[name].dtype))
    for name, factor in factors.items():
        out[name] = (out[name] * factor).astype(out[name].dtype)
    return out
```

```python
import concourse.bass as bass
from concourse import mybir
from contextlib import ExitStack

N, D, E, R, H = 3125, 128, 100000, 8, 4
P = 128
NB = -(-N // P)
NP = NB * P
TAIL = N - (NB - 1) * P
CH = -(-E // P)
STEPS = CH + NB - 1
HALF = 8
BODY = 2 * HALF
LOOPS = STEPS // BODY
REST = STEPS - LOOPS * BODY
HALVES = 2 * LOOPS + 1
QU = 4
QLOOPS = STEPS // (2 * QU)
QREST = STEPS - QLOOPS * 2 * QU
SPARE = P
assert QU < QREST < 2 * QU
G = -(-STEPS // P)
SLOTS = G * P
GB = 5
GROUPS = NB // GB
BIG = 1e30
EPS = 1e-5
FAR = float(E)
assert 0 < REST <= HALF and GROUPS * GB == NB and STEPS * P % P == 0


def gnn_kernel(nc, x, src, dst, etype, ew, w0, b0, w1, b1, gamma, beta, ws1, wn1, b21, ws2, wn2, b22,
               ww, wb, aw, ab, out):
    f32, i32, bf16 = mybir.dt.float32, mybir.dt.int32, mybir.dt.bfloat16
    ALU, ACT, AX = mybir.AluOpType, mybir.ActivationFunctionType, mybir.AxisListType
    ds = bass.ds

    ctx = ExitStack()
    with ctx:
        def sb(name, shape, dt=f32):
            return ctx.enter_context(nc.sbuf_tensor(name, shape, dt))

        def sem(name):
            return ctx.enter_context(nc.semaphore(name))

        def dram(name, shape, dt=f32):
            return nc.dram_tensor(name, shape, dt, kind="Internal").ap()

        chunk_rec = dram("chunk_rec", (SLOTS, 4 * P + 1))
        block_of_step = dram("block_of_step", (SLOTS,), i32)
        rel_rows = dram("rel_rows", (SLOTS, P))
        reset_flat = dram("reset_flat", (SLOTS * P,))
        src_rows = dram("src_rows", (SLOTS, P))
        part_sum = [dram(f"part_sum{k}", (NP + SPARE, D)) for k in range(2 * QU)]
        rel_tab = dram("rel_tab", (NP, R * D))
        node_tab = dram("node_tab", (NP, D))
        hid_tab = dram("hid_tab", (NP, D))
        key_tab = dram("key_tab", (NP, D))
        score_tab = dram("score_tab", (NP, H))
        score_flat = dram("score_flat", (H, SLOTS * P))
        prefix_tab = dram("prefix_tab", (STEPS * P, H))

        iota_row = sb("iota_row", [P, P])
        iota_part = sb("iota_part", [P, 1])
        step_no = sb("step_no", [P, G])
        block_base = sb("block_base", [P, NB])
        ident = sb("ident", [P, P])
        upto = sb("upto", [P, P])
        ones = sb("ones", [P, P])
        before = sb("before", [P, P])
        spare_row = sb("spare_row", [P, 1])
        zeros = sb("zeros", [P, 4 * P])
        prefix = sb("prefix", [P, STEPS, H])
        raw = prefix[:].rearrange("p x h -> p (x h)")[:, 0:3 * SLOTS].bitcast(i32).rearrange("p (f e) -> p f e", f=3)
        chunk_sb = sb("chunk_sb", [P, G, 4, P])
        step_rec = sb("step_rec", [P, G, 4 * P + 1])
        below = sb("below", [P, NB - 1])
        below_i = sb("below_i", [P, NB - 1], i32)
        last_step = sb("last_step", [P, NB - 1])
        step_block = sb("step_block", [P, G])
        step_block_i = sb("step_block_i", [P, G], i32)
        step_base = sb("step_base", [P, G])
        step_chunk = sb("step_chunk", [P, G], i32)
        rel_row = sb("rel_row", [P, G, P])
        valid = sb("valid", [P, G, P])
        invalid_pen = sb("invalid_pen", [P, G, P])
        reset_row = sb("reset_row", [P, G, P])
        tmp_row = sb("tmp_row", [P, G, P])
        block_row = sb("block_row", [1, SLOTS], i32)
        idx_src = sb("idx_src", [P, SLOTS], i32)
        idx_rel = sb("idx_rel", [P, SLOTS], i32)
        rel_col = sb("rel_col", [P, SLOTS])
        w_col = sb("w_col", [P, SLOTS])
        idx_slot = sb("idx_slot", [P, 2, HALF], i32)
        rows = sb("rows", [P, 2, HALF, D])
        onehot = sb("onehot", [P, 2, HALF, P])
        rel_bc = sb("rel_bc", [P, 2, HALF * P])
        dup = sb("dup", [P, QU])
        to_spare = sb("to_spare", [P, QU])
        onehot_t = sb("onehot_t", [P, 2, HALF * P])
        msg = sb("msg", [P, 2, HALF, D])
        prob = sb("prob", [P, 2, HALF, H])
        z_slot = sb("z_slot", [P, HALF, H])
        u_slot = sb("u_slot", [P, 2, HALF, H])
        srow = sb("srow", [P, 2, HALF, H])
        X = sb("X", [P, NB, D])
        Y = sb("Y", [P, NB, D])
        T = sb("T", [P, NB, D])
        nat_slot = sb("nat_slot", [P, GB, D])
        lhs_slot = sb("lhs_slot", [P, GB, D])
        hout = sb("hout", [P, 2, R * D])
        mean = sb("mean", [P, NB])
        var = sb("var", [P, NB])
        rstd = sb("rstd", [P, NB])
        deg = sb("deg", [P, NB])
        rdeg = sb("rdeg", [P, NB])
        has = sb("has", [P, NB])
        src_bc = hout[:, 0, :].rearrange("p (s e) -> p s e", s=2)
        W0, WS1, WN1, WS2, WN2, WW = (sb(n, [P, D]) for n in ("W0", "WS1", "WN1", "WS2", "WN2", "WW"))
        W1 = hout[:, 0, :].rearrange("p (r f) -> p r f", r=R)
        W1T = sb("W1T", [P, R * D])
        B0, GA, BE, B21, B22, WB = (sb(n, [P, D]) for n in ("B0", "GA", "BE", "B21", "B22", "WB"))
        B1 = sb("B1", [P, R * D])
        A_DST, A_SRC = sb("A_DST", [P, H, D // H]), sb("A_SRC", [P, H, D // H])
        AB = sb("AB", [P, H])
        edge_score = sb("edge_score", [P, SLOTS, H])
        score_row = chunk_sb[:].rearrange("p g f e -> p (g f e)").rearrange("p (h g e) -> p h g e", h=H, g=G)
        lanes = step_rec[:].rearrange("p g f -> p (g f)")[:, 0:H * STEPS].rearrange("p (h x) -> p h x", h=H)
        lane_reset = tmp_row[:].rearrange("p g e -> p (g e)")[:, 0:STEPS]
        lane_tail = sb("lane_tail", [P, H])
        lane_flag = sb("lane_flag", [P, 1])
        lane_flag_h = sb("lane_flag_h", [P, H])
        carry_rst = sb("carry_rst", [H, P])
        carry = sb("carry", [H, P + 1])
        carry_col = sb("carry_col", [P, H])
        ends = sb("ends", [P, NB])
        ends_i = sb("ends_i", [P, NB], i32)
        block_sum = sb("block_sum", [P, NB])
        block_cum = sb("block_cum", [P, NB + 1])
        in_max = sb("in_max", [P, NB, H])
        s_src, s_dst = sb("s_src", [P, NB, H]), sb("s_dst", [P, NB, H])
        e_self, e_tmp = sb("e_self", [P, NB, H]), sb("e_tmp", [P, NB, H])
        e_max = sb("e_max", [P, NB, H])
        p_self, den = sb("p_self", [P, NB, H]), sb("den", [P, NB, H])
        node_vals = sb("node_vals", [P, NB, 2 * H])

        part_slot = [T[:]] + [(edge_score, step_rec)[k % 2][:].rearrange("p a b -> p (a b)")[:, 0:NB * D].rearrange("p (b f) -> p b f", f=D)
                              for k in range(1, 2 * QU)]

        acc = ctx.enter_context(nc.psum_tensor("acc", [P, 7 * 512], f32))
        aux = ctx.enter_context(nc.psum_tensor("aux", [P, 512], f32))
        SIDE = NB * D

        s_const, s_pad, s_edges, s_par, s_par2 = (sem(n) for n in ("const", "pad", "edges", "par", "par2"))
        s_x, s_rec_sb, s_rec, s_prev, s_cnt, s_below = (sem(n) for n in ("xin", "rec_sb", "rec", "prev", "cnt", "below"))
        s_chunk, s_steprec, s_bt, s_btd, s_btrow = (sem(n) for n in ("chunk", "steprec", "bt", "btd", "btrow"))
        s_rows_ready, s_rowd, s_tr, s_cols, s_w1t = (sem(n) for n in ("rows_rdy", "rowd", "tr", "cols", "w1t"))
        chain = sem("dve_chain")

        def layers(name, *numbers):
            return {a: sem(f"{name}{a}") for a in numbers}

        half_done, idx_ready, oh_ready = (layers(n, 1, 2, 3, 4) for n in ("half_done", "idx_ready", "oh_ready"))
        gathered = {a: [sem(f"gathered{a}_{p}") for p in range(2)] for a in range(1, 5)}
        oh_plain = sem("oh_plain")
        agg_out, lhs_ready, node_mm = layers("agg_out", 1, 2, 3), layers("lhs_ready", 2, 3), layers("node_mm", 2, 3)
        ln_var, ln_std, x_ready, tab_done = (layers("ln_var", 0, 1, 3, 4), layers("ln_std", 0, 1, 3, 4),
                                             layers("x_ready", 0, 1, 2, 3), layers("tab_done", 2, 3, 4))
        pr_nat, pr_tr, pr_lhs, pr_mm, pr_out = ([sem(f"{n}{a}") for a in range(5)] for n in ("pr_nat", "pr_tr", "pr_lhs", "pr_mm", "pr_out"))
        h_store = [sem(f"h_store{p}") for p in range(2)]
        ln2_var, ln2_std = sem("ln2_var"), sem("ln2_std")
        s_scores, s_idx3, s_g3, s_c3 = sem("scores"), sem("idx3"), [sem("g3_0"), sem("g3_1")], sem("c3")
        s_st, s_srow, s_sflat, s_lanes, s_tail, s_tailT, s_carry, s_carryT, s_prefix, s_preft = (
            sem(n) for n in ("st", "srow_s", "sflat", "lanes_s", "tail", "tailT", "carry_s", "carryT", "prefix_s", "preft"))
        s_degT, s_degP, s_ends, s_inmax, s_eself, s_pself, s_nv = (
            sem(n) for n in ("degT", "degP", "ends_s", "inmax", "eself", "pself", "nv"))
        bc_load, t_ready, expanded, u_ready, p_ready, m_ready, z_done = (
            sem(n) for n in ("bc_load", "t_ready", "expanded", "u_ready", "p_ready", "m_ready", "z_done"))
        bc_load = [bc_load, sem("bc_load1")]
        s_zeroed, bc0, t0_ready, eq_ready, dup_s, idx0_ready = (
            sem(n) for n in ("zeroed", "bc0", "t0_ready", "eq_ready", "dup_s", "idx0_ready"))
        bc0 = [bc0, sem("bc0_1")]
        r_mm, weighted, s_mm, sum_ready, pool_tick, s_part, s_added = (
            sem(n) for n in ("r_mm", "weighted", "s_mm", "sum_ready", "pool_tick", "part", "added"))
        scattered = [sem("scattered0"), sem("scattered1")]
        s_final, s_out = sem("final"), sem("out_s")

        def rows_of(tab):
            return tab.rearrange("(b p) f -> p b f", p=P)

        block = ctx.enter_context(nc.Block())

        @block.sync
        def _(sp):
            full = (G - 1) * P * P
            whole = (E - full) // P
            sp.wait_ge(s_pad, 1)
            for f, ap in enumerate((src, etype, dst)):
                sp.dma_start(raw[:, f, 0:(G - 1) * P].rearrange("p (g e) -> p g e", e=P),
                             ap[0:full].rearrange("(g p e) -> p g e", p=P, e=P)).then_inc(s_edges, 16)
                sp.dma_start(raw[0:whole, f, (G - 1) * P:SLOTS],
                             ap[full:full + whole * P].rearrange("(p e) -> p e", e=P)).then_inc(s_edges, 16)
                sp.dma_start(raw[whole:whole + 1, f, (G - 1) * P:(G - 1) * P + E - full - whole * P],
                             ap[full + whole * P:E].rearrange("(a e) -> a e", a=1)).then_inc(s_edges, 16)
            sp.dma_start(chunk_sb[:, 0:G - 1, 3, :], ew[0:full].rearrange("(g p e) -> p g e", p=P, e=P)).then_inc(s_edges, 16)
            sp.dma_start(chunk_sb[0:whole, G - 1, 3, :],
                         ew[full:full + whole * P].rearrange("(p e) -> p e", e=P)).then_inc(s_edges, 16)
            sp.dma_start(chunk_sb[whole:whole + 1, G - 1, 3, 0:E - full - whole * P],
                         ew[full + whole * P:E].rearrange("(a e) -> a e", a=1)).then_inc(s_edges, 16)
            for buf in part_sum:
                sp.dma_start(buf[0:NP, :].rearrange("(b p) f -> p b f", p=P), Y[:]).then_inc(s_zeroed, 16)
                sp.dma_start(buf[NP:NP + SPARE, :], Y[:, 0, :]).then_inc(s_zeroed, 16)
            sp.dma_start(X[:, 0:NB - 1, :], x[0:(NB - 1) * P, :].rearrange("(b p) f -> p b f", p=P)).then_inc(s_x, 16)
            sp.dma_start(X[0:TAIL, NB - 1, :], x[(NB - 1) * P:N, :]).then_inc(s_x, 16)
            for tile, ap in ((W0, w0), (WS1, ws1), (WN1, wn1), (WS2, ws2), (WN2, wn2), (WW, ww)):
                sp.dma_start(tile[:], ap).then_inc(s_par, 16)
            sp.dma_start(W1, w1.rearrange("r h d -> h r d")).then_inc(s_par, 16)
            sp.wait_ge(s_rec_sb, 1)
            sp.dma_start(chunk_rec[0:SLOTS, 0:4 * P].rearrange("(g p) f -> p g f", p=P),
                         chunk_sb[:].rearrange("p g f e -> p g (f e)")).then_inc(s_rec, 16)
            for g in range(G):
                n = P - (g == G - 1)
                sp.dma_start(chunk_rec[g * P + 1:g * P + n + 1, 4 * P:4 * P + 1],
                             chunk_sb[0:n, g, 2, P - 1:P], allow_slow_non_contiguous=True).then_inc(s_rec, 16)
            sp.dma_start(chunk_rec[0:1, 4 * P:4 * P + 1], ones[0:1, 0:1]).then_inc(s_rec, 16)
            sp.wait_ge(s_bt, 1)
            sp.dma_start(block_of_step.rearrange("(g p) -> p g", p=P), step_block_i[:], allow_slow_non_contiguous=True).then_inc(s_btd, 16)
            sp.wait_ge(s_btd, 16)
            sp.dma_start(block_row[:], block_of_step.rearrange("(a t) -> a t", a=1)).then_inc(s_btrow, 16)
            sp.wait_ge(s_rows_ready, 1)
            sp.dma_start(rel_rows.rearrange("(g p) e -> p g e", p=P), rel_row[:]).then_inc(s_rowd, 16)
            sp.dma_start(reset_flat.rearrange("(g p e) -> p g e", p=P, e=P), reset_row[:]).then_inc(s_rowd, 16)
            sp.dma_start(src_rows.rearrange("(g p) e -> p g e", p=P), step_rec[:, :, 0:P]).then_inc(s_rowd, 16)
            sp.wait_ge(s_rowd, 48)

            def rel_src_quarter(q, p, n):
                for tile, tab in ((rel_bc, rel_rows), (src_bc, src_rows)):
                    sp.dma_start(tile[:, p, 0:n * P],
                                 tab[ds(q * QU, n), :].rearrange("(a t) e -> a (t e)", a=1).to_broadcast([P, n * P])
                                 ).then_inc(bc0[p], 16)

            sp.wait_ge(s_w1t, 1)
            rel_src_quarter(0, 0, QU)
            rel_src_quarter(1, 1, QU)
            with sp.Fori(0, QLOOPS - 1) as j:
                for p in range(2):
                    sp.wait_ge(idx0_ready, j * 2 + p + 1)
                    rel_src_quarter(j * 2 + p + 2, p, QU)
            sp.wait_ge(idx0_ready, 2 * QLOOPS - 1)
            rel_src_quarter(2 * QLOOPS, 0, QU)
            sp.wait_ge(idx0_ready, 2 * QLOOPS)
            rel_src_quarter(2 * QLOOPS + 1, 1, QREST - QU)
            sp.wait_ge(scattered[0], 16 * QU * (QLOOPS + 1))
            sp.wait_ge(scattered[1], 16 * (QU * QLOOPS + QREST - QU))
            for k, buf in enumerate(part_sum):
                if k >= 3:
                    sp.wait_ge(s_added, k - 1)
                sp.dma_start(part_slot[k], buf[0:NP, :].rearrange("(b p) f -> p b f", p=P)).then_inc(s_part, 16)
                sp.wait_ge(s_part, 16 * (k + 1))
            with sp.Fori(0, GROUPS) as i:
                for k in range(GB):
                    sp.wait_ge(pr_out[0], i * GB + k + 1)
                    if k % 2:
                        sp.dma_start(rel_tab[ds((i * GB + k) * P, P), :], hout[:, 1, :]).then_inc(h_store[1], 16)
                    else:
                        sp.dma_start(rel_tab[ds((i * GB + k) * P, P), :], hout[:, 0, :]).then_inc(h_store[0], 16)
            for a, tab in ((2, node_tab), (3, hid_tab)):
                sp.wait_ge(x_ready[a - 1], 1)
                sp.dma_start(rows_of(tab), (X if a == 2 else T)[:]).then_inc(tab_done[a], 16)
            sp.wait_ge(s_scores, 1)
            sp.dma_start(rows_of(score_tab), s_src[:]).then_inc(tab_done[4], 16)
            sp.dma_start(rows_of(key_tab), Y[:]).then_inc(tab_done[4], 16)
            sp.wait_ge(s_srow, 1)
            for h in range(H):
                sp.dma_start(score_flat[h, :].rearrange("(g p e) -> p g e", p=P, e=P), score_row[:, h]).then_inc(s_sflat, 16)
            sp.wait_ge(s_sflat, 16 * H)
            sp.wait_ge(s_rowd, 32)
            for h in range(H):
                sp.dma_start(lanes[:, h, :], score_flat[h, 0:STEPS * P].rearrange("(l x) -> l x", x=STEPS)).then_inc(s_lanes, 16)
            sp.dma_start(lane_reset, reset_flat[0:STEPS * P].rearrange("(l x) -> l x", x=STEPS)).then_inc(s_lanes, 16)
            sp.wait_ge(s_prefix, 1)
            sp.dma_start(prefix_tab.rearrange("(l x) h -> l (x h)", x=STEPS),
                         prefix[:].rearrange("p x h -> p (x h)")).then_inc(s_preft, 16)
            def rel_half(it, p, n):
                sp.wait_ge(half_done[4], it + 1)
                sp.dma_start(rel_bc[:, p, 0:n * P],
                             rel_rows[ds(it * HALF, n), :].rearrange("(a t) e -> a (t e)", a=1).to_broadcast([P, n * P])
                             ).then_inc(bc_load[p], 16)

            with sp.Fori(0, LOOPS) as j:
                for p in range(2):
                    rel_half(j * 2 + p, p, HALF)
            rel_half(2 * LOOPS, 0, REST)
            sp.wait_ge(s_final, 1)
            sp.dma_start(out[0:(NB - 1) * P, :].rearrange("(b p) f -> p b f", p=P), X[:, 0:NB - 1, :]).then_inc(s_out, 16)
            sp.dma_start(out[(NB - 1) * P:N, :], X[0:TAIL, NB - 1, :]).then_inc(s_out, 16)
            sp.wait_ge(s_out, 32)

        @block.gpsimd
        def _(pool):
            nc.gpsimd.iota(iota_row[:], [[1, P]], base=0, channel_multiplier=0, allow_small_or_imprecise_dtypes=True)
            nc.gpsimd.iota(iota_part[:], [[0, 1]], base=0, channel_multiplier=1, allow_small_or_imprecise_dtypes=True)
            nc.gpsimd.iota(block_base[:], [[P, NB]], base=0, channel_multiplier=0, allow_small_or_imprecise_dtypes=True)
            nc.gpsimd.iota(step_no[:], [[P, G]], base=0, channel_multiplier=1,
                           allow_small_or_imprecise_dtypes=True).then_inc(s_const, 1)
            pool.wait_ge(s_rec, 16 * (G + 2))
            pool.wait_ge(s_chunk, 1)
            for g in range(G):
                nc.gpsimd.indirect_dma_start(step_rec[:, g, :], None, chunk_rec,
                                             bass.IndirectOffsetOnAxis(ap=step_chunk[:, g:g + 1], axis=0)).then_inc(s_steprec, 16)

            def gather(a, table):
                def half(it, p, n):
                    pool.wait_ge(idx_ready[a], it + 1)
                    pool.sem_inc(pool_tick)
                    for k in range(n):
                        nc.gpsimd.indirect_dma_start(rows[:, p, k, :], None, table,
                                                     bass.IndirectOffsetOnAxis(ap=idx_slot[:, p, k:k + 1], axis=0)
                                                     ).then_inc(gathered[a][p], 16)

                with pool.Fori(0, LOOPS) as j:
                    for p in range(2):
                        half(j * 2 + p, p, HALF)
                half(2 * LOOPS, 0, REST)

            pool.wait_ge(s_zeroed, 16 * 4 * QU)

            def scatter_quarter(q, p, n):
                pool.wait_ge(idx0_ready, q + 1)
                pool.sem_inc(pool_tick)
                pool.wait_ge(sum_ready, q + 2)
                pool.sem_inc(pool_tick)
                for k in range(n):
                    nc.gpsimd.indirect_dma_start(part_sum[p * QU + k], bass.IndirectOffsetOnAxis(ap=idx_slot[:, p, k:k + 1], axis=0),
                                                 msg[:, p, k, :], None, compute_op=ALU.add).then_inc(scattered[p], 16)

            with pool.Fori(0, QLOOPS) as j:
                for p in range(2):
                    scatter_quarter(j * 2 + p, p, QU)
            scatter_quarter(2 * QLOOPS, 0, QU)
            scatter_quarter(2 * QLOOPS + 1, 1, QREST - QU)
            pool.wait_ge(h_store[0], 16 * GROUPS * 3)
            pool.wait_ge(h_store[1], 16 * GROUPS * 2)
            gather(1, rel_tab.rearrange("n (r f) -> (n r) f", r=R))
            for a, tab in ((2, node_tab), (3, hid_tab)):
                pool.wait_ge(tab_done[a], 16)
                gather(a, tab)
            pool.wait_ge(tab_done[4], 32)

            def score_half(it, p, n):
                pool.wait_ge(s_idx3, it + 1)
                pool.sem_inc(pool_tick)
                for k in range(n):
                    nc.gpsimd.indirect_dma_start(srow[:, p, k, :], None, score_tab,
                                                 bass.IndirectOffsetOnAxis(ap=idx_slot[:, p, k:k + 1], axis=0)
                                                 ).then_inc(s_g3[p], 16)

            with pool.Fori(0, LOOPS) as j:
                for p in range(2):
                    score_half(j * 2 + p, p, HALF)
            score_half(2 * LOOPS, 0, REST)
            pool.wait_ge(s_preft, 16)
            pool.wait_ge(s_ends, 1)
            for b in range(NB):
                nc.gpsimd.indirect_dma_start(in_max[:, b, :], None, prefix_tab,
                                             bass.IndirectOffsetOnAxis(ap=ends_i[:, b:b + 1], axis=0)).then_inc(s_inmax, 16)
            gather(4, key_tab)

        @block.scalar
        def _(act):
            for tile, ap in ((B0, b0), (GA, gamma), (BE, beta), (B21, b21), (B22, b22), (WB, wb)):
                act.dma_start(tile[:], ap.rearrange("(a f) -> a f", a=1).to_broadcast([P, D])).then_inc(s_par2, 16)
            act.dma_start(B1[:], b1.rearrange("r f -> (r f)").rearrange("(a f) -> a f", a=1).to_broadcast([P, R * D])).then_inc(s_par2, 16)
            act.dma_start(A_DST[:], aw[:, 0:D // H].rearrange("(a h) f -> a h f", a=1).to_broadcast([P, H, D // H])).then_inc(s_par2, 16)
            act.dma_start(A_SRC[:], aw[:, D // H:2 * D // H].rearrange("(a h) f -> a h f", a=1).to_broadcast([P, H, D // H])).then_inc(s_par2, 16)
            act.dma_start(AB[:], ab.rearrange("(a h) -> a h", a=1).to_broadcast([P, H])).then_inc(s_par2, 16)

            def sums_to_lhs(a):
                act.wait_ge(half_done[a], 2 + HALVES)
                with act.Fori(0, GROUPS) as i:
                    act.wait_ge(node_mm[a], i)
                    nc.scalar.copy(lhs_slot[:].rearrange("p b f -> p (b f)"), acc[:, ds(i * GB * D, GB * D)]).then_inc(lhs_ready[a], 1)

            def root(a, v, s, var_ready, std_ready):
                act.wait_ge(var_ready, v)
                nc.scalar.activation(rstd[:], var[:], ACT.Sqrt).then_inc(std_ready, 1)

            def project(q, source, ready, count):
                act.wait_ge(ready, count)
                with act.Fori(0, GROUPS) as i:
                    act.wait_ge(pr_tr[q], i * GB)
                    nc.scalar.copy(nat_slot[:], source[:, ds(i * GB, GB), :]).then_inc(pr_nat[q], 1)
                    for k in range(GB):
                        act.wait_ge(pr_tr[q], i * GB + k + 1)
                        if k >= 2:
                            act.wait_ge(pr_mm[q], i * GB + k - 1)
                        else:
                            act.wait_ge(pr_mm[q], i * GB)
                        nc.scalar.copy(lhs_slot[:, k % 2, :], acc[:, (k % 2) * 512:(k % 2) * 512 + P]).then_inc(pr_lhs[q], 1)

            def weigh_quarter(q, j, p, n):
                act.wait_ge(r_mm, q + 1)
                for k in range(n):
                    last = nc.scalar.activation(rows[:, p, k, :], acc[:, p * 512 + k * D:p * 512 + (k + 1) * D], ACT.Copy,
                                                scale=w_col[:, ds(q * QU + k, 1)])
                last.then_inc(weighted, 1)
                act.wait_ge(s_mm, q + 2)
                act.wait_ge(scattered[p], j * 16 * QU)
                nc.scalar.copy(msg[:, p, 0:n, :].rearrange("p k f -> p (k f)"), acc[:, (2 + p) * 512:(2 + p) * 512 + n * D]).then_inc(sum_ready, 1)

            act.nop().then_inc(sum_ready, 1)
            act.wait_ge(s_cols, 1)
            with act.Fori(0, QLOOPS) as j:
                for p in range(2):
                    weigh_quarter(j * 2 + p, j, p, QU)
            weigh_quarter(2 * QLOOPS, QLOOPS, 0, QU)
            weigh_quarter(2 * QLOOPS + 1, QLOOPS, 1, QREST - QU)
            project(4, T, s_added, 2 * QU)
            root(0, 1, 1, ln_var[0], ln_std[0])
            project(0, X, x_ready[0], 1)
            root(1, 1, 1, ln_var[1], ln_std[1])
            root(1, 1, 1, ln2_var, ln2_std)
            project(1, X, x_ready[1], 1)
            sums_to_lhs(2)
            project(2, T, x_ready[2], 1)
            sums_to_lhs(3)
            root(3, 1, 1, ln_var[3], ln_std[3])
            project(3, X, x_ready[3], 1)
            act.wait_ge(s_eself, 1)
            nc.scalar.activation(p_self[:], e_tmp[:], ACT.Exp).then_inc(s_pself, 1)

            def exp_half(it, p, n):
                act.wait_ge(u_ready, it + 1)
                nc.scalar.activation(prob[:, p, 0:n, :], u_slot[:, p, 0:n, :], ACT.Exp).then_inc(p_ready, 1)

            with act.Fori(0, LOOPS) as j:
                for p in range(2):
                    exp_half(j * 2 + p, p, HALF)
            exp_half(2 * LOOPS, 0, REST)
            root(4, 1, 1, ln_var[4], ln_std[4])

        @block.vector
        def _(dve):
            V = nc.vector
            count = [0]

            def then(ins):
                count[0] += 1
                ins.then_inc(chain, 1)
                dve.wait_ge(chain, count[0])

            V.memset(raw[:, 0:2, (G - 1) * P:SLOTS], 0)
            V.memset(raw[:, 2, (G - 1) * P:SLOTS], E)
            V.memset(X[:, NB - 1, :], 0.0)
            V.memset(ones[:], 1.0)
            V.memset(zeros[:], 0.0)
            V.memset(Y[:], 0.0)
            then(V.memset(chunk_sb[:, G - 1, 3, :], 0.0))
            V.memset(carry[:, 0:1], -BIG).then_inc(s_pad, 1)
            dve.wait_ge(s_const, 1)
            V.tensor_scalar(ident[:], iota_row[:], iota_part[:, 0:1], None, ALU.is_equal)
            V.tensor_scalar(before[:], iota_row[:], iota_part[:, 0:1], None, ALU.is_lt)
            V.tensor_scalar(spare_row[:], iota_part[:], float(NP), None, ALU.add)
            V.tensor_scalar(upto[:], iota_row[:], iota_part[:, 0:1], None, ALU.is_ge)
            dve.wait_ge(s_edges, 16 * 12)
            then(V.tensor_copy(chunk_sb[:, :, 0:3, :], raw.rearrange("p f (g e) -> p g f e", e=P)))
            V.engine_nop().then_inc(s_rec_sb, 1)
            for b in range(NB - 1):
                ins = V.tensor_scalar(tmp_row[:], chunk_sb[:, :, 2, :], float((b + 1) * P), 0.0, ALU.is_lt, ALU.add,
                                      accum_out=below[:, b:b + 1])
                then(ins)
            V.engine_nop().then_inc(s_cnt, 1)
            dve.wait_ge(s_below, 1)
            then(V.tensor_copy(below_i[:], aux[:, 0:NB - 1]))
            then(V.tensor_scalar(below_i[:], below_i[:], 7, None, ALU.arith_shift_right))
            then(V.tensor_copy(last_step[:], below_i[:]))
            then(V.scalar_tensor_tensor(last_step[:], block_base[:, 0:NB - 1], 1.0 / P, last_step[:], ALU.mult, ALU.add))
            for g in range(G):
                then(V.tensor_scalar(tmp_row[:, 0, 0:NB - 1], last_step[:], step_no[:, g:g + 1], 0.0, ALU.is_lt, ALU.add,
                                     accum_out=step_block[:, g:g + 1]))
            then(V.tensor_tensor(step_base[:], step_no[:], step_block[:], ALU.subtract))
            V.tensor_copy(step_chunk[:], step_base[:]).then_inc(s_chunk, 1)
            V.tensor_copy(step_block_i[:], step_block[:]).then_inc(s_bt, 1)
            dve.wait_ge(s_chunk, 1)
            then(V.tensor_scalar(step_base[:], step_block[:], float(P), None, ALU.mult))
            dve.wait_ge(s_steprec, 16 * G)
            fields = step_rec[:, :, 0:4 * P].rearrange("p g (f e) -> p g f e", f=4)
            f_src, f_typ, f_dst = (fields[:, :, f, :] for f in range(3))
            then(V.tensor_tensor(rel_row[:], f_dst, step_base[:, :, None].to_broadcast([P, G, P]), ALU.subtract))
            then(V.tensor_scalar(valid[:], rel_row[:], 0.0, None, ALU.is_ge))
            then(V.scalar_tensor_tensor(valid[:], rel_row[:], float(P), valid[:], ALU.is_lt, ALU.mult))
            then(V.tensor_scalar(invalid_pen[:], valid[:], 1.0, BIG, ALU.subtract, ALU.mult))
            then(V.scalar_tensor_tensor(rel_row[:], rel_row[:], 1.0, valid[:], ALU.add, ALU.mult))
            then(V.tensor_scalar(rel_row[:], rel_row[:], 1.0, None, ALU.subtract))
            V.tensor_tensor(tmp_row[:, :, 1:P], f_dst[:, :, 1:P], f_dst[:, :, 0:P - 1], ALU.not_equal)
            then(V.tensor_tensor(tmp_row[:, :, 0:1], f_dst[:, :, 0:1], step_rec[:, :, 4 * P:4 * P + 1], ALU.not_equal))
            then(V.scalar_tensor_tensor(reset_row[:], tmp_row[:], -BIG, valid[:], ALU.mult, ALU.mult))
            then(V.scalar_tensor_tensor(f_typ, f_src, float(R), f_typ, ALU.mult, ALU.add))
            V.engine_nop().then_inc(s_rows_ready, 1)
            dve.wait_ge(s_tr, 1)
            cols = acc[:].rearrange("p (g f t) -> p g f t", g=G, f=4)
            for f, tile in enumerate((idx_src, idx_rel, rel_col, w_col)):
                then(V.tensor_copy(tile[:].rearrange("p (g t) -> p g t", t=P), cols[:, :, f, :]))
            V.engine_nop().then_inc(s_cols, 1)
            dve.wait_ge(s_x, 32)
            dve.wait_ge(s_par2, 160)
            dve.wait_ge(s_zeroed, 16 * 4 * QU)
            dve.wait_ge(s_w1t, 1)
            then(V.tensor_copy(W1T[:], acc[:, 0:R * D]))
            V.engine_nop().then_inc(s_w1t, 1)

            def prepare(a, idx, weights=False):
                def half(it, p, n):
                    dve.wait_ge(half_done[a], it + 1)
                    V.tensor_copy(idx_slot[:, p, 0:n], idx[:, ds(it * HALF, n)]).then_inc(idx_ready[a], 1)
                    oh = V.tensor_tensor(onehot[:, p, 0:n, :], iota_row[:, None, :].to_broadcast([P, n, P]),
                                         rel_col[:, ds(it * HALF, n), None].to_broadcast([P, n, P]), ALU.is_equal)
                    if weights:
                        oh.then_inc(oh_plain, 1)
                        dve.wait_ge(oh_plain, it + 1)
                        oh = V.tensor_tensor(onehot[:, p, 0:n, :], onehot[:, p, 0:n, :],
                                             w_col[:, ds(it * HALF, n), None].to_broadcast([P, n, P]), ALU.mult)
                    oh.then_inc(oh_ready[a], 1)

                with dve.Fori(0, LOOPS) as j:
                    for p in range(2):
                        half(j * 2 + p, p, HALF)
                half(2 * LOOPS, 0, REST)

            def over(v):
                return v[:, :, None].to_broadcast([P, NB, D])

            def normalize(src_, dst_, scratch, var_ready, std_ready):
                then(V.tensor_reduce(mean[:], src_[:], AX.X, ALU.add))
                then(V.tensor_scalar(mean[:], mean[:], 1.0 / D, None, ALU.mult))
                then(V.tensor_tensor(src_[:], src_[:], over(mean), ALU.subtract))
                then(V.tensor_tensor(scratch[:], src_[:], src_[:], ALU.mult))
                then(V.tensor_reduce(var[:], scratch[:], AX.X, ALU.add))
                V.tensor_scalar(var[:], var[:], 1.0 / D, EPS, ALU.mult, ALU.add).then_inc(var_ready, 1)
                dve.wait_ge(std_ready, 1)
                then(V.reciprocal(rstd[:], rstd[:]))
                then(V.tensor_tensor(dst_[:], src_[:], over(rstd), ALU.mult))

            def signal(s):
                V.engine_nop().then_inc(s, 1)

            flat_acc = acc[:, 0:NB * D].rearrange("p (b f) -> p b f", f=D)

            def projected(q, bias):
                with dve.Fori(0, GROUPS) as i:
                    for k in range(GB):
                        dve.wait_ge(pr_mm[q], i * GB + k + 1)
                        V.tensor_tensor(Y[:, ds(i * GB + k, 1), :], acc[:, (2 + k % 2) * 512:(2 + k % 2) * 512 + P][:, None, :], bias[:, None, :],
                                        ALU.add).then_inc(pr_out[q], 1)

            first_sum = hout[:, 1, 0:QU * P].rearrange("p (k e) -> p k e", e=P)

            def sources_quarter(q, j, p, n):
                dve.wait_ge(s_mm, q)
                dve.wait_ge(bc0[p], j * 32 + 32)
                V.tensor_scalar(onehot_t[:, p, 0:n * P], rel_bc[:, p, 0:n * P], iota_part[:, 0:1], None, ALU.is_equal).then_inc(t0_ready, 1)
                V.tensor_tensor(onehot[:, p, 0:n, :], src_bc[:, p, 0:n * P].rearrange("p (k e) -> p k e", e=P),
                                idx_src[:, ds(q * QU, n), None].to_broadcast([P, n, P]), ALU.is_equal).then_inc(eq_ready, 1)
                dve.wait_ge(eq_ready, q + 1)
                V.tensor_tensor(first_sum[:, 0:n, :], onehot[:, p, 0:n, :], before[:, None, :].to_broadcast([P, n, P]), ALU.mult).then_inc(dup_s, 1)
                V.tensor_scalar(to_spare[:, 0:n], idx_src[:, ds(q * QU, n)], -1.0, spare_row[:, 0:1], ALU.mult, ALU.add)
                dve.wait_ge(dup_s, q * 3 + 1)
                V.tensor_reduce(dup[:, 0:n], first_sum[:, 0:n, :], AX.X, ALU.add).then_inc(dup_s, 1)
                dve.wait_ge(dup_s, q * 3 + 2)
                V.scalar_tensor_tensor(dup[:, 0:n], dup[:, 0:n], 0.0, to_spare[:, 0:n], ALU.is_gt, ALU.mult).then_inc(dup_s, 1)
                dve.wait_ge(dup_s, q * 3 + 3)
                dve.wait_ge(scattered[p], j * 16 * QU)
                V.tensor_tensor(idx_slot[:, p, 0:n], dup[:, 0:n], idx_src[:, ds(q * QU, n)], ALU.add).then_inc(idx0_ready, 1)

            with dve.Fori(0, QLOOPS) as j:
                for p in range(2):
                    sources_quarter(j * 2 + p, j, p, QU)
            sources_quarter(2 * QLOOPS, QLOOPS, 0, QU)
            sources_quarter(2 * QLOOPS + 1, QLOOPS, 1, QREST - QU)
            dve.wait_ge(s_part, 16)
            V.engine_nop().then_inc(s_added, 1)
            for k in range(1, 2 * QU):
                dve.wait_ge(s_part, 16 * (k + 1))
                V.tensor_tensor(T[:], T[:], part_slot[k], ALU.add).then_inc(s_added, 1)
                dve.wait_ge(s_added, k + 1)
            projected(4, B0)
            dve.wait_ge(pr_out[4], NB)
            then(V.tensor_tensor(Y[:], Y[:], X[:], ALU.add))
            normalize(Y, X, T, ln_var[0], ln_std[0])
            signal(x_ready[0])
            with dve.Fori(0, GROUPS) as i:
                for k in range(GB):
                    dve.wait_ge(pr_mm[0], i * GB + k + 1)
                    if k % 2:
                        dve.wait_ge(h_store[1], i * 32 + (k // 2) * 16)
                    else:
                        dve.wait_ge(h_store[0], i * 48 + (k // 2) * 16)
                    V.tensor_tensor(hout[:, k % 2, :], acc[:, (k % 2 + 1) * R * D:(k % 2 + 2) * R * D], B1[:], ALU.add).then_inc(pr_out[0], 1)

            prepare(1, idx_rel)
            dve.wait_ge(half_done[1], 2 + HALVES)
            V.tensor_copy(deg[:], acc[:, SIDE:SIDE + NB])
            then(V.tensor_tensor(Y[:], X[:], flat_acc, ALU.add))
            signal(agg_out[1])
            normalize(Y, Y, T, ln_var[1], ln_std[1])
            then(V.tensor_tensor(Y[:], Y[:], GA[:, None, :].to_broadcast([P, NB, D]), ALU.mult))
            then(V.tensor_tensor(Y[:], Y[:], BE[:, None, :].to_broadcast([P, NB, D]), ALU.add))
            then(V.tensor_tensor(Y[:], Y[:], X[:], ALU.add))
            normalize(Y, X, T, ln2_var, ln2_std)
            signal(x_ready[1])
            then(V.tensor_scalar(rdeg[:], deg[:], 1.0, None, ALU.max))
            then(V.reciprocal(rdeg[:], rdeg[:]))
            then(V.tensor_scalar(has[:], deg[:], 0.0, None, ALU.is_gt))

            for a, bias in ((2, B21), (3, B22)):
                projected(a - 1, bias)
                prepare(a, idx_src)
                dve.wait_ge(node_mm[a], GROUPS)
                dve.wait_ge(pr_out[a - 1], NB)
                then(V.tensor_tensor(T[:], flat_acc, over(rdeg), ALU.mult))
                signal(agg_out[a])
                then(V.tensor_tensor(T[:], T[:], Y[:], ALU.add))
                if a == 2:
                    then(V.tensor_scalar(T[:], T[:], 0.0, None, ALU.max))
                    signal(x_ready[2])
                else:
                    then(V.tensor_tensor(Y[:], T[:], X[:], ALU.add))
                    normalize(Y, X, T, ln_var[3], ln_std[3])
                    signal(x_ready[3])

            projected(3, WB)
            dve.wait_ge(pr_out[3], NB)
            for A, s in ((A_SRC, s_src), (A_DST, s_dst)):
                then(V.tensor_tensor(T[:], Y[:], A[:].rearrange("p h f -> p (h f)")[:, None, :].to_broadcast([P, NB, D]), ALU.mult))
                then(V.tensor_reduce(s[:].rearrange("p b h -> p (b h)"), T[:].rearrange("p b (h f) -> p (b h) f", h=H), AX.X, ALU.add))
            then(V.tensor_tensor(s_dst[:], s_dst[:], AB[:, None, :].to_broadcast([P, NB, H]), ALU.add))
            signal(s_scores)
            dve.wait_ge(s_degP, 1)
            V.tensor_copy(block_sum[:], aux[:, P:P + NB])
            then(V.memset(block_cum[:, 0:1], 0.0))
            then(V.tensor_tensor_scan(block_cum[:, 1:NB + 1], zeros[:, 0:NB], block_sum[:], 0.0, ALU.add, ALU.add))
            then(V.tensor_tensor(ends[:], aux[:, 0:NB], block_cum[:, 0:NB], ALU.add))
            then(V.scalar_tensor_tensor(ends[:], ends[:], -1.0, block_base[:], ALU.add, ALU.add))
            then(V.tensor_scalar(ends[:], ends[:], 0.0, None, ALU.max))
            V.tensor_copy(ends_i[:], ends[:]).then_inc(s_ends, 1)

            V.memset(edge_score[:, STEPS:SLOTS, :], 0.0)
            def score_copy(it, p, n):
                dve.wait_ge(s_g3[p], (it + 1) // 2 * 0 + 0) if False else None

            def score_idx(it, p, n):
                V.tensor_copy(idx_slot[:, p, 0:n], idx_src[:, ds(it * HALF, n)]).then_inc(s_idx3, 1)

            def score_take(it, j, p, n):
                dve.wait_ge(s_g3[p], j * 16 * HALF + 16 * n)
                V.tensor_copy(edge_score[:, ds(it * HALF, n), :], srow[:, p, 0:n, :]).then_inc(s_c3, 1)
                dve.wait_ge(s_c3, it + 1)

            score_idx(0, 0, HALF)
            score_idx(1, 1, HALF)
            with dve.Fori(0, LOOPS - 1) as j:
                for p in range(2):
                    score_take(j * 2 + p, j, p, HALF)
                    score_idx(j * 2 + p + 2, p, HALF)
            score_take(2 * LOOPS - 2, LOOPS - 1, 0, HALF)
            score_idx(2 * LOOPS, 0, REST)
            score_take(2 * LOOPS - 1, LOOPS - 1, 1, HALF)
            score_take(2 * LOOPS, LOOPS, 0, REST)
            signal(s_st)
            dve.wait_ge(s_tr, 1 + H)
            for h in range(H):
                then(V.tensor_tensor(score_row[:, h], cols[:, :, h, :], valid[:], ALU.mult))
                then(V.tensor_tensor(score_row[:, h], score_row[:, h], invalid_pen[:], ALU.add))
            signal(s_srow)
            dve.wait_ge(s_lanes, 16 * (H + 1))
            for h in range(H):
                V.tensor_tensor_scan(prefix[:, :, h], lane_reset, lanes[:, h, :], -BIG, ALU.add, ALU.max)
            then(V.tensor_reduce(lane_flag[:], lane_reset, AX.X, ALU.min))
            then(V.tensor_copy(lane_flag_h[:], lane_flag[:, 0:1].to_broadcast([P, H])))
            V.tensor_copy(lane_tail[:], prefix[:, STEPS - 1, :]).then_inc(s_tail, 1)
            dve.wait_ge(s_tailT, 1)
            then(V.tensor_copy(carry_rst[:], aux[0:H, P:2 * P]))
            then(V.tensor_tensor_scan(carry[:, 1:P + 1], carry_rst[:], aux[0:H, 0:P], -BIG, ALU.add, ALU.max))
            V.engine_nop().then_inc(s_carry, 1)
            dve.wait_ge(s_carryT, 1)
            then(V.tensor_copy(carry_col[:], aux[:, 2 * P:2 * P + H]))
            for h in range(H):
                then(V.tensor_tensor_scan(prefix[:, :, h], lane_reset, lanes[:, h, :], carry_col[:, h:h + 1], ALU.add, ALU.max))
            V.engine_nop().then_inc(s_prefix, 1)
            dve.wait_ge(s_inmax, 16 * NB)
            hasb = has[:, :, None].to_broadcast([P, NB, H])
            then(V.tensor_tensor(in_max[:], in_max[:], hasb, ALU.mult))
            then(V.tensor_scalar(den[:], hasb, 1.0, BIG, ALU.subtract, ALU.mult))
            then(V.tensor_tensor(in_max[:], in_max[:], den[:], ALU.add))
            then(V.tensor_tensor(e_max[:], in_max[:], s_src[:], ALU.max))
            then(V.tensor_tensor(e_max[:], e_max[:], s_dst[:], ALU.add))
            then(V.scalar_tensor_tensor(e_max[:], e_max[:], 0.2, e_max[:], ALU.mult, ALU.max))
            then(V.tensor_tensor(e_self[:], s_src[:], s_dst[:], ALU.add))
            then(V.scalar_tensor_tensor(e_self[:], e_self[:], 0.2, e_self[:], ALU.mult, ALU.max))
            then(V.tensor_tensor(e_tmp[:], e_self[:], e_max[:], ALU.subtract))
            V.tensor_copy(node_vals[:, :, 0:H], s_dst[:])
            then(V.tensor_copy(node_vals[:, :, H:2 * H], e_max[:]))
            signal(s_eself)

            def attend(it, j, p, n):
                dve.wait_ge(half_done[4], it + 1)
                V.tensor_copy(idx_slot[:, p, 0:n], idx_src[:, ds(it * HALF, n)]).then_inc(idx_ready[4], 1)
                dve.wait_ge(bc_load[p], j * 16 + 16)
                V.tensor_scalar(onehot_t[:, p, 0:n * P], rel_bc[:, p, 0:n * P], iota_part[:, 0:1], None, ALU.is_equal).then_inc(t_ready, 1)
                V.tensor_tensor(onehot[:, p, 0:n, :], iota_row[:, None, :].to_broadcast([P, n, P]),
                                rel_col[:, ds(it * HALF, n), None].to_broadcast([P, n, P]), ALU.is_equal).then_inc(oh_ready[4], 1)
                dve.wait_ge(expanded, it + 1)
                ex = aux[:, p * HALF * 2 * H:(p * HALF + n) * 2 * H].rearrange("p (k v) -> p k v", v=2 * H)
                V.tensor_tensor(z_slot[:, 0:n, :], ex[:, :, 0:H], edge_score[:, ds(it * HALF, n), :], ALU.add).then_inc(z_done, 1)
                dve.wait_ge(z_done, it * 3 + 1)
                V.scalar_tensor_tensor(z_slot[:, 0:n, :], z_slot[:, 0:n, :], 0.2, z_slot[:, 0:n, :], ALU.mult, ALU.max).then_inc(z_done, 1)
                dve.wait_ge(z_done, it * 3 + 2)
                V.tensor_tensor(z_slot[:, 0:n, :], z_slot[:, 0:n, :], ex[:, :, H:2 * H], ALU.subtract).then_inc(z_done, 1)
                dve.wait_ge(z_done, it * 3 + 3)
                V.tensor_scalar(u_slot[:, p, 0:n, :], z_slot[:, 0:n, :], 0.0, None, ALU.min).then_inc(u_ready, 1)
                dve.wait_ge(u_ready, it + 1)
                dve.wait_ge(p_ready, it + 1)
                dve.wait_ge(gathered[4][p], j * 16 * HALF + 16 * n)
                V.tensor_tensor(msg[:, p, 0:n, :].rearrange("p k (h f) -> p (k h) f", h=H),
                                rows[:, p, 0:n, :].rearrange("p k (h f) -> p (k h) f", h=H),
                                prob[:, p, 0:n, :].rearrange("p k h -> p (k h)")[:, :, None].to_broadcast([P, n * H, D // H]),
                                ALU.mult).then_inc(m_ready, 1)

            with dve.Fori(0, LOOPS) as j:
                for p in range(2):
                    attend(j * 2 + p, j, p, HALF)
            attend(2 * LOOPS, LOOPS, 0, REST)
            dve.wait_ge(half_done[4], 2 + HALVES)
            dve.wait_ge(s_pself, 1)
            heads = "p b (h f) -> p b h f"
            psb = p_self[:, :, :, None].to_broadcast([P, NB, H, D // H])
            for b in range(NB) if False else ():
                pass
            pf = p_self[:].rearrange("p b h -> p (b h)")
            then(V.tensor_tensor(T[:].rearrange("p b (h f) -> p (b h) f", h=H), Y[:].rearrange("p b (h f) -> p (b h) f", h=H),
                                 pf[:, :, None].to_broadcast([P, NB * H, D // H]), ALU.mult))
            then(V.tensor_tensor(T[:], T[:], flat_acc, ALU.add))
            then(V.tensor_tensor(den[:].rearrange("p b h -> p (b h)"), pf, acc[:, SIDE:SIDE + NB * H], ALU.add))
            then(V.reciprocal(den[:], den[:]))
            then(V.tensor_tensor(T[:].rearrange("p b (h f) -> p (b h) f", h=H), T[:].rearrange("p b (h f) -> p (b h) f", h=H),
                                 den[:].rearrange("p b h -> p (b h)")[:, :, None].to_broadcast([P, NB * H, D // H]), ALU.mult))
            then(V.tensor_tensor(Y[:], T[:], X[:], ALU.add))
            normalize(Y, X, T, ln_var[4], ln_std[4])
            signal(s_final)

        @block.tensor
        def _(pe):
            M = nc.tensor
            pe.wait_ge(s_cnt, 1)
            M.matmul(aux[:, 0:NB - 1], ones[:], below[:], start=True, stop=True).then_inc(s_below, 1)
            pe.wait_ge(s_rows_ready, 1)
            fields = step_rec[:, :, 0:4 * P].rearrange("p g (f e) -> p g f e", f=4)
            for g in range(G):
                for f, row in enumerate((fields[:, g, 0, :], fields[:, g, 1, :], rel_row[:, g, :], fields[:, g, 3, :])):
                    last = M.transpose(acc[:, (g * 4 + f) * P:(g * 4 + f + 1) * P], row, ident[:])
            last.then_inc(s_tr, 1)
            pe.wait_ge(s_cols, 1)
            pe.wait_ge(s_par, 16 * 7)
            for r in range(R):
                last = M.transpose(acc[:, r * D:(r + 1) * D], W1[:, r, :], ident[:])
            last.then_inc(s_w1t, 1)
            pe.wait_ge(s_w1t, 2)
            pe.wait_ge(s_btrow, 16)

            def clear(a):
                for k in range(7):
                    M.matmul(acc[:, k * 512:(k + 1) * 512], zeros[:, 0:P], zeros[:], start=True, stop=True)

            def begin(a):
                for _ in range(2):
                    pe.nop().then_inc(half_done[a], 1)

            def aggregate(a, transposed, side=False):
                def half(it, j, p, n):
                    _, blk = nc.values_load_multi_w_load_instructions(
                        block_row[0:1, ds(it * HALF, n)], engines=[pe.engine], min_val=0, max_val=NB - 1,
                        skip_runtime_bounds_check_because="a step's block counts which of the NB - 1 others lie before it")
                    pe.wait_ge(oh_ready[a], it + 1)
                    pe.wait_ge(gathered[a][p], j * 16 * HALF + 16 * n)
                    for k in range(n):
                        lhs, rhs = onehot[:, p, k, :], rows[:, p, k, :]
                        if transposed:
                            lhs, rhs = rhs, lhs
                        last = M.matmul(acc[:, ds(blk[k] * D, D)], lhs, rhs, start=False, stop=True, skip_group_check=True)
                        if side:
                            last = M.matmul(acc[:, ds(blk[k] + SIDE, 1)], lhs, ones[:, 0:1], start=False, stop=True, skip_group_check=True)
                    last.then_inc(half_done[a], 1)

                with pe.Fori(0, LOOPS) as j:
                    for p in range(2):
                        half(j * 2 + p, j, p, HALF)
                half(2 * LOOPS, LOOPS, 0, REST)

            def node_product(a, W):
                with pe.Fori(0, GROUPS) as i:
                    pe.wait_ge(lhs_ready[a], i + 1)
                    for k in range(GB):
                        last = M.matmul(acc[:, ds(i * GB * D + k * D, D)], lhs_slot[:, k, :], W[:], start=True, stop=True)
                    last.then_inc(node_mm[a], 1)

            def project(q, W, wide=False):
                with pe.Fori(0, GROUPS) as i:
                    pe.wait_ge(pr_nat[q], i + 1)
                    for k in range(GB):
                        if k >= 2:
                            pe.wait_ge(pr_lhs[q], i * GB + k - 1)
                        else:
                            pe.wait_ge(pr_lhs[q], i * GB)
                        M.transpose(acc[:, (k % 2) * 512:(k % 2) * 512 + P], nat_slot[:, k, :], ident[:]).then_inc(pr_tr[q], 1)
                        pe.wait_ge(pr_lhs[q], i * GB + k + 1)
                        if k >= 2:
                            pe.wait_ge(pr_out[q], i * GB + k - 1)
                        else:
                            pe.wait_ge(pr_out[q], i * GB)
                        if wide:
                            for c in range(2):
                                last = M.matmul(acc[:, (k % 2 + 1) * R * D + c * 512:(k % 2 + 1) * R * D + (c + 1) * 512],
                                                lhs_slot[:, k % 2, :], W[:, c * 512:(c + 1) * 512], start=True, stop=True)
                        else:
                            last = M.matmul(acc[:, (2 + k % 2) * 512:(2 + k % 2) * 512 + P], lhs_slot[:, k % 2, :], W[:], start=True, stop=True)
                        last.then_inc(pr_mm[q], 1)

            def weighted_quarter(q, p, n):
                _, blk = nc.values_load_multi_w_load_instructions(
                    block_row[0:1, ds(q * QU, n)], engines=[pe.engine], min_val=0, max_val=NB - 1,
                    skip_runtime_bounds_check_because="a step's block counts which of the NB - 1 others lie before it")
                pe.wait_ge(t0_ready, q + 1)
                for k in range(n):
                    last = M.matmul(acc[:, p * 512 + k * D:p * 512 + (k + 1) * D], onehot_t[:, p, k * P:(k + 1) * P],
                                    X[:].rearrange("p b f -> p (b f)")[:, ds(blk[k] * D, D)], start=True, stop=True)
                last.then_inc(r_mm, 1)
                pe.wait_ge(weighted, q + 1)
                pe.wait_ge(eq_ready, q + 1)
                pe.wait_ge(sum_ready, q)
                for k in range(n):
                    last = M.matmul(acc[:, (2 + p) * 512 + k * D:(2 + p) * 512 + (k + 1) * D], onehot[:, p, k, :], rows[:, p, k, :],
                                    start=True, stop=True)
                last.then_inc(s_mm, 1)

            pe.wait_ge(s_x, 32)
            pe.nop().then_inc(s_mm, 1)
            with pe.Fori(0, QLOOPS) as j:
                for p in range(2):
                    weighted_quarter(j * 2 + p, p, QU)
            weighted_quarter(2 * QLOOPS, 0, QU)
            weighted_quarter(2 * QLOOPS + 1, 1, QREST - QU)
            project(4, W0)
            pe.wait_ge(pr_out[4], NB)
            project(0, W1T, wide=True)
            pe.wait_ge(pr_out[0], NB)
            begin(1)
            clear(1)
            aggregate(1, False, side=True)
            pe.wait_ge(agg_out[1], 1)
            begin(2)
            project(1, WS1)
            pe.wait_ge(pr_out[1], NB)
            clear(2)
            aggregate(2, True)
            node_product(2, WN1)
            pe.wait_ge(agg_out[2], 1)
            begin(3)
            project(2, WS2)
            pe.wait_ge(pr_out[2], NB)
            clear(3)
            aggregate(3, True)
            node_product(3, WN2)
            pe.wait_ge(agg_out[3], 1)
            project(3, WW)
            pe.wait_ge(pr_out[3], NB)
            M.matmul(aux[:, 0:NB], upto[:], deg[:], start=True, stop=True)
            M.matmul(aux[:, P:P + NB], ones[:], deg[:], start=True, stop=True).then_inc(s_degP, 1)
            pe.wait_ge(s_st, 1)
            for h in range(H):
                for g in range(G):
                    last = M.transpose(acc[:, (g * 4 + h) * P:(g * 4 + h + 1) * P], edge_score[:, g * P:(g + 1) * P, h], ident[:])
                last.then_inc(s_tr, 1)
            pe.wait_ge(s_tail, 1)
            M.transpose(aux[0:H, 0:P], lane_tail[:], ident[:])
            M.transpose(aux[0:H, P:2 * P], lane_flag_h[:], ident[:]).then_inc(s_tailT, 1)
            pe.wait_ge(s_carry, 1)
            M.transpose(aux[:, 2 * P:2 * P + H], carry[:, 0:P], ident[0:H, 0:H]).then_inc(s_carryT, 1)
            pe.wait_ge(s_srow, 1)
            begin(4)
            clear(4)
            pe.wait_ge(s_eself, 1)

            def attend(it, j, p, n):
                _, blk = nc.values_load_multi_w_load_instructions(
                    block_row[0:1, ds(it * HALF, n)], engines=[pe.engine], min_val=0, max_val=NB - 1,
                    skip_runtime_bounds_check_because="a step's block counts which of the NB - 1 others lie before it")
                pe.wait_ge(t_ready, it + 1)
                for k in range(n):
                    col = (p * HALF + k) * 2 * H
                    last = M.matmul(aux[:, col:col + 2 * H], onehot_t[:, p, k * P:(k + 1) * P],
                                    node_vals[:].rearrange("p b v -> p (b v)")[:, ds(blk[k] * (2 * H), 2 * H)], start=True, stop=True)
                last.then_inc(expanded, 1)
                pe.wait_ge(oh_ready[4], it + 1)
                pe.wait_ge(m_ready, it + 1)
                for k in range(n):
                    M.matmul(acc[:, ds(blk[k] * D, D)], onehot[:, p, k, :], msg[:, p, k, :], start=False, stop=True, skip_group_check=True)
                    last = M.matmul(acc[:, ds(blk[k] * H + SIDE, H)], onehot[:, p, k, :], prob[:, p, k, :], start=False, stop=True, skip_group_check=True)
                last.then_inc(half_done[4], 1)

            with pe.Fori(0, LOOPS) as j:
                for p in range(2):
                    attend(j * 2 + p, j, p, HALF)
            attend(2 * LOOPS, LOOPS, 0, REST)


_INS = ['x', 'src', 'dst', 'edge_type_8', 'edge_weight', 'L0_gnn_weight', 'L0_gnn_bias', 'L1_gnn_W', 'L1_gnn_b',
        'L1_gnn_gamma', 'L1_gnn_beta', 'L2_gnn_Wself1', 'L2_gnn_Wneigh1', 'L2_gnn_b1', 'L2_gnn_Wself2',
        'L2_gnn_Wneigh2', 'L2_gnn_b2', 'L3_gnn_W_w', 'L3_gnn_W_b', 'L3_gnn_a_w', 'L3_gnn_a_b']


def kernel(**inputs):
    import numpy as _np
    import concourse.bacc as _bacc
    from concourse import mybir as _mybir
    from concourse.bass_utils import run_bass_kernel_spmd as _run

    nc = _bacc.Bacc("TRN2", target_bir_lowering=False, num_devices=1)
    arrays, args = {}, []
    for name in _INS:
        a = _np.ascontiguousarray(inputs[name])
        arrays[f"in_{name}_dram"] = a
        args.append(nc.dram_tensor(f"in_{name}_dram", a.shape, _mybir.dt.from_np(a.dtype), kind="ExternalInput").ap())
    args.append(nc.dram_tensor("out_0_dram", (N, D), _mybir.dt.float32, kind="ExternalOutput").ap())
    gnn_kernel(nc, *args)
    r = _run(nc, [arrays], core_ids=[0])
    return r.results[0]["out_0_dram"]
```

```python
import concourse.bass as bass
from concourse import mybir
from contextlib import ExitStack

N, D, E, R, H = 3125, 128, 100000, 8, 4
P = 128
NB = -(-N // P)
NP = NB * P
TAIL = N - (NB - 1) * P
CH = -(-E // P)
STEPS = CH + NB - 1
HALF = 8
BODY = 2 * HALF
LOOPS = STEPS // BODY
REST = STEPS - LOOPS * BODY
HALVES = 2 * LOOPS + 1
QU = 4
QLOOPS = STEPS // (4 * QU)
QREST = STEPS - QLOOPS * 4 * QU
SPARE = P
STASHED = HALVES // 2
assert STASHED % 2 == 0 and HALVES * HALF <= -(-STEPS // P) * P
assert QU < QREST < 2 * QU
G = -(-STEPS // P)
SLOTS = G * P
GB = 5
GROUPS = NB // GB
BIG = 1e30
EPS = 1e-5
FAR = float(E)
assert 0 < REST <= HALF and GROUPS * GB == NB and STEPS * P % P == 0


def gnn_kernel(nc, x, src, dst, etype, ew, w0, b0, w1, b1, gamma, beta, ws1, wn1, b21, ws2, wn2, b22,
               ww, wb, aw, ab, out):
    f32, i32, bf16 = mybir.dt.float32, mybir.dt.int32, mybir.dt.bfloat16
    ALU, ACT, AX = mybir.AluOpType, mybir.ActivationFunctionType, mybir.AxisListType
    ds = bass.ds

    ctx = ExitStack()
    with ctx:
        def sb(name, shape, dt=f32):
            return ctx.enter_context(nc.sbuf_tensor(name, shape, dt))

        def sem(name):
            return ctx.enter_context(nc.semaphore(name))

        def dram(name, shape, dt=f32):
            return nc.dram_tensor(name, shape, dt, kind="Internal").ap()

        chunk_rec = dram("chunk_rec", (SLOTS, 4 * P + 1))
        block_of_step = dram("block_of_step", (SLOTS,), i32)
        rel_rows = dram("rel_rows", (SLOTS, P))
        reset_flat = dram("reset_flat", (SLOTS * P,))
        src_rows = dram("src_rows", (SLOTS, P))
        lo_rows = dram("lo_rows", (SLOTS, P))
        part_sum = [dram(f"part_sum{k}", (NP + SPARE, D)) for k in range(QU)]
        rel_tab = dram("rel_tab", (NP, R * D))
        node_tab = dram("node_tab", (NP, D))
        hid_tab = dram("hid_tab", (NP, D))
        key_tab = dram("key_tab", (NP, D))
        score_flat = dram("score_flat", (H, SLOTS * P))
        stash = dram("stash", (STASHED * P, HALF * D))
        prefix_tab = dram("prefix_tab", (STEPS * P, H))

        iota_row = sb("iota_row", [P, P])
        iota_part = sb("iota_part", [P, 1])
        step_no = sb("step_no", [P, G])
        block_base = sb("block_base", [P, NB])
        ident = sb("ident", [P, P])
        upto = sb("upto", [P, P])
        ones = sb("ones", [P, P])
        before = sb("before", [P, P])
        spare_row = sb("spare_row", [P, 1])
        zeros = sb("zeros", [P, 4 * P])
        prefix = sb("prefix", [P, STEPS, H])
        raw = prefix[:].rearrange("p x h -> p (x h)")[:, 0:3 * SLOTS].bitcast(i32).rearrange("p (f e) -> p f e", f=3)
        chunk_sb = sb("chunk_sb", [P, G, 4, P])
        step_rec = sb("step_rec", [P, G, 4 * P + 1])
        below = sb("below", [P, NB - 1])
        last_step = sb("last_step", [P, NB - 1])
        step_block = sb("step_block", [P, G])
        step_block_i = sb("step_block_i", [P, G], i32)
        step_base = sb("step_base", [P, G])
        step_chunk = sb("step_chunk", [P, G], i32)
        rel_row = sb("rel_row", [P, G, P])
        valid = sb("valid", [P, G, P])
        invalid_pen = rel_row
        reset_row = sb("reset_row", [P, G, P])
        tmp_row = sb("tmp_row", [P, G, P])
        block_row = sb("block_row", [1, SLOTS], i32)
        idx_src = sb("idx_src", [P, SLOTS], i32)
        idx_rel = sb("idx_rel", [P, SLOTS], i32)
        rel_col = sb("rel_col", [P, SLOTS])
        w_col = sb("w_col", [P, SLOTS])
        src_block = w_col
        idx_slot = sb("idx_slot", [P, 2, HALF], i32)
        rows = sb("rows", [P, 2, HALF, D])
        onehot = sb("onehot", [P, 2, HALF, P])
        rel_bc = sb("rel_bc", [P, 2, HALF * P])
        dup = sb("dup", [P, QU])
        to_spare = sb("to_spare", [P, QU])
        onehot_t = sb("onehot_t", [P, 2, HALF * P])
        msg = sb("msg", [P, 2, HALF, D])
        idx_quarter = idx_slot[:].rearrange("p a (b k) -> p (a b) k", k=QU)
        msg_quarter = msg[:].rearrange("p a (b k) f -> p (a b) k f", k=QU)
        prob = sb("prob", [P, 2, HALF, H])
        z_slot = sb("z_slot", [P, HALF, H])
        u_slot = sb("u_slot", [P, 2, HALF, H])
        step_no_block = sb("step_no_block", [P, NB])
        X = sb("X", [P, NB, D])
        Y = sb("Y", [P, NB, D])
        T = sb("T", [P, NB, D])
        nat_slot = sb("nat_slot", [P, GB, D])
        lhs_slot = sb("lhs_slot", [P, GB, D])
        hout = sb("hout", [P, 2, R * D])
        mean = sb("mean", [P, NB])
        var = sb("var", [P, NB])
        rstd = sb("rstd", [P, NB])
        stats = sb("stats", [P, NB, 6])
        deg = sb("deg", [P, NB])
        rdeg = sb("rdeg", [P, NB])
        has = sb("has", [P, NB])
        src_bc = hout[:, 0, :].rearrange("p (s e) -> p s e", s=2)
        W0, WS1, WN1, WS2, WN2, WW = (sb(n, [P, D]) for n in ("W0", "WS1", "WN1", "WS2", "WN2", "WW"))
        W1 = hout[:, 0, :].rearrange("p (r f) -> p r f", r=R)
        W1T = sb("W1T", [P, R * D])
        B0, GA, BE, B21, B22, WB = (sb(n, [P, D]) for n in ("B0", "GA", "BE", "B21", "B22", "WB"))
        B1 = sb("B1", [P, R * D])
        A_DST, A_SRC = sb("A_DST", [P, H, D // H]), sb("A_SRC", [P, H, D // H])
        AB = sb("AB", [P, H])
        edge_score = sb("edge_score", [P, SLOTS, H])
        score_row = chunk_sb[:].rearrange("p g f e -> p (g f e)").rearrange("p (h g e) -> p h g e", h=H, g=G)
        lanes = step_rec[:].rearrange("p g f -> p (g f)")[:, 0:H * STEPS].rearrange("p (h x) -> p h x", h=H)
        lane_reset = tmp_row[:].rearrange("p g e -> p (g e)")[:, 0:STEPS]
        lane_tail = sb("lane_tail", [P, H])
        lane_flag = sb("lane_flag", [P, 1])
        lane_flag_h = sb("lane_flag_h", [P, H])
        carry_rst = sb("carry_rst", [H, P])
        carry = sb("carry", [H, P + 1])
        carry_col = sb("carry_col", [P, H])
        ends = sb("ends", [P, NB])
        ends_i = sb("ends_i", [P, NB], i32)
        block_sum = sb("block_sum", [P, NB])
        block_cum = sb("block_cum", [P, NB + 1])
        in_max = sb("in_max", [P, NB, H])
        s_src, s_dst = sb("s_src", [P, NB, H]), sb("s_dst", [P, NB, H])
        e_self, e_tmp = sb("e_self", [P, NB, H]), sb("e_tmp", [P, NB, H])
        e_max = sb("e_max", [P, NB, H])
        p_self, den = sb("p_self", [P, NB, H]), sb("den", [P, NB, H])
        node_vals = sb("node_vals", [P, NB, 2 * H])

        stash_rows = T[:, 0:2 * HALF, :].rearrange("p (s k) f -> p s k f", s=2)
        part_slot = [T[:]] + [(edge_score, step_rec)[k % 2][:].rearrange("p a b -> p (a b)")[:, 0:NB * D].rearrange("p (b f) -> p b f", f=D)
                              for k in range(1, QU)]

        acc = ctx.enter_context(nc.psum_tensor("acc", [P, 7 * 512], f32))
        aux = ctx.enter_context(nc.psum_tensor("aux", [P, 512], f32))
        SIDE = NB * D

        s_const, s_pad, s_edges, s_par, s_par2 = (sem(n) for n in ("const", "pad", "edges", "par", "par2"))
        s_x, s_rec_sb, s_rec, s_prev, s_cnt, s_below = (sem(n) for n in ("xin", "rec_sb", "rec", "prev", "cnt", "below"))
        s_chunk, s_steprec, s_bt, s_btd, s_btrow = (sem(n) for n in ("chunk", "steprec", "bt", "btd", "btrow"))
        s_rows_ready, s_rowd, s_tr, s_cols, s_w1t = (sem(n) for n in ("rows_rdy", "rowd", "tr", "cols", "w1t"))
        chain = sem("dve_chain")

        def layers(name, *numbers):
            return {a: sem(f"{name}{a}") for a in numbers}

        half_done, oh_ready = (layers(n, 1, 2, 3, 4) for n in ("half_done", "oh_ready"))
        idx_ready = layers("idx_ready", 1, 2, 3, 4)
        stored, stash_in = ([sem(f"{n}{p}") for p in range(2)] for n in ("stored", "stash_in"))
        gathered = {a: [sem(f"gathered{a}_{p}") for p in range(2)] for a in range(1, 5)}
        oh_plain = sem("oh_plain")
        agg_out, lhs_ready, node_mm = layers("agg_out", 1, 2, 3), layers("lhs_ready", 2, 3), layers("node_mm", 2, 3)
        ln_var, ln_std, x_ready, tab_done = (layers("ln_var", 0, 1, 3, 4), layers("ln_std", 0, 1, 3, 4),
                                             layers("x_ready", 0, 1, 2, 3), layers("tab_done", 2, 3, 4))
        pr_nat, pr_tr, pr_lhs, pr_mm, pr_out = ([sem(f"{n}{a}") for a in range(5)] for n in ("pr_nat", "pr_tr", "pr_lhs", "pr_mm", "pr_out"))
        h_store = [sem(f"h_store{p}") for p in range(2)]
        ln2_var, ln2_std, ln_loop, s_copied = sem("ln2_var"), sem("ln2_std"), sem("ln_loop"), sem("copied")
        s_scores, s_lo, lo_used, sc_mm, sc_used, sc_c = (sem(n) for n in ("scores", "lo", "lo_used", "sc_mm", "sc_used", "sc_c"))
        lo_bc = [sem("lo_bc0"), sem("lo_bc1")]
        s_st, s_srow, s_sflat, s_lanes, s_tail, s_tailT, s_carry, s_carryT, s_prefix, s_preft = (
            sem(n) for n in ("st", "srow_s", "sflat", "lanes_s", "tail", "tailT", "carry_s", "carryT", "prefix_s", "preft"))
        s_degT, s_degP, s_ends, s_inmax, s_eself, s_pself, s_nv = (
            sem(n) for n in ("degT", "degP", "ends_s", "inmax", "eself", "pself", "nv"))
        bc_load, t_ready, expanded, u_ready, p_ready, m_ready, z_done = (
            sem(n) for n in ("bc_load", "t_ready", "expanded", "u_ready", "p_ready", "m_ready", "z_done"))
        bc_load = [bc_load, sem("bc_load1")]
        s_zeroed, bc0, t0_ready, eq_ready, dup_s, idx0_ready = (
            sem(n) for n in ("zeroed", "bc0", "t0_ready", "eq_ready", "dup_s", "idx0_ready"))
        bc0 = [bc0, sem("bc0_1")]
        r_mm, weighted, s_mm, sum_ready, pool_tick, row_free, s_added = (
            sem(n) for n in ("r_mm", "weighted", "s_mm", "sum_ready", "pool_tick", "row_free", "added"))
        s_part = [sem(f"part{k}") for k in range(QU)]
        scattered = [sem(f"scattered{k}") for k in range(QU)]
        s_final, s_out = sem("final"), sem("out_s")

        def rows_of(tab):
            return tab.rearrange("(b p) f -> p b f", p=P)

        block = ctx.enter_context(nc.Block())

        @block.sync
        def _(sp):
            full = (G - 1) * P * P
            whole = (E - full) // P
            sp.wait_ge(s_pad, 1)
            for f, ap in enumerate((src, etype, dst)):
                sp.dma_start(raw[:, f, 0:(G - 1) * P].rearrange("p (g e) -> p g e", e=P),
                             ap[0:full].rearrange("(g p e) -> p g e", p=P, e=P)).then_inc(s_edges, 16)
                sp.dma_start(raw[0:whole, f, (G - 1) * P:SLOTS],
                             ap[full:full + whole * P].rearrange("(p e) -> p e", e=P)).then_inc(s_edges, 16)
                sp.dma_start(raw[whole:whole + 1, f, (G - 1) * P:(G - 1) * P + E - full - whole * P],
                             ap[full + whole * P:E].rearrange("(a e) -> a e", a=1)).then_inc(s_edges, 16)
            sp.dma_start(chunk_sb[:, 0:G - 1, 3, :], ew[0:full].rearrange("(g p e) -> p g e", p=P, e=P)).then_inc(s_edges, 16)
            sp.dma_start(chunk_sb[0:whole, G - 1, 3, :],
                         ew[full:full + whole * P].rearrange("(p e) -> p e", e=P)).then_inc(s_edges, 16)
            sp.dma_start(chunk_sb[whole:whole + 1, G - 1, 3, 0:E - full - whole * P],
                         ew[full + whole * P:E].rearrange("(a e) -> a e", a=1)).then_inc(s_edges, 16)
            sp.dma_start(X[:, 0:NB - 1, :], x[0:(NB - 1) * P, :].rearrange("(b p) f -> p b f", p=P)).then_inc(s_x, 16)
            sp.dma_start(X[0:TAIL, NB - 1, :], x[(NB - 1) * P:N, :]).then_inc(s_x, 16)
            for tile, ap in ((W0, w0), (WS1, ws1), (WN1, wn1), (WS2, ws2), (WN2, wn2), (WW, ww)):
                sp.dma_start(tile[:], ap).then_inc(s_par, 16)
            sp.dma_start(W1, w1.rearrange("r h d -> h r d")).then_inc(s_par, 16)
            sp.wait_ge(s_rec_sb, 1)
            sp.dma_start(chunk_rec[0:SLOTS, 0:4 * P].rearrange("(g p) f -> p g f", p=P),
                         chunk_sb[:].rearrange("p g f e -> p g (f e)")).then_inc(s_rec, 16)
            for g in range(G):
                n = P - (g == G - 1)
                sp.dma_start(chunk_rec[g * P + 1:g * P + n + 1, 4 * P:4 * P + 1],
                             chunk_sb[0:n, g, 2, P - 1:P], allow_slow_non_contiguous=True).then_inc(s_rec, 16)
            sp.dma_start(chunk_rec[0:1, 4 * P:4 * P + 1], ones[0:1, 0:1]).then_inc(s_rec, 16)
            sp.wait_ge(s_bt, 1)
            sp.dma_start(block_of_step.rearrange("(g p) -> p g", p=P), step_block_i[:], allow_slow_non_contiguous=True).then_inc(s_btd, 16)
            sp.wait_ge(s_btd, 16)
            sp.dma_start(block_row[:], block_of_step.rearrange("(a t) -> a t", a=1)).then_inc(s_btrow, 16)
            sp.wait_ge(s_rows_ready, 1)
            sp.dma_start(rel_rows.rearrange("(g p) e -> p g e", p=P), rel_row[:]).then_inc(s_rowd, 16)
            sp.dma_start(reset_flat.rearrange("(g p e) -> p g e", p=P, e=P), reset_row[:]).then_inc(s_rowd, 16)
            sp.dma_start(src_rows.rearrange("(g p) e -> p g e", p=P), step_rec[:, :, 0:P]).then_inc(s_rowd, 16)
            sp.wait_ge(s_lo, 1)
            sp.dma_start(lo_rows.rearrange("(g p) e -> p g e", p=P), tmp_row[:]).then_inc(s_rowd, 16)
            sp.wait_ge(s_rowd, 64)

            def rel_src_quarter(q, p, n):
                for tile, tab in ((rel_bc, rel_rows), (src_bc, src_rows)):
                    sp.dma_start(tile[:, p, 0:n * P],
                                 tab[ds(q * QU, n), :].rearrange("(a t) e -> a (t e)", a=1).to_broadcast([P, n * P])
                                 ).then_inc(bc0[p], 16)

            sp.wait_ge(s_w1t, 1)
            rel_src_quarter(0, 0, QU)
            rel_src_quarter(1, 1, QU)
            with sp.Fori(0, 2 * QLOOPS - 1) as j:
                for p in range(2):
                    sp.wait_ge(idx0_ready, j * 2 + p + 1)
                    rel_src_quarter(j * 2 + p + 2, p, QU)
            sp.wait_ge(idx0_ready, 4 * QLOOPS - 1)
            rel_src_quarter(4 * QLOOPS, 0, QU)
            sp.wait_ge(idx0_ready, 4 * QLOOPS)
            rel_src_quarter(4 * QLOOPS + 1, 1, QREST - QU)
            for k in range(QU):
                sp.wait_ge(scattered[k], 16 * (4 * QLOOPS + 1 + (k < QREST - QU)))
            for k, buf in enumerate(part_sum):
                if k >= 3:
                    sp.wait_ge(s_added, k - 1)
                sp.dma_start(part_slot[k], buf[0:NP, :].rearrange("(b p) f -> p b f", p=P)).then_inc(s_part[k], 16)
            sp.nop().then_inc(h_store[0], 16)
            sp.nop().then_inc(h_store[1], 16)
            with sp.Fori(0, GROUPS) as i:
                for k in range(GB):
                    sp.wait_ge(pr_out[0], i * GB + k + 2)
                    if k % 2:
                        sp.dma_start(rel_tab[ds((i * GB + k) * P, P), :], hout[:, 1, :]).then_inc(h_store[1], 16)
                    else:
                        sp.dma_start(rel_tab[ds((i * GB + k) * P, P), :], hout[:, 0, :]).then_inc(h_store[0], 16)
            for a, tab in ((2, node_tab), (3, hid_tab)):
                sp.wait_ge(x_ready[a - 1], 1)
                sp.dma_start(rows_of(tab), (X if a == 2 else T)[:]).then_inc(tab_done[a], 16)
            sp.wait_ge(s_scores, 1)
            sp.dma_start(rows_of(key_tab), Y[:]).then_inc(tab_done[4], 16)
            def place_rows(it, p, n):
                sp.dma_start(rel_bc[:, p, 0:n * P],
                             lo_rows[ds(it * HALF, n), :].rearrange("(a t) e -> a (t e)", a=1).to_broadcast([P, n * P])
                             ).then_inc(lo_bc[p], 16)

            place_rows(0, 0, HALF)
            place_rows(1, 1, HALF)
            with sp.Fori(0, LOOPS - 1) as j:
                for p in range(2):
                    sp.wait_ge(lo_used, j * 2 + p + 1)
                    place_rows(j * 2 + p + 2, p, HALF)
            sp.wait_ge(lo_used, 2 * LOOPS - 1)
            place_rows(2 * LOOPS, 0, REST)
            sp.wait_ge(s_srow, 1)
            for h in range(H):
                sp.dma_start(score_flat[h, :].rearrange("(g p e) -> p g e", p=P, e=P), score_row[:, h]).then_inc(s_sflat, 16)
            sp.wait_ge(s_sflat, 16 * H)
            for h in range(H):
                sp.dma_start(lanes[:, h, :], score_flat[h, 0:STEPS * P].rearrange("(l x) -> l x", x=STEPS)).then_inc(s_lanes, 16)
            sp.dma_start(lane_reset, reset_flat[0:STEPS * P].rearrange("(l x) -> l x", x=STEPS)).then_inc(s_lanes, 16)
            sp.wait_ge(s_prefix, 1)
            sp.dma_start(prefix_tab.rearrange("(l x) h -> l (x h)", x=STEPS),
                         prefix[:].rearrange("p x h -> p (x h)")).then_inc(s_preft, 16)
            def rel_half(half, p):
                sp.dma_start(rel_bc[:, p, :],
                             rel_rows[ds(half * HALF, HALF), :].rearrange("(a t) e -> a (t e)", a=1).to_broadcast([P, HALF * P])
                             ).then_inc(bc_load[p], 16)

            def stash_half(half, s):
                sp.dma_start(stash_rows[:, s].rearrange("p k f -> p (k f)"), stash[ds(half * P, P), :]).then_inc(stash_in[s], 16)

            for p in range(2):
                sp.wait_ge(stored[p], 16 * (STASHED // 2))
            rel_half(STASHED, 0)
            rel_half(0, 1)
            for s in range(2):
                stash_half(s, s)
            with sp.Fori(0, STASHED // 2 - 1) as j:
                for s in range(2):
                    sp.wait_ge(t_ready, j * 4 + 2 * s + 1)
                    rel_half(j * 2 + (STASHED + s + 1), 0)
                    sp.wait_ge(t_ready, j * 4 + 2 * s + 2)
                    rel_half(j * 2 + (s + 1), 1)
                    sp.wait_ge(m_ready, j * 4 + 2 * s + 2)
                    stash_half(j * 2 + (s + 2), s)
            turn = 2 * STASHED
            sp.wait_ge(t_ready, turn - 3)
            rel_half(HALVES - 2, 0)
            sp.wait_ge(t_ready, turn - 2)
            rel_half(STASHED - 1, 1)
            sp.wait_ge(t_ready, turn - 1)
            rel_half(HALVES - 1, 0)
            sp.wait_ge(s_final, 1)
            sp.dma_start(out[0:(NB - 1) * P, :].rearrange("(b p) f -> p b f", p=P), X[:, 0:NB - 1, :]).then_inc(s_out, 16)
            sp.dma_start(out[(NB - 1) * P:N, :], X[0:TAIL, NB - 1, :]).then_inc(s_out, 16)
            sp.wait_ge(s_out, 32)

        @block.gpsimd
        def _(pool):
            nc.gpsimd.iota(iota_row[:], [[1, P]], base=0, channel_multiplier=0, allow_small_or_imprecise_dtypes=True)
            nc.gpsimd.iota(iota_part[:], [[0, 1]], base=0, channel_multiplier=1, allow_small_or_imprecise_dtypes=True)
            nc.gpsimd.iota(block_base[:], [[P, NB]], base=0, channel_multiplier=0, allow_small_or_imprecise_dtypes=True)
            nc.gpsimd.iota(step_no[:], [[P, G]], base=0, channel_multiplier=1,
                           allow_small_or_imprecise_dtypes=True).then_inc(s_const, 1)
            pool.wait_ge(s_rec, 16 * (G + 2))
            pool.wait_ge(s_chunk, 1)
            for g in range(G):
                nc.gpsimd.indirect_dma_start(step_rec[:, g, :], None, chunk_rec,
                                             bass.IndirectOffsetOnAxis(ap=step_chunk[:, g:g + 1], axis=0)).then_inc(s_steprec, 16)

            def gather_half(a, table, it, p, n):
                pool.wait_ge(idx_ready[a], it + 1)
                pool.sem_inc(pool_tick)
                for k in range(n):
                    nc.gpsimd.indirect_dma_start(rows[:, p, k, :], None, table,
                                                 bass.IndirectOffsetOnAxis(ap=idx_slot[:, p, k:k + 1], axis=0)
                                                 ).then_inc(gathered[a][p], 16)

            def gather(a, table, start=0):
                with pool.Fori(start, LOOPS) as j:
                    for p in range(2):
                        gather_half(a, table, j * 2 + p, p, HALF)
                gather_half(a, table, 2 * LOOPS, 0, REST)

            pool.wait_ge(s_zeroed, 16 * 2 * QU)
            for _ in range(3):
                pool.sem_inc(row_free)

            def scatter_quarter(q, s, n, first=False):
                pool.wait_ge(idx0_ready, q + 1)
                pool.sem_inc(pool_tick)
                pool.wait_ge(sum_ready, q + 3)
                pool.sem_inc(pool_tick)
                for k in range(n):
                    if not first:
                        pool.wait_ge(scattered[k], q * 16)
                        pool.sem_inc(pool_tick)
                    if k == QU - 1:
                        pool.sem_inc(row_free)
                    nc.gpsimd.indirect_dma_start(part_sum[k], bass.IndirectOffsetOnAxis(ap=idx_quarter[:, s, k:k + 1], axis=0),
                                                 msg_quarter[:, s, k, :], None, compute_op=ALU.add).then_inc(scattered[k], 16)

            scatter_quarter(0, 0, QU, first=True)
            with pool.Fori(0, QLOOPS) as j:
                for s in range(4):
                    scatter_quarter(j * 4 + s + 1, (s + 1) % 4, QU)
            scatter_quarter(4 * QLOOPS + 1, 1, QREST - QU)
            pool.wait_ge(h_store[0], 16 * (1 + GROUPS * 3))
            pool.wait_ge(h_store[1], 16 * (1 + GROUPS * 2))
            gather(1, rel_tab.rearrange("n (r f) -> (n r) f", r=R))
            for a, tab in ((2, node_tab), (3, hid_tab)):
                pool.wait_ge(tab_done[a], 16)
                gather(a, tab)
            def keys_half(half, p):
                nc.gpsimd.tensor_copy(idx_slot[:, p, :], idx_src[:, ds(half * HALF, HALF)]).then_inc(idx_ready[4], 1)
                pool.wait_ge(idx_ready[4], half + 1)
                pool.sem_inc(pool_tick)
                for k in range(HALF):
                    nc.gpsimd.indirect_dma_start(rows[:, p, k, :], None, key_tab,
                                                 bass.IndirectOffsetOnAxis(ap=idx_slot[:, p, k:k + 1], axis=0)
                                                 ).then_inc(gathered[4][p], 16)

            pool.wait_ge(tab_done[4], 16)
            for p in range(2):
                keys_half(p, p)
            with pool.Fori(1, STASHED // 2) as j:
                for p in range(2):
                    pool.wait_ge(stored[p], j * 16)
                    keys_half(j * 2 + p, p)
            pool.wait_ge(s_preft, 16)
            pool.wait_ge(s_ends, 1)
            for b in range(NB):
                nc.gpsimd.indirect_dma_start(in_max[:, b, :], None, prefix_tab,
                                             bass.IndirectOffsetOnAxis(ap=ends_i[:, b:b + 1], axis=0)).then_inc(s_inmax, 16)
            for p in range(2):
                pool.wait_ge(stored[p], 16 * (STASHED // 2))
                keys_half(STASHED + p, p)
            with pool.Fori(1, STASHED // 2) as j:
                for p in range(2):
                    pool.wait_ge(m_ready, j * 4 + (2 * p - 3))
                    keys_half(j * 2 + (STASHED + p), p)
            pool.wait_ge(m_ready, 2 * STASHED - 3)
            keys_half(HALVES - 1, 0)

        @block.scalar
        def _(act):
            act.wait_ge(s_pad, 1)
            for buf in part_sum:
                act.dma_start(buf[0:NP, :].rearrange("(b p) f -> p b f", p=P), Y[:]).then_inc(s_zeroed, 16)
                act.dma_start(buf[NP:NP + SPARE, :], Y[:, 0, :]).then_inc(s_zeroed, 16)
            for tile, ap in ((B0, b0), (GA, gamma), (BE, beta), (B21, b21), (B22, b22), (WB, wb)):
                act.dma_start(tile[:], ap.rearrange("(a f) -> a f", a=1).to_broadcast([P, D])).then_inc(s_par2, 16)
            act.dma_start(B1[:], b1.rearrange("r f -> (r f)").rearrange("(a f) -> a f", a=1).to_broadcast([P, R * D])).then_inc(s_par2, 16)
            act.dma_start(A_DST[:], aw[:, 0:D // H].rearrange("(a h) f -> a h f", a=1).to_broadcast([P, H, D // H])).then_inc(s_par2, 16)
            act.dma_start(A_SRC[:], aw[:, D // H:2 * D // H].rearrange("(a h) f -> a h f", a=1).to_broadcast([P, H, D // H])).then_inc(s_par2, 16)
            act.dma_start(AB[:], ab.rearrange("(a h) -> a h", a=1).to_broadcast([P, H])).then_inc(s_par2, 16)

            def sums_to_lhs(a):
                act.wait_ge(half_done[a], 2 + HALVES)
                with act.Fori(0, GROUPS) as i:
                    act.wait_ge(node_mm[a], i + 1)
                    nc.scalar.copy(lhs_slot[:].rearrange("p b f -> p (b f)"), acc[:, ds(i * GB * D, GB * D)]).then_inc(lhs_ready[a], 1)

            def root(a, v, s, var_ready, std_ready):
                act.wait_ge(var_ready, v)
                nc.scalar.activation(rstd[:], var[:], ACT.Sqrt).then_inc(std_ready, 1)

            def project(q, source, ready, count):
                act.wait_ge(ready, count)
                act.nop().then_inc(pr_lhs[q], 1)
                with act.Fori(0, GROUPS) as i:
                    act.wait_ge(pr_tr[q], i * GB + 1)
                    nc.scalar.copy(nat_slot[:], source[:, ds(i * GB, GB), :]).then_inc(pr_nat[q], 1)
                    for k in range(GB):
                        act.wait_ge(pr_tr[q], i * GB + k + 2)
                        act.wait_ge(pr_mm[q], i * GB + max(k, 1))
                        nc.scalar.copy(lhs_slot[:, k % 2, :], acc[:, (k % 2) * 512:(k % 2) * 512 + P]).then_inc(pr_lhs[q], 1)

            def weigh_quarter(q, s, n):
                p = s % 2
                act.wait_ge(r_mm, q + 1)
                for k in range(n):
                    last = nc.scalar.activation(rows[:, p, k, :], acc[:, p * 512 + k * D:p * 512 + (k + 1) * D], ACT.Copy,
                                                scale=w_col[:, ds(q * QU + k, 1)])
                last.then_inc(weighted, 1)
                act.wait_ge(s_mm, q + 3)
                act.wait_ge(row_free, q + 1)
                nc.scalar.copy(msg_quarter[:, s, 0:n, :].rearrange("p k f -> p (k f)"), acc[:, (2 + p) * 512:(2 + p) * 512 + n * D]).then_inc(sum_ready, 1)

            for _ in range(2):
                act.nop().then_inc(sum_ready, 1)
            act.wait_ge(s_cols, 1)
            nc.scalar.activation(rstd[:, 0:1], w_col[:, 0:1], ACT.Copy)
            with act.Fori(0, QLOOPS) as j:
                for s in range(4):
                    weigh_quarter(j * 4 + s, s, QU)
            weigh_quarter(4 * QLOOPS, 0, QU)
            weigh_quarter(4 * QLOOPS + 1, 1, QREST - QU)
            project(4, T, s_added, QU)
            root(0, 1, 1, ln_var[0], ln_std[0])
            project(0, X, x_ready[0], 1)
            root(1, 1, 1, ln_var[1], ln_std[1])
            root(1, 1, 1, ln2_var, ln2_std)
            project(1, X, x_ready[1], 1)
            sums_to_lhs(2)
            project(2, T, x_ready[2], 1)
            sums_to_lhs(3)
            root(3, 1, 1, ln_var[3], ln_std[3])
            project(3, X, x_ready[3], 1)
            with act.Fori(0, STASHED // 2) as j:
                for p in range(2):
                    act.wait_ge(gathered[4][p], j * (16 * HALF) + 16 * HALF)
                    act.dma_start(stash[ds((j * 2 + p) * P, P), :], rows[:, p].rearrange("p k f -> p (k f)")).then_inc(stored[p], 16)
            act.wait_ge(s_eself, 1)
            nc.scalar.activation(p_self[:], e_tmp[:], ACT.Exp).then_inc(s_pself, 1)

            def exp_half(turn, p):
                act.wait_ge(u_ready, turn + 1)
                nc.scalar.activation(prob[:, p], u_slot[:, p], ACT.Exp).then_inc(p_ready, 1)

            with act.Fori(0, STASHED) as j:
                for p in range(2):
                    exp_half(j * 2 + p, p)
            exp_half(2 * STASHED, 0)
            root(4, 1, 1, ln_var[4], ln_std[4])

        @block.vector
        def _(dve):
            V = nc.vector
            count = [0]

            def then(ins):
                count[0] += 1
                ins.then_inc(chain, 1)
                dve.wait_ge(chain, count[0])

            V.memset(raw[:, 0:2, (G - 1) * P:SLOTS], 0)
            V.memset(raw[:, 2, (G - 1) * P:SLOTS], E)
            V.memset(X[:, NB - 1, :], 0.0)
            V.memset(ones[:], 1.0)
            V.memset(zeros[:], 0.0)
            V.memset(Y[:], 0.0)
            then(V.memset(chunk_sb[:, G - 1, 3, :], 0.0))
            V.memset(carry[:, 0:1], -BIG).then_inc(s_pad, 1)
            dve.wait_ge(s_const, 1)
            V.tensor_scalar(ident[:], iota_row[:], iota_part[:, 0:1], None, ALU.is_equal)
            V.tensor_scalar(before[:], iota_row[:], iota_part[:, 0:1], None, ALU.is_lt)
            V.tensor_scalar(step_no_block[:], block_base[:], 1.0 / P, None, ALU.mult)
            V.tensor_scalar(spare_row[:], iota_part[:], float(NP), None, ALU.add)
            V.tensor_scalar(upto[:], iota_row[:], iota_part[:, 0:1], None, ALU.is_ge)
            dve.wait_ge(s_edges, 16 * 12)
            then(V.tensor_copy(chunk_sb[:, :, 0:3, :], raw.rearrange("p f (g e) -> p g f e", e=P)))
            V.engine_nop().then_inc(s_rec_sb, 1)
            ended = tmp_row[:].rearrange("p g e -> p (g e)")[:, 0:(NB - 1) * G].rearrange("p (b g) -> p b g", g=G)
            then(V.tensor_tensor(ended, chunk_sb[:, :, 2, P - 1][:, None, :].to_broadcast([P, NB - 1, G]),
                                 block_base[:, 1:NB, None].to_broadcast([P, NB - 1, G]), ALU.is_lt))
            V.tensor_reduce(below[:], ended, AX.X, ALU.add).then_inc(s_cnt, 1)
            dve.wait_ge(s_below, 1)
            then(V.scalar_tensor_tensor(last_step[:], block_base[:, 0:NB - 1], 1.0 / P, aux[:, 0:NB - 1], ALU.mult, ALU.add))
            for g in range(G):
                then(V.tensor_scalar(tmp_row[:, 0, 0:NB - 1], last_step[:], step_no[:, g:g + 1], 0.0, ALU.is_lt, ALU.add,
                                     accum_out=step_block[:, g:g + 1]))
            then(V.tensor_tensor(step_base[:], step_no[:], step_block[:], ALU.subtract))
            V.tensor_copy(step_chunk[:], step_base[:]).then_inc(s_chunk, 1)
            V.tensor_copy(step_block_i[:], step_block[:]).then_inc(s_bt, 1)
            dve.wait_ge(s_chunk, 1)
            then(V.tensor_scalar(step_base[:], step_block[:], float(P), None, ALU.mult))
            dve.wait_ge(s_steprec, 16 * G)
            fields = step_rec[:, :, 0:4 * P].rearrange("p g (f e) -> p g f e", f=4)
            f_src, f_typ, f_dst = (fields[:, :, f, :] for f in range(3))
            then(V.tensor_tensor(rel_row[:], f_dst, step_base[:, :, None].to_broadcast([P, G, P]), ALU.subtract))
            then(V.tensor_scalar(valid[:], rel_row[:], 0.0, None, ALU.is_ge))
            then(V.scalar_tensor_tensor(valid[:], rel_row[:], float(P), valid[:], ALU.is_lt, ALU.mult))
            then(V.scalar_tensor_tensor(rel_row[:], rel_row[:], 1.0, valid[:], ALU.add, ALU.mult))
            then(V.tensor_scalar(rel_row[:], rel_row[:], 1.0, None, ALU.subtract))
            V.tensor_tensor(tmp_row[:, :, 1:P], f_dst[:, :, 1:P], f_dst[:, :, 0:P - 1], ALU.not_equal)
            then(V.tensor_tensor(tmp_row[:, :, 0:1], f_dst[:, :, 0:1], step_rec[:, :, 4 * P:4 * P + 1], ALU.not_equal))
            then(V.scalar_tensor_tensor(reset_row[:], tmp_row[:], -BIG, valid[:], ALU.mult, ALU.mult))
            then(V.scalar_tensor_tensor(f_typ, f_src, float(R), f_typ, ALU.mult, ALU.add))
            V.engine_nop().then_inc(s_rows_ready, 1)
            lo_i = raw[:, 0, :].rearrange("p (g e) -> p g e", e=P)
            then(V.tensor_copy(lo_i, f_src))
            then(V.tensor_scalar(lo_i, lo_i, P - 1, None, ALU.bitwise_and))
            V.tensor_copy(tmp_row[:], lo_i).then_inc(s_lo, 1)
            dve.wait_ge(s_tr, 1)
            cols = acc[:].rearrange("p (g f t) -> p g f t", g=G, f=4)
            for f, tile in enumerate((idx_src, idx_rel, rel_col, w_col)):
                then(V.tensor_copy(tile[:].rearrange("p (g t) -> p g t", t=P), cols[:, :, f, :]))
            V.engine_nop().then_inc(s_cols, 1)
            dve.wait_ge(s_x, 32)
            dve.wait_ge(s_par2, 160)
            dve.wait_ge(s_zeroed, 16 * 2 * QU)
            dve.wait_ge(s_w1t, 1)
            then(V.tensor_copy(W1T[:], acc[:, 0:R * D]))
            V.engine_nop().then_inc(s_w1t, 1)

            def prepare_half(a, idx, it, p, n):
                dve.wait_ge(half_done[a], it + 1)
                V.tensor_copy(idx_slot[:, p, 0:n], idx[:, ds(it * HALF, n)]).then_inc(idx_ready[a], 1)
                V.tensor_tensor(onehot[:, p, 0:n, :], iota_row[:, None, :].to_broadcast([P, n, P]),
                                rel_col[:, ds(it * HALF, n), None].to_broadcast([P, n, P]), ALU.is_equal).then_inc(oh_ready[a], 1)

            def prime(a, idx):
                for p in range(2):
                    prepare_half(a, idx, p, p, HALF)

            def prepare(a, idx):
                with dve.Fori(1, LOOPS) as j:
                    for p in range(2):
                        prepare_half(a, idx, j * 2 + p, p, HALF)
                prepare_half(a, idx, 2 * LOOPS, 0, REST)

            def over(v):
                return v[:, :, None].to_broadcast([P, NB, D])

            halves_of = stats[:].rearrange("p b (h v) -> p b h v", h=2)
            loops_done = [0]

            def grouped(step):
                with dve.Fori(0, GROUPS) as i:
                    for k in range(GB):
                        last = step(i * GB + k, (i * GB + k) * D)
                    last.then_inc(ln_loop, 1)
                loops_done[0] += GROUPS
                dve.wait_ge(ln_loop, loops_done[0])

            def moments(v, var_ready, std_ready):
                flat = v[:].rearrange("p b f -> p (b f)")
                grouped(lambda b, c: V.bn_stats(stats[:].rearrange("p b v -> p (b v)")[:, ds(b * 6, 6)], flat[:, ds(c, D)]))
                V.tensor_tensor(mean[:], halves_of[:, :, 0, 1], halves_of[:, :, 1, 1], ALU.add)
                V.tensor_tensor(rstd[:], halves_of[:, :, 0, 1], halves_of[:, :, 1, 1], ALU.subtract)
                then(V.tensor_tensor(var[:], halves_of[:, :, 0, 2], halves_of[:, :, 1, 2], ALU.add))
                V.tensor_scalar(mean[:], mean[:], 0.5, None, ALU.mult)
                V.tensor_scalar(var[:], var[:], 1.0 / D, EPS, ALU.mult, ALU.add)
                then(V.scalar_tensor_tensor(rstd[:], rstd[:], 0.25, rstd[:], ALU.mult, ALU.mult))
                V.tensor_tensor(var[:], var[:], rstd[:], ALU.add).then_inc(var_ready, 1)
                dve.wait_ge(std_ready, 1)
                then(V.reciprocal(rstd[:], rstd[:]))

            def normalize(src_, dst_, var_ready, std_ready):
                moments(src_, var_ready, std_ready)
                a, b_ = src_[:].rearrange("p b f -> p (b f)"), dst_[:].rearrange("p b f -> p (b f)")
                grouped(lambda b, c: V.tensor_scalar(b_[:, ds(c, D)], a[:, ds(c, D)], mean[:, ds(b, 1)], rstd[:, ds(b, 1)],
                                                     ALU.subtract, ALU.mult))

            def signal(s):
                V.engine_nop().then_inc(s, 1)

            flat_acc = acc[:, 0:NB * D].rearrange("p (b f) -> p b f", f=D)

            def projected(q, bias):
                V.engine_nop().then_inc(pr_out[q], 1)
                with dve.Fori(0, GROUPS) as i:
                    for k in range(GB):
                        dve.wait_ge(pr_mm[q], i * GB + k + 2)
                        V.tensor_tensor(Y[:, ds(i * GB + k, 1), :], acc[:, (2 + k % 2) * 512:(2 + k % 2) * 512 + P][:, None, :], bias[:, None, :],
                                        ALU.add).then_inc(pr_out[q], 1)

            first_sum = hout[:, 1, 0:QU * P].rearrange("p (k e) -> p k e", e=P)

            def sources_quarter(q, s, n):
                p = s % 2
                dve.wait_ge(s_mm, q + 1)
                dve.wait_ge(bc0[p], (q - p) * 16 + 32)
                V.tensor_scalar(onehot_t[:, p, 0:n * P], rel_bc[:, p, 0:n * P], iota_part[:, 0:1], None, ALU.is_equal).then_inc(t0_ready, 1)
                V.tensor_tensor(onehot[:, p, 0:n, :], src_bc[:, p, 0:n * P].rearrange("p (k e) -> p k e", e=P),
                                idx_src[:, ds(q * QU, n), None].to_broadcast([P, n, P]), ALU.is_equal).then_inc(eq_ready, 1)
                dve.wait_ge(eq_ready, q + 1)
                V.tensor_tensor(first_sum[:, 0:n, :], onehot[:, p, 0:n, :], before[:, None, :].to_broadcast([P, n, P]), ALU.mult).then_inc(dup_s, 1)
                V.tensor_scalar(to_spare[:, 0:n], idx_src[:, ds(q * QU, n)], -1.0, spare_row[:, 0:1], ALU.mult, ALU.add)
                dve.wait_ge(dup_s, q * 3 + 1)
                V.tensor_reduce(dup[:, 0:n], first_sum[:, 0:n, :], AX.X, ALU.add).then_inc(dup_s, 1)
                dve.wait_ge(dup_s, q * 3 + 2)
                V.scalar_tensor_tensor(dup[:, 0:n], dup[:, 0:n], 0.0, to_spare[:, 0:n], ALU.is_gt, ALU.mult).then_inc(dup_s, 1)
                dve.wait_ge(dup_s, q * 3 + 3)
                dve.wait_ge(row_free, q + 1)
                V.tensor_tensor(idx_quarter[:, s, 0:n], dup[:, 0:n], idx_src[:, ds(q * QU, n)], ALU.add).then_inc(idx0_ready, 1)

            with dve.Fori(0, QLOOPS) as j:
                for s in range(4):
                    sources_quarter(j * 4 + s, s, QU)
            sources_quarter(4 * QLOOPS, 0, QU)
            sources_quarter(4 * QLOOPS + 1, 1, QREST - QU)
            dve.wait_ge(s_part[0], 16)
            V.engine_nop().then_inc(s_added, 1)
            for k in range(1, QU):
                dve.wait_ge(s_part[k], 16)
                V.tensor_tensor(T[:], T[:], part_slot[k], ALU.add).then_inc(s_added, 1)
                dve.wait_ge(s_added, k + 1)
            projected(4, B0)
            dve.wait_ge(pr_out[4], NB + 1)
            then(V.tensor_tensor(Y[:], Y[:], X[:], ALU.add))
            normalize(Y, X, ln_var[0], ln_std[0])
            signal(x_ready[0])
            V.engine_nop().then_inc(pr_out[0], 1)
            with dve.Fori(0, GROUPS) as i:
                for k in range(GB):
                    dve.wait_ge(pr_mm[0], i * GB + k + 2)
                    if k % 2:
                        dve.wait_ge(h_store[1], i * 32 + (k // 2) * 16 + 16)
                    else:
                        dve.wait_ge(h_store[0], i * 48 + (k // 2) * 16 + 16)
                    V.tensor_tensor(hout[:, k % 2, :], acc[:, (k % 2 + 1) * R * D:(k % 2 + 2) * R * D], B1[:], ALU.add).then_inc(pr_out[0], 1)

            prime(1, idx_rel)
            V.tensor_copy(T[:], X[:]).then_inc(s_copied, 1)
            dve.wait_ge(s_copied, 1)
            then(V.tensor_tensor(X[:], X[:], BE[:, None, :].to_broadcast([P, NB, D]), ALU.add))
            prepare(1, idx_rel)
            dve.wait_ge(half_done[1], 2 + HALVES)
            V.tensor_copy(deg[:], acc[:, SIDE:SIDE + NB])
            then(V.tensor_tensor(Y[:], T[:], flat_acc, ALU.add))
            signal(agg_out[1])
            moments(Y, ln_var[1], ln_std[1])
            y, t, xb = (v[:].rearrange("p b f -> p (b f)") for v in (Y, T, X))
            grouped(lambda b, c: V.scalar_tensor_tensor(t[:, ds(c, D)], y[:, ds(c, D)], mean[:, ds(b, 1)], GA[:], ALU.subtract, ALU.mult))
            grouped(lambda b, c: V.scalar_tensor_tensor(y[:, ds(c, D)], t[:, ds(c, D)], rstd[:, ds(b, 1)], xb[:, ds(c, D)], ALU.mult, ALU.add))
            normalize(Y, X, ln2_var, ln2_std)
            signal(x_ready[1])
            then(V.tensor_scalar(rdeg[:], deg[:], 1.0, None, ALU.max))
            then(V.reciprocal(rdeg[:], rdeg[:]))
            then(V.tensor_scalar(has[:], deg[:], 0.0, None, ALU.is_gt))

            for a, bias in ((2, B21), (3, B22)):
                prime(a, idx_src)
                projected(a - 1, bias)
                prepare(a, idx_src)
                dve.wait_ge(node_mm[a], 1 + GROUPS)
                dve.wait_ge(pr_out[a - 1], NB + 1)
                then(V.tensor_tensor(T[:], flat_acc, over(rdeg), ALU.mult))
                signal(agg_out[a])
                then(V.tensor_tensor(T[:], T[:], Y[:], ALU.add))
                if a == 2:
                    then(V.tensor_scalar(T[:], T[:], 0.0, None, ALU.max))
                    signal(x_ready[2])
                else:
                    then(V.tensor_tensor(Y[:], T[:], X[:], ALU.add))
                    normalize(Y, X, ln_var[3], ln_std[3])
                    signal(x_ready[3])

            projected(3, WB)
            dve.wait_ge(pr_out[3], NB + 1)
            for A, s in ((A_SRC, s_src), (A_DST, s_dst)):
                then(V.tensor_tensor(T[:], Y[:], A[:].rearrange("p h f -> p (h f)")[:, None, :].to_broadcast([P, NB, D]), ALU.mult))
                then(V.tensor_reduce(s[:].rearrange("p b h -> p (b h)"), T[:].rearrange("p b (h f) -> p (b h) f", h=H), AX.X, ALU.add))
            then(V.tensor_tensor(s_dst[:], s_dst[:], AB[:, None, :].to_broadcast([P, NB, H]), ALU.add))
            signal(s_scores)
            dve.wait_ge(s_degP, 1)
            V.tensor_copy(block_sum[:], aux[:, P:P + NB])
            then(V.memset(block_cum[:, 0:1], 0.0))
            then(V.tensor_tensor_scan(block_cum[:, 1:NB + 1], zeros[:, 0:NB], block_sum[:], 0.0, ALU.add, ALU.add))
            then(V.tensor_tensor(ends[:], aux[:, 0:NB], block_cum[:, 0:NB], ALU.add))
            then(V.scalar_tensor_tensor(ends[:], ends[:], -1.0, block_base[:], ALU.add, ALU.add))
            then(V.tensor_scalar(ends[:], ends[:], 0.0, None, ALU.max))
            V.tensor_copy(ends_i[:], ends[:]).then_inc(s_ends, 1)

            V.memset(edge_score[:, STEPS:SLOTS, :], 0.0)
            hi_i = raw[:, 0, :]
            then(V.tensor_scalar(hi_i, idx_src[:], 7, None, ALU.arith_shift_right))
            then(V.tensor_copy(src_block[:], hi_i))
            for _ in range(2):
                V.engine_nop().then_inc(sc_used, 1)

            def place_hot(it, j, p, n):
                dve.wait_ge(lo_bc[p], j * 16 + 16)
                V.tensor_scalar(onehot_t[:, p, 0:n * P], rel_bc[:, p, 0:n * P], iota_part[:, 0:1], None, ALU.is_equal).then_inc(lo_used, 1)

            def choose_half(it, p, n):
                in_block = onehot[:, p, :, 0:NB]
                chosen = msg[:, p, :, 0:NB * H].rearrange("p k (b h) -> p k b h", h=H)
                V.tensor_tensor(in_block[:, 0:n, :], step_no_block[:, None, :].to_broadcast([P, n, NB]),
                                src_block[:, ds(it * HALF, n), None].to_broadcast([P, n, NB]), ALU.is_equal).then_inc(sc_c, 1)
                dve.wait_ge(sc_c, it * 2 + 1)
                dve.wait_ge(sc_mm, it + 1)
                for c in range(0, n, QU):
                    m = min(QU, n - c)
                    bank = acc[:, (2 * p + c // QU) * 512:(2 * p + c // QU) * 512 + m * NB * H].rearrange("p (k b h) -> p k b h", b=NB, h=H)
                    last = V.tensor_tensor(chosen[:, c:c + m], bank, in_block[:, c:c + m, :, None].to_broadcast([P, m, NB, H]), ALU.mult)
                last.then_inc(sc_used, 1)
                dve.wait_ge(sc_used, it + 3)
                V.tensor_reduce(edge_score[:, ds(it * HALF, n), :], chosen[:, 0:n].rearrange("p k b h -> p k h b"), AX.X, ALU.add).then_inc(sc_c, 1)

            place_hot(0, 0, 0, HALF)
            place_hot(1, 0, 1, HALF)
            with dve.Fori(0, LOOPS - 1) as j:
                for p in range(2):
                    choose_half(j * 2 + p, p, HALF)
                    place_hot(j * 2 + p + 2, j + 1, p, HALF)
            choose_half(2 * LOOPS - 2, 0, HALF)
            place_hot(2 * LOOPS, LOOPS, 0, REST)
            choose_half(2 * LOOPS - 1, 1, HALF)
            choose_half(2 * LOOPS, 0, REST)
            dve.wait_ge(sc_c, 2 * HALVES)
            signal(s_st)
            then(V.tensor_scalar(invalid_pen[:], valid[:], 1.0, BIG, ALU.subtract, ALU.mult))
            dve.wait_ge(s_tr, 1 + H)
            for h in range(H):
                then(V.tensor_tensor(score_row[:, h], cols[:, :, h, :], valid[:], ALU.mult))
                then(V.tensor_tensor(score_row[:, h], score_row[:, h], invalid_pen[:], ALU.add))
            signal(s_srow)
            dve.wait_ge(s_lanes, 16 * (H + 1))
            for h in range(H):
                V.tensor_tensor_scan(prefix[:, :, h], lane_reset, lanes[:, h, :], -BIG, ALU.add, ALU.max)
            then(V.tensor_reduce(lane_flag[:], lane_reset, AX.X, ALU.min))
            then(V.tensor_copy(lane_flag_h[:], lane_flag[:, 0:1].to_broadcast([P, H])))
            V.tensor_copy(lane_tail[:], prefix[:, STEPS - 1, :]).then_inc(s_tail, 1)
            dve.wait_ge(s_tailT, 1)
            then(V.tensor_copy(carry_rst[:], aux[0:H, P:2 * P]))
            then(V.tensor_tensor_scan(carry[:, 1:P + 1], carry_rst[:], aux[0:H, 0:P], -BIG, ALU.add, ALU.max))
            V.engine_nop().then_inc(s_carry, 1)
            dve.wait_ge(s_carryT, 1)
            then(V.tensor_copy(carry_col[:], aux[:, 2 * P:2 * P + H]))
            for h in range(H):
                then(V.tensor_tensor_scan(prefix[:, :, h], lane_reset, lanes[:, h, :], carry_col[:, h:h + 1], ALU.add, ALU.max))
            V.engine_nop().then_inc(s_prefix, 1)
            dve.wait_ge(s_inmax, 16 * NB)
            hasb = has[:, :, None].to_broadcast([P, NB, H])
            then(V.tensor_tensor(in_max[:], in_max[:], hasb, ALU.mult))
            then(V.tensor_scalar(den[:], hasb, 1.0, BIG, ALU.subtract, ALU.mult))
            then(V.tensor_tensor(in_max[:], in_max[:], den[:], ALU.add))
            then(V.tensor_tensor(e_max[:], in_max[:], s_src[:], ALU.max))
            then(V.tensor_tensor(e_max[:], e_max[:], s_dst[:], ALU.add))
            then(V.scalar_tensor_tensor(e_max[:], e_max[:], 0.2, e_max[:], ALU.mult, ALU.max))
            then(V.tensor_tensor(e_self[:], s_src[:], s_dst[:], ALU.add))
            then(V.scalar_tensor_tensor(e_self[:], e_self[:], 0.2, e_self[:], ALU.mult, ALU.max))
            then(V.tensor_tensor(e_tmp[:], e_self[:], e_max[:], ALU.subtract))
            V.tensor_copy(node_vals[:, :, 0:H], s_dst[:])
            then(V.tensor_copy(node_vals[:, :, H:2 * H], e_max[:]))
            signal(s_eself)

            def turned_hot(turn, j, p):
                dve.wait_ge(bc_load[p], j * 16 + 16)
                V.tensor_scalar(onehot_t[:, p, :], rel_bc[:, p, :], iota_part[:, 0:1], None, ALU.is_equal).then_inc(t_ready, 1)

            def attend(turn, half, p, arrived, count, keys, more=None):
                dve.wait_ge(half_done[4], turn + 1)
                V.tensor_tensor(onehot[:, p], iota_row[:, None, :].to_broadcast([P, HALF, P]),
                                rel_col[:, ds(half * HALF, HALF), None].to_broadcast([P, HALF, P]), ALU.is_equal).then_inc(oh_ready[4], 1)
                if more is not None:
                    dve.wait_ge(expanded, turn + 1)
                    turned_hot(turn + 1, more, 1 - p)
                dve.wait_ge(expanded, turn + 2)
                ex = aux[:, p * HALF * 2 * H:(p + 1) * HALF * 2 * H].rearrange("p (k v) -> p k v", v=2 * H)
                V.tensor_tensor(z_slot[:], ex[:, :, 0:H], edge_score[:, ds(half * HALF, HALF), :], ALU.add).then_inc(z_done, 1)
                dve.wait_ge(z_done, turn * 3 + 1)
                V.scalar_tensor_tensor(z_slot[:], z_slot[:], 0.2, z_slot[:], ALU.mult, ALU.max).then_inc(z_done, 1)
                dve.wait_ge(z_done, turn * 3 + 2)
                V.tensor_tensor(z_slot[:], z_slot[:], ex[:, :, H:2 * H], ALU.subtract).then_inc(z_done, 1)
                dve.wait_ge(z_done, turn * 3 + 3)
                V.tensor_scalar(u_slot[:, p], z_slot[:], 0.0, None, ALU.min).then_inc(u_ready, 1)
                dve.wait_ge(p_ready, turn + 1)
                dve.wait_ge(arrived, count)
                V.tensor_tensor(msg[:, p].rearrange("p k (h f) -> p (k h) f", h=H), keys.rearrange("p k (h f) -> p (k h) f", h=H),
                                prob[:, p].rearrange("p k h -> p (k h)")[:, :, None].to_broadcast([P, HALF * H, D // H]),
                                ALU.mult).then_inc(m_ready, 1)

            turned_hot(0, 0, 0)
            with dve.Fori(0, STASHED // 2) as j:
                for s in range(2):
                    attend(j * 4 + 2 * s, j * 2 + (STASHED + s), 0, gathered[4][s], (j + STASHED // 2) * (16 * HALF) + 16 * HALF, rows[:, s], more=j * 2 + s)
                    attend(j * 4 + (2 * s + 1), j * 2 + s, 1, stash_in[s], j * 16 + 16, stash_rows[:, s], more=j * 2 + (s + 1))
            attend(2 * STASHED, HALVES - 1, 0, gathered[4][0], (STASHED + 1) * 16 * HALF, rows[:, 0])
            dve.wait_ge(s_pself, 1)
            pf = p_self[:].rearrange("p b h -> p (b h)")
            then(V.tensor_tensor(T[:].rearrange("p b (h f) -> p (b h) f", h=H), Y[:].rearrange("p b (h f) -> p (b h) f", h=H),
                                 pf[:, :, None].to_broadcast([P, NB * H, D // H]), ALU.mult))
            dve.wait_ge(half_done[4], 2 + HALVES)
            then(V.tensor_tensor(T[:], T[:], flat_acc, ALU.add))
            then(V.tensor_tensor(den[:].rearrange("p b h -> p (b h)"), pf, acc[:, SIDE:SIDE + NB * H], ALU.add))
            then(V.reciprocal(den[:], den[:]))
            then(V.tensor_tensor(T[:].rearrange("p b (h f) -> p (b h) f", h=H), T[:].rearrange("p b (h f) -> p (b h) f", h=H),
                                 den[:].rearrange("p b h -> p (b h)")[:, :, None].to_broadcast([P, NB * H, D // H]), ALU.mult))
            then(V.tensor_tensor(Y[:], T[:], X[:], ALU.add))
            normalize(Y, X, ln_var[4], ln_std[4])
            signal(s_final)

        @block.tensor
        def _(pe):
            M = nc.tensor
            pe.wait_ge(s_cnt, 1)
            M.matmul(aux[:, 0:NB - 1], ones[:], below[:], start=True, stop=True).then_inc(s_below, 1)
            pe.wait_ge(s_rows_ready, 1)
            fields = step_rec[:, :, 0:4 * P].rearrange("p g (f e) -> p g f e", f=4)
            for g in range(G):
                for f, row in enumerate((fields[:, g, 0, :], fields[:, g, 1, :], rel_row[:, g, :], fields[:, g, 3, :])):
                    last = M.transpose(acc[:, (g * 4 + f) * P:(g * 4 + f + 1) * P], row, ident[:])
            last.then_inc(s_tr, 1)
            pe.wait_ge(s_cols, 1)
            pe.wait_ge(s_par, 16 * 7)
            for r in range(R):
                last = M.transpose(acc[:, r * D:(r + 1) * D], W1[:, r, :], ident[:])
            last.then_inc(s_w1t, 1)
            pe.wait_ge(s_w1t, 2)
            pe.wait_ge(s_btrow, 16)

            def clear(a):
                for k in range(7):
                    M.matmul(acc[:, k * 512:(k + 1) * 512], zeros[:, 0:P], zeros[:], start=True, stop=True)

            def begin(a):
                for _ in range(2):
                    pe.nop().then_inc(half_done[a], 1)

            def aggregate(a, transposed, side=False):
                def half(it, j, p, n):
                    _, blk = nc.values_load_multi_w_load_instructions(
                        block_row[0:1, ds(it * HALF, n)], engines=[pe.engine], min_val=0, max_val=NB - 1,
                        skip_runtime_bounds_check_because="a step's block counts which of the NB - 1 others lie before it")
                    pe.wait_ge(oh_ready[a], it + 1)
                    pe.wait_ge(gathered[a][p], j * 16 * HALF + 16 * n)
                    for k in range(n):
                        lhs, rhs = onehot[:, p, k, :], rows[:, p, k, :]
                        if transposed:
                            lhs, rhs = rhs, lhs
                        last = M.matmul(acc[:, ds(blk[k] * D, D)], lhs, rhs, start=False, stop=True, skip_group_check=True)
                        if side:
                            last = M.matmul(acc[:, ds(blk[k] + SIDE, 1)], lhs, ones[:, 0:1], start=False, stop=True, skip_group_check=True)
                    last.then_inc(half_done[a], 1)

                with pe.Fori(0, LOOPS) as j:
                    for p in range(2):
                        half(j * 2 + p, j, p, HALF)
                half(2 * LOOPS, LOOPS, 0, REST)

            def node_product(a, W):
                pe.nop().then_inc(node_mm[a], 1)
                with pe.Fori(0, GROUPS) as i:
                    pe.wait_ge(lhs_ready[a], i + 1)
                    for k in range(GB):
                        last = M.matmul(acc[:, ds(i * GB * D + k * D, D)], lhs_slot[:, k, :], W[:], start=True, stop=True)
                    last.then_inc(node_mm[a], 1)

            def project(q, W, wide=False):
                pe.nop().then_inc(pr_tr[q], 1)
                pe.nop().then_inc(pr_mm[q], 1)
                with pe.Fori(0, GROUPS) as i:
                    pe.wait_ge(pr_nat[q], i + 1)

                    def turn(k):
                        pe.wait_ge(pr_lhs[q], i * GB + max(k, 1))
                        M.transpose(acc[:, (k % 2) * 512:(k % 2) * 512 + P], nat_slot[:, k, :], ident[:]).then_inc(pr_tr[q], 1)

                    turn(0)
                    for k in range(GB):
                        if k + 1 < GB:
                            turn(k + 1)
                        pe.wait_ge(pr_lhs[q], i * GB + k + 2)
                        pe.wait_ge(pr_out[q], i * GB + max(k, 1))
                        if wide:
                            for c in range(2):
                                last = M.matmul(acc[:, (k % 2 + 1) * R * D + c * 512:(k % 2 + 1) * R * D + (c + 1) * 512],
                                                lhs_slot[:, k % 2, :], W[:, c * 512:(c + 1) * 512], start=True, stop=True)
                        else:
                            last = M.matmul(acc[:, (2 + k % 2) * 512:(2 + k % 2) * 512 + P], lhs_slot[:, k % 2, :], W[:], start=True, stop=True)
                        last.then_inc(pr_mm[q], 1)

            def weighted_quarter(q, p, n):
                _, blk = nc.values_load_multi_w_load_instructions(
                    block_row[0:1, ds(q * QU, n)], engines=[pe.engine], min_val=0, max_val=NB - 1,
                    skip_runtime_bounds_check_because="a step's block counts which of the NB - 1 others lie before it")
                pe.wait_ge(t0_ready, q + 1)
                for k in range(n):
                    last = M.matmul(acc[:, p * 512 + k * D:p * 512 + (k + 1) * D], onehot_t[:, p, k * P:(k + 1) * P],
                                    X[:].rearrange("p b f -> p (b f)")[:, ds(blk[k] * D, D)], start=True, stop=True)
                last.then_inc(r_mm, 1)
                pe.wait_ge(weighted, q + 1)
                pe.wait_ge(eq_ready, q + 1)
                pe.wait_ge(sum_ready, q + 1)
                for k in range(n):
                    last = M.matmul(acc[:, (2 + p) * 512 + k * D:(2 + p) * 512 + (k + 1) * D], onehot[:, p, k, :], rows[:, p, k, :],
                                    start=True, stop=True)
                last.then_inc(s_mm, 1)

            pe.wait_ge(s_x, 32)
            for _ in range(2):
                pe.nop().then_inc(s_mm, 1)
            with pe.Fori(0, 2 * QLOOPS) as j:
                for p in range(2):
                    weighted_quarter(j * 2 + p, p, QU)
            weighted_quarter(4 * QLOOPS, 0, QU)
            weighted_quarter(4 * QLOOPS + 1, 1, QREST - QU)
            project(4, W0)
            pe.wait_ge(pr_out[4], NB + 1)
            project(0, W1T, wide=True)
            pe.wait_ge(pr_out[0], NB + 1)
            begin(1)
            clear(1)
            aggregate(1, False, side=True)
            pe.wait_ge(agg_out[1], 1)
            begin(2)
            project(1, WS1)
            pe.wait_ge(pr_out[1], NB + 1)
            clear(2)
            aggregate(2, True)
            node_product(2, WN1)
            pe.wait_ge(agg_out[2], 1)
            begin(3)
            project(2, WS2)
            pe.wait_ge(pr_out[2], NB + 1)
            clear(3)
            aggregate(3, True)
            node_product(3, WN2)
            pe.wait_ge(agg_out[3], 1)
            project(3, WW)
            pe.wait_ge(pr_out[3], NB + 1)
            M.matmul(aux[:, 0:NB], upto[:], deg[:], start=True, stop=True)
            M.matmul(aux[:, P:P + NB], ones[:], deg[:], start=True, stop=True).then_inc(s_degP, 1)
            def score_half(it, p, n):
                pe.wait_ge(lo_used, it + 1)
                pe.wait_ge(sc_used, it + 1)
                for k in range(n):
                    col = (2 * p + k // QU) * 512 + k % QU * NB * H
                    last = M.matmul(acc[:, col:col + NB * H], onehot_t[:, p, k * P:(k + 1) * P],
                                    s_src[:].rearrange("p b h -> p (b h)"), start=True, stop=True)
                last.then_inc(sc_mm, 1)

            pe.wait_ge(s_scores, 1)
            with pe.Fori(0, LOOPS) as j:
                for p in range(2):
                    score_half(j * 2 + p, p, HALF)
            score_half(2 * LOOPS, 0, REST)
            pe.wait_ge(s_st, 1)
            for h in range(H):
                for g in range(G):
                    last = M.transpose(acc[:, (g * 4 + h) * P:(g * 4 + h + 1) * P], edge_score[:, g * P:(g + 1) * P, h], ident[:])
                last.then_inc(s_tr, 1)
            pe.wait_ge(s_tail, 1)
            M.transpose(aux[0:H, 0:P], lane_tail[:], ident[:])
            M.transpose(aux[0:H, P:2 * P], lane_flag_h[:], ident[:]).then_inc(s_tailT, 1)
            pe.wait_ge(s_carry, 1)
            M.transpose(aux[:, 2 * P:2 * P + H], carry[:, 0:P], ident[0:H, 0:H]).then_inc(s_carryT, 1)
            pe.wait_ge(s_srow, 1)
            begin(4)
            clear(4)
            pe.wait_ge(s_eself, 1)

            def blocks(half):
                _, blk = nc.values_load_multi_w_load_instructions(
                    block_row[0:1, ds(half * HALF, HALF)], engines=[pe.engine], min_val=0, max_val=NB - 1,
                    skip_runtime_bounds_check_because="a step's block counts which of the NB - 1 others lie before it")
                return blk

            def expand(turn, half, p):
                blk = blocks(half)
                pe.wait_ge(t_ready, turn + 1)
                for k in range(HALF):
                    col = (p * HALF + k) * 2 * H
                    last = M.matmul(aux[:, col:col + 2 * H], onehot_t[:, p, k * P:(k + 1) * P],
                                    node_vals[:].rearrange("p b v -> p (b v)")[:, ds(blk[k] * (2 * H), 2 * H)], start=True, stop=True)
                last.then_inc(expanded, 1)

            def attend(turn, half, p):
                blk = blocks(half)
                pe.wait_ge(oh_ready[4], turn + 1)
                pe.wait_ge(m_ready, turn + 1)
                for k in range(HALF):
                    M.matmul(acc[:, ds(blk[k] * D, D)], onehot[:, p, k, :], msg[:, p, k, :], start=False, stop=True, skip_group_check=True)
                    last = M.matmul(acc[:, ds(blk[k] * H + SIDE, H)], onehot[:, p, k, :], prob[:, p, k, :], start=False, stop=True, skip_group_check=True)
                last.then_inc(half_done[4], 1)

            pe.nop().then_inc(expanded, 1)
            expand(0, STASHED, 0)
            with pe.Fori(0, STASHED) as j:
                pe.wait_ge(z_done, j * 6 + 3)
                expand(j * 2 + 1, j, 1)
                attend(j * 2, j + STASHED, 0)
                pe.wait_ge(z_done, j * 6 + 6)
                expand(j * 2 + 2, j + (STASHED + 1), 0)
                attend(j * 2 + 1, j, 1)
            attend(2 * STASHED, HALVES - 1, 0)


_INS = ['x', 'src', 'dst', 'edge_type_8', 'edge_weight', 'L0_gnn_weight', 'L0_gnn_bias', 'L1_gnn_W', 'L1_gnn_b',
        'L1_gnn_gamma', 'L1_gnn_beta', 'L2_gnn_Wself1', 'L2_gnn_Wneigh1', 'L2_gnn_b1', 'L2_gnn_Wself2',
        'L2_gnn_Wneigh2', 'L2_gnn_b2', 'L3_gnn_W_w', 'L3_gnn_W_b', 'L3_gnn_a_w', 'L3_gnn_a_b']


def kernel(**inputs):
    import numpy as _np
    import concourse.bacc as _bacc
    from concourse import mybir as _mybir
    from concourse.bass_utils import run_bass_kernel_spmd as _run

    nc = _bacc.Bacc("TRN2", target_bir_lowering=False, num_devices=1)
    arrays, args = {}, []
    for name in _INS:
        a = _np.ascontiguousarray(inputs[name])
        arrays[f"in_{name}_dram"] = a
        args.append(nc.dram_tensor(f"in_{name}_dram", a.shape, _mybir.dt.from_np(a.dtype), kind="ExternalInput").ap())
    args.append(nc.dram_tensor("out_0_dram", (N, D), _mybir.dt.float32, kind="ExternalOutput").ap())
    gnn_kernel(nc, *args)
    r = _run(nc, [arrays], core_ids=[0])
    return r.results[0]["out_0_dram"]
```

```python
import concourse.bass as bass
from concourse import mybir
from contextlib import ExitStack

N, D, E, R, H = 3125, 128, 100000, 8, 4
P = 128
NB = -(-N // P)
NP = NB * P
TAIL = N - (NB - 1) * P
CH = -(-E // P)
STEPS = CH + NB - 1
G = -(-STEPS // P)
SLOTS = G * P
HALF = 8
LOOPS = STEPS // (2 * HALF)
REST = STEPS - LOOPS * 2 * HALF
HALVES = 2 * LOOPS + 1
QU = 4
QLOOPS = STEPS // (4 * QU)
QREST = STEPS - QLOOPS * 4 * QU
SPARE = P
STASHED = HALVES // 2
GB = 5
GROUPS = NB // GB
BIG = 1e30
EPS = 1e-5
assert 0 < REST <= HALF and QU < QREST < 2 * QU and GROUPS * GB == NB
assert STASHED % 2 == 0 and HALVES * HALF <= SLOTS


def gnn_kernel(nc, x, src, dst, etype, ew, w0, b0, w1, b1, gamma, beta, ws1, wn1, b21, ws2, wn2, b22,
               ww, wb, aw, ab, out):
    f32, i32, bf16 = mybir.dt.float32, mybir.dt.int32, mybir.dt.bfloat16
    ALU, ACT, AX = mybir.AluOpType, mybir.ActivationFunctionType, mybir.AxisListType
    ds = bass.ds

    ctx = ExitStack()
    with ctx:
        def sb(name, shape, dt=f32):
            return ctx.enter_context(nc.sbuf_tensor(name, shape, dt))

        def sem(name):
            return ctx.enter_context(nc.semaphore(name))

        def dram(name, shape, dt=f32):
            return nc.dram_tensor(name, shape, dt, kind="Internal").ap()

        chunk_rec = dram("chunk_rec", (SLOTS, 4 * P + 1))
        block_of_step = dram("block_of_step", (SLOTS,), i32)
        rel_rows = dram("rel_rows", (SLOTS, P))
        reset_flat = dram("reset_flat", (SLOTS * P,))
        src_rows = dram("src_rows", (SLOTS, P))
        lo_rows = dram("lo_rows", (SLOTS, P))
        part_sum = [dram(f"part_sum{k}", (NP + SPARE, D)) for k in range(QU)]
        rel_tab = dram("rel_tab", (NP, R * D))
        node_tab = dram("node_tab", (NP, D))
        hid_tab = dram("hid_tab", (NP, D))
        key_tab = dram("key_tab", (NP, D))
        score_flat = dram("score_flat", (H, SLOTS * P))
        stash = dram("stash", (STASHED * P, HALF * D))
        prefix_tab = dram("prefix_tab", (STEPS * P, H))

        iota_row = sb("iota_row", [P, P])
        iota_part = sb("iota_part", [P, 1])
        step_no = sb("step_no", [P, G])
        block_base = sb("block_base", [P, NB])
        ident = sb("ident", [P, P])
        upto = sb("upto", [P, P])
        ones = sb("ones", [P, P])
        before = sb("before", [P, P])
        spare_row = sb("spare_row", [P, 1])
        zeros = sb("zeros", [P, 4 * P])
        prefix = sb("prefix", [P, STEPS, H])
        raw = prefix[:].rearrange("p x h -> p (x h)")[:, 0:3 * SLOTS].bitcast(i32).rearrange("p (f e) -> p f e", f=3)
        chunk_sb = sb("chunk_sb", [P, G, 4, P])
        step_rec = sb("step_rec", [P, G, 4 * P + 1])
        below = sb("below", [P, NB - 1])
        last_step = sb("last_step", [P, NB - 1])
        step_block = sb("step_block", [P, G])
        step_block_i = sb("step_block_i", [P, G], i32)
        step_base = sb("step_base", [P, G])
        step_chunk = sb("step_chunk", [P, G], i32)
        rel_row = sb("rel_row", [P, G, P])
        valid = sb("valid", [P, G, P])
        invalid_pen = rel_row
        reset_row = sb("reset_row", [P, G, P])
        tmp_row = sb("tmp_row", [P, G, P])
        block_row = sb("block_row", [1, SLOTS], i32)
        idx_src = sb("idx_src", [P, SLOTS], i32)
        idx_rel = sb("idx_rel", [P, SLOTS], i32)
        rel_col = sb("rel_col", [P, SLOTS])
        w_col = sb("w_col", [P, SLOTS])
        src_block = w_col
        idx_slot = sb("idx_slot", [P, 2, HALF], i32)
        rows = sb("rows", [P, 2, HALF, D])
        onehot = sb("onehot", [P, 2, HALF, P])
        rel_bc = sb("rel_bc", [P, 2, HALF * P])
        dup = sb("dup", [P, QU])
        to_spare = sb("to_spare", [P, QU])
        onehot_t = sb("onehot_t", [P, 2, HALF * P])
        msg = sb("msg", [P, 2, HALF, D])
        idx_quarter = idx_slot[:].rearrange("p a (b k) -> p (a b) k", k=QU)
        msg_quarter = msg[:].rearrange("p a (b k) f -> p (a b) k f", k=QU)
        prob = sb("prob", [P, 2, HALF, H])
        z_slot = sb("z_slot", [P, HALF, H])
        u_slot = sb("u_slot", [P, 2, HALF, H])
        step_no_block = sb("step_no_block", [P, NB])
        X = sb("X", [P, NB, D])
        Y = sb("Y", [P, NB, D])
        T = sb("T", [P, NB, D])
        nat_slot = sb("nat_slot", [P, GB, D])
        lhs_slot = sb("lhs_slot", [P, GB, D])
        hout = sb("hout", [P, 2, R * D])
        mean = sb("mean", [P, NB])
        var = sb("var", [P, NB])
        rstd = sb("rstd", [P, NB])
        stats = sb("stats", [P, NB, 6])
        deg = sb("deg", [P, NB])
        rdeg = sb("rdeg", [P, NB])
        has = sb("has", [P, NB])
        src_bc = hout[:, 0, :].rearrange("p (s e) -> p s e", s=2)
        W0, WS1, WN1, WS2, WN2, WW = (sb(n, [P, D]) for n in ("W0", "WS1", "WN1", "WS2", "WN2", "WW"))
        W1 = hout[:, 0, :].rearrange("p (r f) -> p r f", r=R)
        W1T = sb("W1T", [P, R * D])
        B0, GA, BE, B21, B22, WB = (sb(n, [P, D]) for n in ("B0", "GA", "BE", "B21", "B22", "WB"))
        B1 = sb("B1", [P, R * D])
        A_DST, A_SRC = sb("A_DST", [P, H, D // H]), sb("A_SRC", [P, H, D // H])
        AB = sb("AB", [P, H])
        edge_score = sb("edge_score", [P, SLOTS, H])
        score_row = chunk_sb[:].rearrange("p g f e -> p (g f e)").rearrange("p (h g e) -> p h g e", h=H, g=G)
        lanes = step_rec[:].rearrange("p g f -> p (g f)")[:, 0:H * STEPS].rearrange("p (h x) -> p h x", h=H)
        lane_reset = tmp_row[:].rearrange("p g e -> p (g e)")[:, 0:STEPS]
        lane_tail = sb("lane_tail", [P, H])
        lane_flag = sb("lane_flag", [P, 1])
        lane_flag_h = sb("lane_flag_h", [P, H])
        carry_rst = sb("carry_rst", [H, P])
        carry = sb("carry", [H, P + 1])
        carry_col = sb("carry_col", [P, H])
        ends = sb("ends", [P, NB])
        ends_i = sb("ends_i", [P, NB], i32)
        block_sum = sb("block_sum", [P, NB])
        block_cum = sb("block_cum", [P, NB + 1])
        in_max = sb("in_max", [P, NB, H])
        s_src, s_dst = sb("s_src", [P, NB, H]), sb("s_dst", [P, NB, H])
        e_self, e_tmp = sb("e_self", [P, NB, H]), sb("e_tmp", [P, NB, H])
        e_max = sb("e_max", [P, NB, H])
        p_self, den = sb("p_self", [P, NB, H]), sb("den", [P, NB, H])
        node_vals = sb("node_vals", [P, NB, 2 * H])
        node_rest = sb("node_rest", [P, NB, 2 * H])
        node_parts = sb("node_parts", [P, NB, 3, 2 * H], bf16)
        dest_vals = sb("dest_vals", [P, HALF, 2 * H])
        prob_rest = sb("prob_rest", [P, HALF, H])
        prob_parts = sb("prob_parts", [P, 2, HALF, 3, H], bf16)
        hot_t = onehot_t[:, 0, :].bitcast(bf16).rearrange("p (s e) -> p s e", s=2)
        hot = chunk_sb[:].rearrange("p g f e -> p (g f e)")[:, 0:HALF * P].bitcast(bf16).rearrange("p (s k e) -> p s k e", s=2, k=HALF)

        h_slot = [hout[:, 0, :], hout[:, 1, :]] + [T[:].rearrange("p b f -> p (b f)")[:, k * R * D:(k + 1) * R * D] for k in range(GB - 2)]
        stash_rows = T[:, 0:2 * HALF, :].rearrange("p (s k) f -> p s k f", s=2)
        part_slot = [T[:]] + [(edge_score, step_rec)[k % 2][:].rearrange("p a b -> p (a b)")[:, 0:NB * D].rearrange("p (b f) -> p b f", f=D)
                              for k in range(1, QU)]

        acc = ctx.enter_context(nc.psum_tensor("acc", [P, 7 * 512], f32))
        aux = ctx.enter_context(nc.psum_tensor("aux", [P, 512], f32))
        SIDE = NB * D

        def sems(names):
            return (sem(n) for n in names.split())

        def pair(name):
            return [sem(f"{name}{p}") for p in range(2)]

        def layers(name, *numbers):
            return {a: sem(f"{name}{a}") for a in numbers}

        chain = sem("chain")
        constants_ready, padding_set, edges_loaded, weights_loaded, vectors_loaded, nodes_loaded = sems(
            "constants_ready padding_set edges_loaded weights_loaded vectors_loaded nodes_loaded")
        records_in_sbuf, records_stored, counts_ready, counts_summed, step_chunk_ready, step_records_loaded = sems(
            "records_in_sbuf records_stored counts_ready counts_summed step_chunk_ready step_records_loaded")
        step_block_ready, step_block_stored, block_row_loaded, step_rows_ready, step_rows_stored = sems(
            "step_block_ready step_block_stored block_row_loaded step_rows_ready step_rows_stored")
        columns_turned, columns_ready, w1_turned, places_ready = sems("columns_turned columns_ready w1_turned places_ready")
        rel_src_loaded = pair("rel_src_loaded")
        spread_hot_ready, same_source_ready, repeat_step, scatter_idx_ready, rows_spread, weighted, rows_summed, sum_ready = sems(
            "spread_hot_ready same_source_ready repeat_step scatter_idx_ready rows_spread weighted rows_summed sum_ready")
        part_sum_zeroed, row_free, parts_added = sems("part_sum_zeroed row_free parts_added")
        scattered = [sem(f"scattered{k}") for k in range(QU)]
        part_loaded = [sem(f"part_loaded{k}") for k in range(QU)]
        pool_tick = sem("pool_tick")
        idx_ready, onehot_ready, half_done = (layers(n, 1, 2, 3, 4) for n in ("idx_ready", "onehot_ready", "half_done"))
        gathered = {a: pair(f"gathered{a}_") for a in range(1, 5)}
        group_copied, block_turned, lhs_copied, product_ready, product_read = (
            [sem(f"{n}{q}") for q in range(5)] for n in ("group_copied", "block_turned", "lhs_copied", "product_ready", "product_read"))
        products_stored = [sem(f"products_stored{k}") for k in range(GB)]
        lhs_ready, node_product_ready, sums_read = layers("lhs_ready", 2, 3), layers("node_product_ready", 2, 3), layers("sums_read", 1, 2, 3)
        x_copied, table_stored, x_ready = sem("x_copied"), layers("table_stored", 2, 3, 4), layers("x_ready", 2)
        ln_var, ln_std, ln_groups, centred = sems("ln_var ln_std ln_groups centred")
        places_loaded = pair("places_loaded")
        scores_ready, place_hot_ready, place_scores_ready, place_scores_read, choice_step, edge_scores_ready = sems(
            "scores_ready place_hot_ready place_scores_ready place_scores_read choice_step edge_scores_ready")
        score_rows_ready, score_rows_stored, lanes_loaded, tails_ready, tails_turned, carry_ready, carry_turned = sems(
            "score_rows_ready score_rows_stored lanes_loaded tails_ready tails_turned carry_ready carry_turned")
        prefix_ready, prefix_stored, degrees_summed, ends_ready, in_max_loaded, self_exponent_ready, self_prob_ready = sems(
            "prefix_ready prefix_stored degrees_summed ends_ready in_max_loaded self_exponent_ready self_prob_ready")
        stored, stash_in, rel_loaded = pair("stored"), pair("stash_in"), pair("rel_loaded")
        turned_hot_ready, expanded, dest_vals_read, z_step, exponent_ready, prob_ready, msg_ready = sems(
            "turned_hot_ready expanded dest_vals_read z_step exponent_ready prob_ready msg_ready")
        hot_ready, first_part_ready, rest_step, parts_ready = sems("hot_ready first_part_ready rest_step parts_ready")
        result_ready, result_stored = sems("result_ready result_stored")

        def rows_of(tab):
            return tab.rearrange("(b p) f -> p b f", p=P)

        block = ctx.enter_context(nc.Block())

        @block.sync
        def _(sp):
            full = (G - 1) * P * P
            whole = (E - full) // P
            sp.wait_ge(padding_set, 1)
            for f, ap in enumerate((src, etype, dst)):
                sp.dma_start(raw[:, f, 0:(G - 1) * P].rearrange("p (g e) -> p g e", e=P),
                             ap[0:full].rearrange("(g p e) -> p g e", p=P, e=P)).then_inc(edges_loaded, 16)
                sp.dma_start(raw[0:whole, f, (G - 1) * P:SLOTS],
                             ap[full:full + whole * P].rearrange("(p e) -> p e", e=P)).then_inc(edges_loaded, 16)
                sp.dma_start(raw[whole:whole + 1, f, (G - 1) * P:(G - 1) * P + E - full - whole * P],
                             ap[full + whole * P:E].rearrange("(a e) -> a e", a=1)).then_inc(edges_loaded, 16)
            sp.dma_start(chunk_sb[:, 0:G - 1, 3, :], ew[0:full].rearrange("(g p e) -> p g e", p=P, e=P)).then_inc(edges_loaded, 16)
            sp.dma_start(chunk_sb[0:whole, G - 1, 3, :],
                         ew[full:full + whole * P].rearrange("(p e) -> p e", e=P)).then_inc(edges_loaded, 16)
            sp.dma_start(chunk_sb[whole:whole + 1, G - 1, 3, 0:E - full - whole * P],
                         ew[full + whole * P:E].rearrange("(a e) -> a e", a=1)).then_inc(edges_loaded, 16)
            sp.dma_start(X[:, 0:NB - 1, :], x[0:(NB - 1) * P, :].rearrange("(b p) f -> p b f", p=P)).then_inc(nodes_loaded, 16)
            sp.dma_start(X[0:TAIL, NB - 1, :], x[(NB - 1) * P:N, :]).then_inc(nodes_loaded, 16)
            for tile, ap in ((W0, w0), (WS1, ws1), (WN1, wn1), (WS2, ws2), (WN2, wn2), (WW, ww)):
                sp.dma_start(tile[:], ap).then_inc(weights_loaded, 16)
            sp.dma_start(W1, w1.rearrange("r h d -> h r d")).then_inc(weights_loaded, 16)
            sp.wait_ge(records_in_sbuf, 1)
            sp.dma_start(chunk_rec[0:SLOTS, 0:4 * P].rearrange("(g p) f -> p g f", p=P),
                         chunk_sb[:].rearrange("p g f e -> p g (f e)")).then_inc(records_stored, 16)
            for g in range(G):
                n = P - (g == G - 1)
                sp.dma_start(chunk_rec[g * P + 1:g * P + n + 1, 4 * P:4 * P + 1],
                             chunk_sb[0:n, g, 2, P - 1:P], allow_slow_non_contiguous=True).then_inc(records_stored, 16)
            sp.dma_start(chunk_rec[0:1, 4 * P:4 * P + 1], ones[0:1, 0:1]).then_inc(records_stored, 16)
            sp.wait_ge(step_block_ready, 1)
            sp.dma_start(block_of_step.rearrange("(g p) -> p g", p=P), step_block_i[:], allow_slow_non_contiguous=True).then_inc(step_block_stored, 16)
            sp.wait_ge(step_block_stored, 16)
            sp.dma_start(block_row[:], block_of_step.rearrange("(a t) -> a t", a=1)).then_inc(block_row_loaded, 16)
            sp.wait_ge(step_rows_ready, 1)
            sp.dma_start(rel_rows.rearrange("(g p) e -> p g e", p=P), rel_row[:]).then_inc(step_rows_stored, 16)
            sp.dma_start(reset_flat.rearrange("(g p e) -> p g e", p=P, e=P), reset_row[:]).then_inc(step_rows_stored, 16)
            sp.dma_start(src_rows.rearrange("(g p) e -> p g e", p=P), step_rec[:, :, 0:P]).then_inc(step_rows_stored, 16)
            sp.wait_ge(places_ready, 1)
            sp.dma_start(lo_rows.rearrange("(g p) e -> p g e", p=P), tmp_row[:]).then_inc(step_rows_stored, 16)
            sp.wait_ge(step_rows_stored, 64)

            def rel_src_quarter(q, p, n):
                for tile, tab in ((rel_bc, rel_rows), (src_bc, src_rows)):
                    sp.dma_start(tile[:, p, 0:n * P],
                                 tab[ds(q * QU, n), :].rearrange("(a t) e -> a (t e)", a=1).to_broadcast([P, n * P])
                                 ).then_inc(rel_src_loaded[p], 16)

            sp.wait_ge(w1_turned, 1)
            rel_src_quarter(0, 0, QU)
            rel_src_quarter(1, 1, QU)
            with sp.Fori(0, 2 * QLOOPS - 1) as j:
                for p in range(2):
                    sp.wait_ge(scatter_idx_ready, j * 2 + p + 1)
                    rel_src_quarter(j * 2 + p + 2, p, QU)
            sp.wait_ge(scatter_idx_ready, 4 * QLOOPS - 1)
            rel_src_quarter(4 * QLOOPS, 0, QU)
            sp.wait_ge(scatter_idx_ready, 4 * QLOOPS)
            rel_src_quarter(4 * QLOOPS + 1, 1, QREST - QU)
            for k in range(QU):
                sp.wait_ge(scattered[k], 16 * (4 * QLOOPS + 1 + (k < QREST - QU)))
            for k, buf in enumerate(part_sum):
                if k >= 3:
                    sp.wait_ge(parts_added, k - 1)
                sp.dma_start(part_slot[k], buf[0:NP, :].rearrange("(b p) f -> p b f", p=P)).then_inc(part_loaded[k], 16)
            for k in range(GB):
                sp.nop().then_inc(products_stored[k], 16)
            with sp.Fori(0, GROUPS) as i:
                for k in range(GB):
                    sp.wait_ge(product_read[0], i * GB + k + 2)
                    sp.dma_start(rel_tab[ds((i * GB + k) * P, P), :], h_slot[k]).then_inc(products_stored[k], 16)
            for i in range(GROUPS):
                sp.wait_ge(ln_groups, 4 * GROUPS + i + 1)
                sp.dma_start(rows_of(node_tab)[:, i * GB:(i + 1) * GB, :], X[:, i * GB:(i + 1) * GB, :]).then_inc(table_stored[2], 16)
            sp.wait_ge(x_ready[2], 1)
            sp.dma_start(rows_of(hid_tab), T[:]).then_inc(table_stored[3], 16)
            for i in range(GROUPS):
                sp.wait_ge(product_read[3], 1 + (i + 1) * GB)
                sp.dma_start(rows_of(key_tab)[:, i * GB:(i + 1) * GB, :], Y[:, i * GB:(i + 1) * GB, :]).then_inc(table_stored[4], 16)
            def place_rows(it, p, n):
                sp.dma_start(rel_bc[:, p, 0:n * P],
                             lo_rows[ds(it * HALF, n), :].rearrange("(a t) e -> a (t e)", a=1).to_broadcast([P, n * P])
                             ).then_inc(places_loaded[p], 16)

            place_rows(0, 0, HALF)
            place_rows(1, 1, HALF)
            with sp.Fori(0, LOOPS - 1) as j:
                for p in range(2):
                    sp.wait_ge(place_hot_ready, j * 2 + p + 1)
                    place_rows(j * 2 + p + 2, p, HALF)
            sp.wait_ge(place_hot_ready, 2 * LOOPS - 1)
            place_rows(2 * LOOPS, 0, REST)
            sp.wait_ge(score_rows_ready, 1)
            for h in range(H):
                sp.dma_start(score_flat[h, :].rearrange("(g p e) -> p g e", p=P, e=P), score_row[:, h]).then_inc(score_rows_stored, 16)
            sp.wait_ge(score_rows_stored, 16 * H)
            for h in range(H):
                sp.dma_start(lanes[:, h, :], score_flat[h, 0:STEPS * P].rearrange("(l x) -> l x", x=STEPS)).then_inc(lanes_loaded, 16)
            sp.dma_start(lane_reset, reset_flat[0:STEPS * P].rearrange("(l x) -> l x", x=STEPS)).then_inc(lanes_loaded, 16)
            sp.wait_ge(prefix_ready, 1)
            sp.dma_start(prefix_tab.rearrange("(l x) h -> l (x h)", x=STEPS),
                         prefix[:].rearrange("p x h -> p (x h)")).then_inc(prefix_stored, 16)
            def rel_half(half, p):
                sp.dma_start(rel_bc[:, p, :],
                             rel_rows[ds(half * HALF, HALF), :].rearrange("(a t) e -> a (t e)", a=1).to_broadcast([P, HALF * P])
                             ).then_inc(rel_loaded[p], 16)

            def stash_half(half, s):
                sp.dma_start(stash_rows[:, s].rearrange("p k f -> p (k f)"), stash[ds(half * P, P), :]).then_inc(stash_in[s], 16)

            for p in range(2):
                sp.wait_ge(stored[p], 16 * (STASHED // 2))
            rel_half(STASHED, 0)
            rel_half(0, 1)
            for s in range(2):
                stash_half(s, s)
            with sp.Fori(0, STASHED // 2 - 1) as j:
                for s in range(2):
                    sp.wait_ge(turned_hot_ready, j * 4 + 2 * s + 1)
                    rel_half(j * 2 + (STASHED + s + 1), 0)
                    sp.wait_ge(turned_hot_ready, j * 4 + 2 * s + 2)
                    rel_half(j * 2 + (s + 1), 1)
                    sp.wait_ge(msg_ready, j * 4 + 2 * s + 2)
                    stash_half(j * 2 + (s + 2), s)
            turn = 2 * STASHED
            sp.wait_ge(turned_hot_ready, turn - 3)
            rel_half(HALVES - 2, 0)
            sp.wait_ge(turned_hot_ready, turn - 2)
            rel_half(STASHED - 1, 1)
            sp.wait_ge(turned_hot_ready, turn - 1)
            rel_half(HALVES - 1, 0)
            sp.wait_ge(result_ready, 1)
            sp.dma_start(out[0:(NB - 1) * P, :].rearrange("(b p) f -> p b f", p=P), X[:, 0:NB - 1, :]).then_inc(result_stored, 16)
            sp.dma_start(out[(NB - 1) * P:N, :], X[0:TAIL, NB - 1, :]).then_inc(result_stored, 16)
            sp.wait_ge(result_stored, 32)

        @block.gpsimd
        def _(pool):
            nc.gpsimd.iota(iota_row[:], [[1, P]], base=0, channel_multiplier=0, allow_small_or_imprecise_dtypes=True)
            nc.gpsimd.iota(iota_part[:], [[0, 1]], base=0, channel_multiplier=1, allow_small_or_imprecise_dtypes=True)
            nc.gpsimd.iota(block_base[:], [[P, NB]], base=0, channel_multiplier=0, allow_small_or_imprecise_dtypes=True)
            nc.gpsimd.iota(step_no[:], [[P, G]], base=0, channel_multiplier=1,
                           allow_small_or_imprecise_dtypes=True).then_inc(constants_ready, 1)
            pool.wait_ge(records_stored, 16 * (G + 2))
            pool.wait_ge(step_chunk_ready, 1)
            for g in range(G):
                nc.gpsimd.indirect_dma_start(step_rec[:, g, :], None, chunk_rec,
                                             bass.IndirectOffsetOnAxis(ap=step_chunk[:, g:g + 1], axis=0)).then_inc(step_records_loaded, 16)

            def gather_half(a, table, it, p, n):
                pool.wait_ge(idx_ready[a], it + 1)
                pool.sem_inc(pool_tick)
                for k in range(n):
                    nc.gpsimd.indirect_dma_start(rows[:, p, k, :], None, table,
                                                 bass.IndirectOffsetOnAxis(ap=idx_slot[:, p, k:k + 1], axis=0)
                                                 ).then_inc(gathered[a][p], 16)

            def gather(a, table):
                with pool.Fori(0, LOOPS) as j:
                    for p in range(2):
                        gather_half(a, table, j * 2 + p, p, HALF)
                gather_half(a, table, 2 * LOOPS, 0, REST)

            pool.wait_ge(part_sum_zeroed, 16 * 2 * QU)
            for _ in range(3):
                pool.sem_inc(row_free)

            def scatter_quarter(q, s, n, first=False):
                pool.wait_ge(scatter_idx_ready, q + 1)
                pool.sem_inc(pool_tick)
                pool.wait_ge(sum_ready, q + 3)
                pool.sem_inc(pool_tick)
                for k in range(n):
                    if not first:
                        pool.wait_ge(scattered[k], q * 16)
                        pool.sem_inc(pool_tick)
                    if k == QU - 1:
                        pool.sem_inc(row_free)
                    nc.gpsimd.indirect_dma_start(part_sum[k], bass.IndirectOffsetOnAxis(ap=idx_quarter[:, s, k:k + 1], axis=0),
                                                 msg_quarter[:, s, k, :], None, compute_op=ALU.add).then_inc(scattered[k], 16)

            scatter_quarter(0, 0, QU, first=True)
            with pool.Fori(0, QLOOPS) as j:
                for s in range(4):
                    scatter_quarter(j * 4 + s + 1, (s + 1) % 4, QU)
            scatter_quarter(4 * QLOOPS + 1, 1, QREST - QU)
            for k in range(GB):
                pool.wait_ge(products_stored[k], 16 * (1 + GROUPS))
            gather(1, rel_tab.rearrange("n (r f) -> (n r) f", r=R))
            for a, tab in ((2, node_tab), (3, hid_tab)):
                pool.wait_ge(table_stored[a], 16 * (GROUPS if a == 2 else 1))
                gather(a, tab)
            def keys_half(half, p):
                nc.gpsimd.tensor_copy(idx_slot[:, p, :], idx_src[:, ds(half * HALF, HALF)]).then_inc(idx_ready[4], 1)
                pool.wait_ge(idx_ready[4], half + 1)
                pool.sem_inc(pool_tick)
                for k in range(HALF):
                    nc.gpsimd.indirect_dma_start(rows[:, p, k, :], None, key_tab,
                                                 bass.IndirectOffsetOnAxis(ap=idx_slot[:, p, k:k + 1], axis=0)
                                                 ).then_inc(gathered[4][p], 16)

            pool.wait_ge(table_stored[4], 16 * GROUPS)
            for p in range(2):
                keys_half(p, p)
            with pool.Fori(1, STASHED // 2) as j:
                for p in range(2):
                    pool.wait_ge(stored[p], j * 16)
                    keys_half(j * 2 + p, p)
            pool.wait_ge(prefix_stored, 16)
            pool.wait_ge(ends_ready, 1)
            for b in range(NB):
                nc.gpsimd.indirect_dma_start(in_max[:, b, :], None, prefix_tab,
                                             bass.IndirectOffsetOnAxis(ap=ends_i[:, b:b + 1], axis=0)).then_inc(in_max_loaded, 16)
            for p in range(2):
                pool.wait_ge(stored[p], 16 * (STASHED // 2))
                keys_half(STASHED + p, p)
            with pool.Fori(1, STASHED // 2) as j:
                for p in range(2):
                    pool.wait_ge(msg_ready, j * 4 + (2 * p - 3))
                    keys_half(j * 2 + (STASHED + p), p)
            pool.wait_ge(msg_ready, 2 * STASHED - 3)
            keys_half(HALVES - 1, 0)

        @block.scalar
        def _(act):
            act.wait_ge(padding_set, 1)
            for buf in part_sum:
                act.dma_start(buf[0:NP, :].rearrange("(b p) f -> p b f", p=P), Y[:]).then_inc(part_sum_zeroed, 16)
                act.dma_start(buf[NP:NP + SPARE, :], Y[:, 0, :]).then_inc(part_sum_zeroed, 16)
            for tile, ap in ((B0, b0), (GA, gamma), (BE, beta), (B21, b21), (B22, b22), (WB, wb)):
                act.dma_start(tile[:], ap.rearrange("(a f) -> a f", a=1).to_broadcast([P, D])).then_inc(vectors_loaded, 16)
            act.dma_start(B1[:], b1.rearrange("r f -> (r f)").rearrange("(a f) -> a f", a=1).to_broadcast([P, R * D])).then_inc(vectors_loaded, 16)
            act.dma_start(A_DST[:], aw[:, 0:D // H].rearrange("(a h) f -> a h f", a=1).to_broadcast([P, H, D // H])).then_inc(vectors_loaded, 16)
            act.dma_start(A_SRC[:], aw[:, D // H:2 * D // H].rearrange("(a h) f -> a h f", a=1).to_broadcast([P, H, D // H])).then_inc(vectors_loaded, 16)
            act.dma_start(AB[:], ab.rearrange("(a h) -> a h", a=1).to_broadcast([P, H])).then_inc(vectors_loaded, 16)

            def sums_to_lhs(a):
                act.wait_ge(half_done[a], 2 + HALVES)
                for i in range(GROUPS):
                    if i >= 2:
                        act.wait_ge(node_product_ready[a], i - 1)
                    nc.scalar.copy((lhs_slot, nat_slot)[i % 2][:].rearrange("p b f -> p (b f)"),
                                   acc[:, i * GB * D:(i + 1) * GB * D]).then_inc(lhs_ready[a], 1)

            def root(count):
                act.wait_ge(ln_var, count)
                nc.scalar.activation(rstd[:], var[:], ACT.Sqrt).then_inc(ln_std, 1)

            def project(q, source, ready, count, by_group=False):
                if not by_group:
                    act.wait_ge(ready, count)
                act.nop().then_inc(lhs_copied[q], 1)
                with act.Fori(0, GROUPS) as i:
                    act.wait_ge(block_turned[q], i * GB + 1)
                    if by_group:
                        act.wait_ge(ready, i + (count + 1))
                    nc.scalar.copy(nat_slot[:], source[:, ds(i * GB, GB), :]).then_inc(group_copied[q], 1)
                    for k in range(GB):
                        act.wait_ge(block_turned[q], i * GB + k + 2)
                        act.wait_ge(product_ready[q], i * GB + max(k, 1))
                        nc.scalar.copy(lhs_slot[:, k % 2, :], acc[:, (k % 2) * 512:(k % 2) * 512 + P]).then_inc(lhs_copied[q], 1)

            def weigh_quarter(q, s, n):
                p = s % 2
                act.wait_ge(rows_spread, q + 1)
                for k in range(n):
                    last = nc.scalar.activation(rows[:, p, k, :], acc[:, p * 512 + k * D:p * 512 + (k + 1) * D], ACT.Copy,
                                                scale=w_col[:, ds(q * QU + k, 1)])
                last.then_inc(weighted, 1)
                act.wait_ge(rows_summed, q + 3)
                act.wait_ge(row_free, q + 1)
                nc.scalar.copy(msg_quarter[:, s, 0:n, :].rearrange("p k f -> p (k f)"), acc[:, (2 + p) * 512:(2 + p) * 512 + n * D]).then_inc(sum_ready, 1)

            for _ in range(2):
                act.nop().then_inc(sum_ready, 1)
            act.wait_ge(columns_ready, 1)
            nc.scalar.activation(rstd[:, 0:1], w_col[:, 0:1], ACT.Copy)
            with act.Fori(0, QLOOPS) as j:
                for s in range(4):
                    weigh_quarter(j * 4 + s, s, QU)
            weigh_quarter(4 * QLOOPS, 0, QU)
            weigh_quarter(4 * QLOOPS + 1, 1, QREST - QU)
            project(4, T, parts_added, QU)
            root(1)
            project(0, X, ln_groups, GROUPS, by_group=True)
            root(2)
            root(3)
            project(1, X, ln_groups, 4 * GROUPS, by_group=True)
            sums_to_lhs(2)
            project(2, T, x_ready[2], 1)
            sums_to_lhs(3)
            root(4)
            project(3, X, ln_groups, 6 * GROUPS, by_group=True)
            with act.Fori(0, STASHED // 2) as j:
                for p in range(2):
                    act.wait_ge(gathered[4][p], j * (16 * HALF) + 16 * HALF)
                    act.dma_start(stash[ds((j * 2 + p) * P, P), :], rows[:, p].rearrange("p k f -> p (k f)")).then_inc(stored[p], 16)
            act.wait_ge(self_exponent_ready, 1)
            nc.scalar.activation(p_self[:], e_tmp[:], ACT.Exp).then_inc(self_prob_ready, 1)

            def exp_half(turn, p):
                act.wait_ge(onehot_ready[4], turn + 1)
                nc.scalar.copy(hot[:, p], onehot[:, p]).then_inc(hot_ready, 1)
                act.wait_ge(exponent_ready, turn + 1)
                nc.scalar.activation(prob[:, p], u_slot[:, p], ACT.Exp).then_inc(prob_ready, 1)
                act.wait_ge(prob_ready, turn + 1)
                nc.scalar.copy(prob_parts[:, p, :, 0], prob[:, p]).then_inc(first_part_ready, 1)

            with act.Fori(0, STASHED) as j:
                for p in range(2):
                    exp_half(j * 2 + p, p)
            exp_half(2 * STASHED, 0)
            root(5)

        @block.vector
        def _(dve):
            V = nc.vector
            count = [0]

            def then(ins):
                count[0] += 1
                ins.then_inc(chain, 1)
                dve.wait_ge(chain, count[0])

            V.memset(raw[:, 0:2, (G - 1) * P:SLOTS], 0)
            V.memset(raw[:, 2, (G - 1) * P:SLOTS], E)
            V.memset(X[:, NB - 1, :], 0.0)
            V.memset(ones[:], 1.0)
            V.memset(zeros[:], 0.0)
            V.memset(Y[:], 0.0)
            then(V.memset(chunk_sb[:, G - 1, 3, :], 0.0))
            V.memset(carry[:, 0:1], -BIG).then_inc(padding_set, 1)
            dve.wait_ge(constants_ready, 1)
            V.tensor_scalar(ident[:], iota_row[:], iota_part[:, 0:1], None, ALU.is_equal).then_inc(constants_ready, 1)
            V.tensor_scalar(before[:], iota_row[:], iota_part[:, 0:1], None, ALU.is_lt)
            V.tensor_scalar(step_no_block[:], block_base[:], 1.0 / P, None, ALU.mult)
            V.tensor_scalar(spare_row[:], iota_part[:], float(NP), None, ALU.add)
            V.tensor_scalar(upto[:], iota_row[:], iota_part[:, 0:1], None, ALU.is_ge)
            dve.wait_ge(edges_loaded, 16 * 12)
            then(V.tensor_copy(chunk_sb[:, :, 0:3, :], raw.rearrange("p f (g e) -> p g f e", e=P)))
            V.engine_nop().then_inc(records_in_sbuf, 1)
            ended = tmp_row[:].rearrange("p g e -> p (g e)")[:, 0:(NB - 1) * G].rearrange("p (b g) -> p b g", g=G)
            then(V.tensor_tensor(ended, chunk_sb[:, :, 2, P - 1][:, None, :].to_broadcast([P, NB - 1, G]),
                                 block_base[:, 1:NB, None].to_broadcast([P, NB - 1, G]), ALU.is_lt))
            V.tensor_reduce(below[:], ended, AX.X, ALU.add).then_inc(counts_ready, 1)
            dve.wait_ge(counts_summed, 1)
            then(V.scalar_tensor_tensor(last_step[:], block_base[:, 0:NB - 1], 1.0 / P, aux[:, 0:NB - 1], ALU.mult, ALU.add))
            for g in range(G):
                then(V.tensor_scalar(tmp_row[:, 0, 0:NB - 1], last_step[:], step_no[:, g:g + 1], 0.0, ALU.is_lt, ALU.add,
                                     accum_out=step_block[:, g:g + 1]))
            then(V.tensor_tensor(step_base[:], step_no[:], step_block[:], ALU.subtract))
            V.tensor_copy(step_chunk[:], step_base[:]).then_inc(step_chunk_ready, 1)
            V.tensor_copy(step_block_i[:], step_block[:]).then_inc(step_block_ready, 1)
            dve.wait_ge(step_chunk_ready, 1)
            then(V.tensor_scalar(step_base[:], step_block[:], float(P), None, ALU.mult))
            dve.wait_ge(w1_turned, 1)
            V.tensor_copy(W1T[:], acc[:, 0:R * D]).then_inc(w1_turned, 1)
            dve.wait_ge(step_records_loaded, 16 * G)
            fields = step_rec[:, :, 0:4 * P].rearrange("p g (f e) -> p g f e", f=4)
            f_src, f_typ, f_dst = (fields[:, :, f, :] for f in range(3))
            then(V.tensor_tensor(rel_row[:], f_dst, step_base[:, :, None].to_broadcast([P, G, P]), ALU.subtract))
            then(V.tensor_scalar(valid[:], rel_row[:], 0.0, None, ALU.is_ge))
            then(V.scalar_tensor_tensor(valid[:], rel_row[:], float(P), valid[:], ALU.is_lt, ALU.mult))
            then(V.scalar_tensor_tensor(rel_row[:], rel_row[:], 1.0, valid[:], ALU.add, ALU.mult))
            then(V.tensor_scalar(rel_row[:], rel_row[:], 1.0, None, ALU.subtract))
            V.tensor_tensor(tmp_row[:, :, 1:P], f_dst[:, :, 1:P], f_dst[:, :, 0:P - 1], ALU.not_equal)
            then(V.tensor_tensor(tmp_row[:, :, 0:1], f_dst[:, :, 0:1], step_rec[:, :, 4 * P:4 * P + 1], ALU.not_equal))
            then(V.scalar_tensor_tensor(reset_row[:], tmp_row[:], -BIG, valid[:], ALU.mult, ALU.mult))
            then(V.scalar_tensor_tensor(f_typ, f_src, float(R), f_typ, ALU.mult, ALU.add))
            V.engine_nop().then_inc(step_rows_ready, 1)
            lo_i = raw[:, 0, :].rearrange("p (g e) -> p g e", e=P)
            then(V.tensor_copy(lo_i, f_src))
            then(V.tensor_scalar(lo_i, lo_i, P - 1, None, ALU.bitwise_and))
            V.tensor_copy(tmp_row[:], lo_i).then_inc(places_ready, 1)
            dve.wait_ge(columns_turned, 1)
            cols = acc[:].rearrange("p (g f t) -> p g f t", g=G, f=4)
            for f, tile in enumerate((idx_src, idx_rel, rel_col, w_col)):
                then(V.tensor_copy(tile[:].rearrange("p (g t) -> p g t", t=P), cols[:, :, f, :]))
            V.engine_nop().then_inc(columns_ready, 1)

            def prepare_half(a, idx, it, p, n):
                dve.wait_ge(half_done[a], it + 1)
                V.tensor_copy(idx_slot[:, p, 0:n], idx[:, ds(it * HALF, n)]).then_inc(idx_ready[a], 1)
                V.tensor_tensor(onehot[:, p, 0:n, :], iota_row[:, None, :].to_broadcast([P, n, P]),
                                rel_col[:, ds(it * HALF, n), None].to_broadcast([P, n, P]), ALU.is_equal).then_inc(onehot_ready[a], 1)

            def prime(a, idx):
                for p in range(2):
                    prepare_half(a, idx, p, p, HALF)

            def prepare(a, idx):
                with dve.Fori(1, LOOPS) as j:
                    for p in range(2):
                        prepare_half(a, idx, j * 2 + p, p, HALF)
                prepare_half(a, idx, 2 * LOOPS, 0, REST)

            def over(v, g=slice(0, NB)):
                return v[:, g, None].to_broadcast([P, g.stop - g.start, D])

            halves_of = stats[:].rearrange("p b (h v) -> p b h v", h=2)
            loops_done, norms_done = [0], [0]

            def grouped(step):
                with dve.Fori(0, GROUPS) as i:
                    for k in range(GB):
                        last = step(i * GB + k, (i * GB + k) * D)
                    last.then_inc(ln_groups, 1)
                loops_done[0] += GROUPS
                dve.wait_ge(ln_groups, loops_done[0])

            def moments(v, count):
                flat = v[:].rearrange("p b f -> p (b f)")
                grouped(lambda b, c: V.bn_stats(stats[:].rearrange("p b v -> p (b v)")[:, ds(b * 6, 6)], flat[:, ds(c, D)]))
                V.tensor_tensor(mean[:], halves_of[:, :, 0, 1], halves_of[:, :, 1, 1], ALU.add)
                V.tensor_tensor(rstd[:], halves_of[:, :, 0, 1], halves_of[:, :, 1, 1], ALU.subtract)
                then(V.tensor_tensor(var[:], halves_of[:, :, 0, 2], halves_of[:, :, 1, 2], ALU.add))
                V.tensor_scalar(mean[:], mean[:], 0.5, None, ALU.mult)
                V.tensor_scalar(var[:], var[:], 1.0 / D, EPS, ALU.mult, ALU.add)
                then(V.scalar_tensor_tensor(rstd[:], rstd[:], 0.25, rstd[:], ALU.mult, ALU.mult))
                V.tensor_tensor(var[:], var[:], rstd[:], ALU.add).then_inc(ln_var, 1)
                dve.wait_ge(ln_std, count)
                then(V.reciprocal(rstd[:], rstd[:]))

            def normalize(src_, dst_, count):
                moments(src_, count)

                def centre(g):
                    return V.tensor_tensor(dst_[:, g, :], src_[:, g, :], over(mean, g), ALU.subtract)

                def scale(g):
                    return V.tensor_tensor(dst_[:, g, :], dst_[:, g, :], over(rstd, g), ALU.mult)

                groups = [slice(i * GB, (i + 1) * GB) for i in range(GROUPS)]
                for i in range(GROUPS + 1):
                    if i < GROUPS:
                        centre(groups[i]).then_inc(centred, 1)
                    if i:
                        dve.wait_ge(centred, norms_done[0] * GROUPS + i)
                        scale(groups[i - 1]).then_inc(ln_groups, 1)
                norms_done[0] += 1
                loops_done[0] += GROUPS
                dve.wait_ge(ln_groups, loops_done[0])

            def signal(s):
                V.engine_nop().then_inc(s, 1)

            flat_acc = acc[:, 0:NB * D].rearrange("p (b f) -> p b f", f=D)

            def projected(q, bias):
                V.engine_nop().then_inc(product_read[q], 1)
                with dve.Fori(0, GROUPS) as i:
                    for k in range(GB):
                        dve.wait_ge(product_ready[q], i * GB + k + 2)
                        to = Y[:, ds(i * GB + k, 1), :]
                        V.tensor_tensor(to, acc[:, (2 + k % 2) * 512:(2 + k % 2) * 512 + P][:, None, :], to if bias is None else bias[:, None, :],
                                        ALU.add).then_inc(product_read[q], 1)

            first_sum = hout[:, 1, 0:QU * P].rearrange("p (k e) -> p k e", e=P)

            def sources_quarter(q, s, n):
                p = s % 2
                dve.wait_ge(rows_summed, q + 1)
                dve.wait_ge(rel_src_loaded[p], (q - p) * 16 + 32)
                V.tensor_scalar(onehot_t[:, p, 0:n * P], rel_bc[:, p, 0:n * P], iota_part[:, 0:1], None, ALU.is_equal).then_inc(spread_hot_ready, 1)
                V.tensor_tensor(onehot[:, p, 0:n, :], src_bc[:, p, 0:n * P].rearrange("p (k e) -> p k e", e=P),
                                idx_src[:, ds(q * QU, n), None].to_broadcast([P, n, P]), ALU.is_equal).then_inc(same_source_ready, 1)
                dve.wait_ge(same_source_ready, q + 1)
                V.tensor_tensor(first_sum[:, 0:n, :], onehot[:, p, 0:n, :], before[:, None, :].to_broadcast([P, n, P]), ALU.mult).then_inc(repeat_step, 1)
                V.tensor_scalar(to_spare[:, 0:n], idx_src[:, ds(q * QU, n)], -1.0, spare_row[:, 0:1], ALU.mult, ALU.add)
                dve.wait_ge(repeat_step, q * 3 + 1)
                V.tensor_reduce(dup[:, 0:n], first_sum[:, 0:n, :], AX.X, ALU.add).then_inc(repeat_step, 1)
                dve.wait_ge(repeat_step, q * 3 + 2)
                V.scalar_tensor_tensor(dup[:, 0:n], dup[:, 0:n], 0.0, to_spare[:, 0:n], ALU.is_gt, ALU.mult).then_inc(repeat_step, 1)
                dve.wait_ge(repeat_step, q * 3 + 3)
                dve.wait_ge(row_free, q + 1)
                V.tensor_tensor(idx_quarter[:, s, 0:n], dup[:, 0:n], idx_src[:, ds(q * QU, n)], ALU.add).then_inc(scatter_idx_ready, 1)

            with dve.Fori(0, QLOOPS) as j:
                for s in range(4):
                    sources_quarter(j * 4 + s, s, QU)
            sources_quarter(4 * QLOOPS, 0, QU)
            sources_quarter(4 * QLOOPS + 1, 1, QREST - QU)
            dve.wait_ge(nodes_loaded, 32)
            dve.wait_ge(vectors_loaded, 160)
            dve.wait_ge(part_sum_zeroed, 16 * 2 * QU)
            V.tensor_tensor(Y[:], X[:], B0[:, None, :].to_broadcast([P, NB, D]), ALU.add)
            dve.wait_ge(part_loaded[0], 16)
            V.engine_nop().then_inc(parts_added, 1)
            for k in range(1, QU):
                dve.wait_ge(part_loaded[k], 16)
                V.tensor_tensor(T[:], T[:], part_slot[k], ALU.add).then_inc(parts_added, 1)
                dve.wait_ge(parts_added, k + 1)
            projected(4, None)
            dve.wait_ge(product_read[4], NB + 1)
            normalize(Y, X, 1)
            V.engine_nop().then_inc(product_read[0], 1)
            with dve.Fori(0, GROUPS) as i:
                for k in range(GB):
                    dve.wait_ge(product_ready[0], i * GB + k + 2)
                    dve.wait_ge(products_stored[k], i * 16 + 16)
                    V.tensor_tensor(h_slot[k], acc[:, (k % 2 + 1) * R * D:(k % 2 + 2) * R * D], B1[:], ALU.add).then_inc(product_read[0], 1)

            prime(1, idx_rel)
            for k in range(2, GB):
                dve.wait_ge(products_stored[k], 16 * (1 + GROUPS))
            V.tensor_copy(T[:], X[:]).then_inc(x_copied, 1)
            dve.wait_ge(x_copied, 1)
            then(V.tensor_tensor(X[:], X[:], BE[:, None, :].to_broadcast([P, NB, D]), ALU.add))
            prepare(1, idx_rel)
            dve.wait_ge(half_done[1], 2 + HALVES)
            V.tensor_copy(deg[:], acc[:, SIDE:SIDE + NB])
            then(V.tensor_tensor(Y[:], T[:], flat_acc, ALU.add))
            signal(sums_read[1])
            moments(Y, 2)
            then(V.tensor_tensor(Y[:], Y[:], over(mean), ALU.subtract))
            then(V.tensor_tensor(Y[:], Y[:], over(rstd), ALU.mult))
            then(V.tensor_tensor(Y[:], Y[:], GA[:, None, :].to_broadcast([P, NB, D]), ALU.mult))
            then(V.tensor_tensor(Y[:], Y[:], X[:], ALU.add))
            normalize(Y, X, 3)
            then(V.tensor_scalar(rdeg[:], deg[:], 1.0, None, ALU.max))
            then(V.reciprocal(rdeg[:], rdeg[:]))
            then(V.tensor_scalar(has[:], deg[:], 0.0, None, ALU.is_gt))

            for a, bias in ((2, B21), (3, B22)):
                prime(a, idx_src)
                projected(a - 1, bias)
                if a == 3:
                    dve.wait_ge(product_read[a - 1], NB + 1)
                    then(V.tensor_tensor(Y[:], Y[:], X[:], ALU.add))
                prepare(a, idx_src)
                dve.wait_ge(node_product_ready[a], GROUPS)
                dve.wait_ge(product_read[a - 1], NB + 1)
                then(V.tensor_tensor(T[:], flat_acc, over(rdeg), ALU.mult))
                signal(sums_read[a])
                if a == 2:
                    then(V.tensor_tensor(T[:], T[:], Y[:], ALU.add))
                    then(V.tensor_scalar(T[:], T[:], 0.0, None, ALU.max))
                    signal(x_ready[2])
                else:
                    then(V.tensor_tensor(Y[:], T[:], Y[:], ALU.add))
                    normalize(Y, X, 4)

            projected(3, WB)
            dve.wait_ge(product_read[3], NB + 1)
            for A, s in ((A_SRC, s_src), (A_DST, s_dst)):
                then(V.tensor_tensor(T[:], Y[:], A[:].rearrange("p h f -> p (h f)")[:, None, :].to_broadcast([P, NB, D]), ALU.mult))
                then(V.tensor_reduce(s[:].rearrange("p b h -> p (b h)"), T[:].rearrange("p b (h f) -> p (b h) f", h=H), AX.X, ALU.add))
            then(V.tensor_tensor(s_dst[:], s_dst[:], AB[:, None, :].to_broadcast([P, NB, H]), ALU.add))
            signal(scores_ready)
            dve.wait_ge(degrees_summed, 1)
            V.tensor_copy(block_sum[:], aux[:, P:P + NB])
            then(V.memset(block_cum[:, 0:1], 0.0))
            then(V.tensor_tensor_scan(block_cum[:, 1:NB + 1], zeros[:, 0:NB], block_sum[:], 0.0, ALU.add, ALU.add))
            then(V.tensor_tensor(ends[:], aux[:, 0:NB], block_cum[:, 0:NB], ALU.add))
            then(V.scalar_tensor_tensor(ends[:], ends[:], -1.0, block_base[:], ALU.add, ALU.add))
            then(V.tensor_scalar(ends[:], ends[:], 0.0, None, ALU.max))
            V.tensor_copy(ends_i[:], ends[:]).then_inc(ends_ready, 1)

            V.memset(edge_score[:, STEPS:SLOTS, :], 0.0)
            hi_i = raw[:, 0, :]
            then(V.tensor_scalar(hi_i, idx_src[:], 7, None, ALU.arith_shift_right))
            then(V.tensor_copy(src_block[:], hi_i))
            for _ in range(2):
                V.engine_nop().then_inc(place_scores_read, 1)

            def place_hot(it, j, p, n):
                dve.wait_ge(places_loaded[p], j * 16 + 16)
                V.tensor_scalar(onehot_t[:, p, 0:n * P], rel_bc[:, p, 0:n * P], iota_part[:, 0:1], None, ALU.is_equal).then_inc(place_hot_ready, 1)

            def choose_half(it, p, n):
                in_block = onehot[:, p, :, 0:NB]
                chosen = msg[:, p, :, 0:NB * H].rearrange("p k (b h) -> p k b h", h=H)
                V.tensor_tensor(in_block[:, 0:n, :], step_no_block[:, None, :].to_broadcast([P, n, NB]),
                                src_block[:, ds(it * HALF, n), None].to_broadcast([P, n, NB]), ALU.is_equal).then_inc(choice_step, 1)
                dve.wait_ge(choice_step, it * 2 + 1)
                dve.wait_ge(place_scores_ready, it + 1)
                for c in range(0, n, QU):
                    m = min(QU, n - c)
                    bank = acc[:, (2 * p + c // QU) * 512:(2 * p + c // QU) * 512 + m * NB * H].rearrange("p (k b h) -> p k b h", b=NB, h=H)
                    last = V.tensor_tensor(chosen[:, c:c + m], bank, in_block[:, c:c + m, :, None].to_broadcast([P, m, NB, H]), ALU.mult)
                last.then_inc(place_scores_read, 1)
                dve.wait_ge(place_scores_read, it + 3)
                V.tensor_reduce(edge_score[:, ds(it * HALF, n), :], chosen[:, 0:n].rearrange("p k b h -> p k h b"), AX.X, ALU.add).then_inc(choice_step, 1)

            place_hot(0, 0, 0, HALF)
            place_hot(1, 0, 1, HALF)
            with dve.Fori(0, LOOPS - 1) as j:
                for p in range(2):
                    choose_half(j * 2 + p, p, HALF)
                    place_hot(j * 2 + p + 2, j + 1, p, HALF)
            choose_half(2 * LOOPS - 2, 0, HALF)
            place_hot(2 * LOOPS, LOOPS, 0, REST)
            choose_half(2 * LOOPS - 1, 1, HALF)
            choose_half(2 * LOOPS, 0, REST)
            dve.wait_ge(choice_step, 2 * HALVES)
            signal(edge_scores_ready)
            then(V.tensor_scalar(invalid_pen[:], valid[:], 1.0, BIG, ALU.subtract, ALU.mult))
            dve.wait_ge(columns_turned, 1 + H)
            for h in range(H):
                then(V.tensor_tensor(score_row[:, h], cols[:, :, h, :], valid[:], ALU.mult))
                then(V.tensor_tensor(score_row[:, h], score_row[:, h], invalid_pen[:], ALU.add))
            signal(score_rows_ready)
            dve.wait_ge(lanes_loaded, 16 * (H + 1))
            for h in range(H):
                V.tensor_tensor_scan(prefix[:, :, h], lane_reset, lanes[:, h, :], -BIG, ALU.add, ALU.max)
            then(V.tensor_reduce(lane_flag[:], lane_reset, AX.X, ALU.min))
            then(V.tensor_copy(lane_flag_h[:], lane_flag[:, 0:1].to_broadcast([P, H])))
            V.tensor_copy(lane_tail[:], prefix[:, STEPS - 1, :]).then_inc(tails_ready, 1)
            dve.wait_ge(tails_turned, 1)
            then(V.tensor_copy(carry_rst[:], aux[0:H, P:2 * P]))
            then(V.tensor_tensor_scan(carry[:, 1:P + 1], carry_rst[:], aux[0:H, 0:P], -BIG, ALU.add, ALU.max))
            V.engine_nop().then_inc(carry_ready, 1)
            dve.wait_ge(carry_turned, 1)
            then(V.tensor_copy(carry_col[:], aux[:, 2 * P:2 * P + H]))
            for h in range(H):
                then(V.tensor_tensor_scan(prefix[:, :, h], lane_reset, lanes[:, h, :], carry_col[:, h:h + 1], ALU.add, ALU.max))
            V.engine_nop().then_inc(prefix_ready, 1)
            dve.wait_ge(in_max_loaded, 16 * NB)
            hasb = has[:, :, None].to_broadcast([P, NB, H])
            then(V.tensor_tensor(in_max[:], in_max[:], hasb, ALU.mult))
            then(V.tensor_scalar(den[:], hasb, 1.0, BIG, ALU.subtract, ALU.mult))
            then(V.tensor_tensor(in_max[:], in_max[:], den[:], ALU.add))
            then(V.tensor_tensor(e_max[:], in_max[:], s_src[:], ALU.max))
            then(V.tensor_tensor(e_max[:], e_max[:], s_dst[:], ALU.add))
            then(V.scalar_tensor_tensor(e_max[:], e_max[:], 0.2, e_max[:], ALU.mult, ALU.max))
            then(V.tensor_tensor(e_self[:], s_src[:], s_dst[:], ALU.add))
            then(V.scalar_tensor_tensor(e_self[:], e_self[:], 0.2, e_self[:], ALU.mult, ALU.max))
            then(V.tensor_tensor(e_tmp[:], e_self[:], e_max[:], ALU.subtract))
            V.tensor_copy(node_vals[:, :, 0:H], s_dst[:])
            then(V.tensor_copy(node_vals[:, :, H:2 * H], e_max[:]))
            then(V.tensor_copy(node_parts[:, :, 0], node_vals[:]))
            then(V.tensor_tensor(node_rest[:], node_vals[:], node_parts[:, :, 0], ALU.subtract))
            then(V.tensor_copy(node_parts[:, :, 1], node_rest[:]))
            then(V.tensor_tensor(node_parts[:, :, 2], node_rest[:], node_parts[:, :, 1], ALU.subtract))
            signal(self_exponent_ready)

            def turned_hot(turn, j, p):
                dve.wait_ge(rel_loaded[p], j * 16 + 16)
                V.tensor_scalar(hot_t[:, p, :], rel_bc[:, p, :], iota_part[:, 0:1], None, ALU.is_equal).then_inc(turned_hot_ready, 1)

            def attend(turn, half, p, arrived, count, keys, more=None):
                dve.wait_ge(half_done[4], turn + 1)
                V.tensor_tensor(onehot[:, p], iota_row[:, None, :].to_broadcast([P, HALF, P]),
                                rel_col[:, ds(half * HALF, HALF), None].to_broadcast([P, HALF, P]), ALU.is_equal).then_inc(onehot_ready[4], 1)
                dve.wait_ge(expanded, turn + 2)
                three = aux[:, p * HALF * 6 * H:(p + 1) * HALF * 6 * H].rearrange("p (k r v) -> p k v r", r=3, v=2 * H)
                V.tensor_reduce(dest_vals[:], three, AX.X, ALU.add).then_inc(dest_vals_read, 1)
                dve.wait_ge(dest_vals_read, turn + 1)
                V.tensor_tensor(z_slot[:], dest_vals[:, :, 0:H], edge_score[:, ds(half * HALF, HALF), :], ALU.add).then_inc(z_step, 1)
                dve.wait_ge(z_step, turn * 3 + 1)
                V.scalar_tensor_tensor(z_slot[:], z_slot[:], 0.2, z_slot[:], ALU.mult, ALU.max).then_inc(z_step, 1)
                dve.wait_ge(z_step, turn * 3 + 2)
                V.tensor_tensor(z_slot[:], z_slot[:], dest_vals[:, :, H:2 * H], ALU.subtract).then_inc(z_step, 1)
                dve.wait_ge(z_step, turn * 3 + 3)
                V.tensor_scalar(u_slot[:, p], z_slot[:], 0.0, None, ALU.min).then_inc(exponent_ready, 1)
                if more is not None:
                    turned_hot(turn + 1, more, 1 - p)
                dve.wait_ge(prob_ready, turn + 1)
                dve.wait_ge(arrived, count)
                V.tensor_tensor(msg[:, p].rearrange("p k (h f) -> p (k h) f", h=H), keys.rearrange("p k (h f) -> p (k h) f", h=H),
                                prob[:, p].rearrange("p k h -> p (k h)")[:, :, None].to_broadcast([P, HALF * H, D // H]),
                                ALU.mult).then_inc(msg_ready, 1)
                dve.wait_ge(first_part_ready, turn + 1)
                V.tensor_tensor(prob_rest[:], prob[:, p], prob_parts[:, p, :, 0], ALU.subtract).then_inc(rest_step, 1)
                dve.wait_ge(rest_step, turn * 2 + 1)
                V.tensor_copy(prob_parts[:, p, :, 1], prob_rest[:]).then_inc(rest_step, 1)
                dve.wait_ge(rest_step, turn * 2 + 2)
                V.tensor_tensor(prob_parts[:, p, :, 2], prob_rest[:], prob_parts[:, p, :, 1], ALU.subtract).then_inc(parts_ready, 1)

            turned_hot(0, 0, 0)
            dve.wait_ge(self_prob_ready, 1)
            V.tensor_tensor(Y[:].rearrange("p b (h f) -> p (b h) f", h=H), Y[:].rearrange("p b (h f) -> p (b h) f", h=H),
                            p_self[:].rearrange("p b h -> p (b h)")[:, :, None].to_broadcast([P, NB * H, D // H]), ALU.mult)
            with dve.Fori(0, STASHED // 2) as j:
                for s in range(2):
                    attend(j * 4 + 2 * s, j * 2 + (STASHED + s), 0, gathered[4][s], (j + STASHED // 2) * (16 * HALF) + 16 * HALF, rows[:, s], more=j * 2 + s)
                    attend(j * 4 + (2 * s + 1), j * 2 + s, 1, stash_in[s], j * 16 + 16, stash_rows[:, s], more=j * 2 + (s + 1))
            attend(2 * STASHED, HALVES - 1, 0, gathered[4][0], (STASHED + 1) * 16 * HALF, rows[:, 0])
            dve.wait_ge(half_done[4], 2 + HALVES)
            V.tensor_tensor(Y[:], Y[:], flat_acc, ALU.add)
            then(V.tensor_reduce(den[:], acc[:, SIDE:SIDE + NB * 3 * H].rearrange("p (b r h) -> p b h r", r=3, h=H), AX.X, ALU.add))
            then(V.tensor_tensor(den[:], den[:], p_self[:], ALU.add))
            then(V.reciprocal(den[:], den[:]))
            then(V.tensor_tensor(Y[:].rearrange("p b (h f) -> p (b h) f", h=H), Y[:].rearrange("p b (h f) -> p (b h) f", h=H),
                                 den[:].rearrange("p b h -> p (b h)")[:, :, None].to_broadcast([P, NB * H, D // H]), ALU.mult))
            then(V.tensor_tensor(Y[:], Y[:], X[:], ALU.add))
            normalize(Y, X, 5)
            signal(result_ready)

        @block.tensor
        def _(pe):
            M = nc.tensor
            pe.wait_ge(constants_ready, 2)
            pe.wait_ge(weights_loaded, 16 * 7)
            for r in range(R):
                last = M.transpose(acc[:, r * D:(r + 1) * D], W1[:, r, :], ident[:])
            last.then_inc(w1_turned, 1)
            pe.wait_ge(counts_ready, 1)
            M.matmul(aux[:, 0:NB - 1], ones[:], below[:], start=True, stop=True).then_inc(counts_summed, 1)
            pe.wait_ge(w1_turned, 2)
            pe.wait_ge(step_rows_ready, 1)
            fields = step_rec[:, :, 0:4 * P].rearrange("p g (f e) -> p g f e", f=4)
            for g in range(G):
                for f, row in enumerate((fields[:, g, 0, :], fields[:, g, 1, :], rel_row[:, g, :], fields[:, g, 3, :])):
                    last = M.transpose(acc[:, (g * 4 + f) * P:(g * 4 + f + 1) * P], row, ident[:])
            last.then_inc(columns_turned, 1)
            pe.wait_ge(columns_ready, 1)
            pe.wait_ge(block_row_loaded, 16)

            def clear():
                for k in range(7):
                    M.matmul(acc[:, k * 512:(k + 1) * 512], zeros[:, 0:P], zeros[:], start=True, stop=True)

            def begin(a):
                for _ in range(2):
                    pe.nop().then_inc(half_done[a], 1)

            def aggregate(a, transposed, side=False):
                def half(it, j, p, n):
                    _, blk = nc.values_load_multi_w_load_instructions(
                        block_row[0:1, ds(it * HALF, n)], engines=[pe.engine], min_val=0, max_val=NB - 1,
                        skip_runtime_bounds_check_because="a step's block counts which of the NB - 1 others lie before it")
                    pe.wait_ge(onehot_ready[a], it + 1)
                    pe.wait_ge(gathered[a][p], j * 16 * HALF + 16 * n)
                    for k in range(n):
                        lhs, rhs = onehot[:, p, k, :], rows[:, p, k, :]
                        if transposed:
                            lhs, rhs = rhs, lhs
                        last = M.matmul(acc[:, ds(blk[k] * D, D)], lhs, rhs, start=False, stop=True, skip_group_check=True)
                        if side:
                            last = M.matmul(acc[:, ds(blk[k] + SIDE, 1)], lhs, ones[:, 0:1], start=False, stop=True, skip_group_check=True)
                    last.then_inc(half_done[a], 1)

                with pe.Fori(0, LOOPS) as j:
                    for p in range(2):
                        half(j * 2 + p, j, p, HALF)
                half(2 * LOOPS, LOOPS, 0, REST)

            def node_product(a, W):
                for i in range(GROUPS):
                    pe.wait_ge(lhs_ready[a], min(i + 2, GROUPS))
                    for k in range(GB):
                        b = i * GB + k
                        last = M.matmul(acc[:, b * D:(b + 1) * D], (lhs_slot, nat_slot)[i % 2][:, k, :], W[:], start=True, stop=True)
                    last.then_inc(node_product_ready[a], 1)

            def project(q, W, wide=False):
                pe.nop().then_inc(block_turned[q], 1)
                pe.nop().then_inc(product_ready[q], 1)
                with pe.Fori(0, GROUPS) as i:
                    pe.wait_ge(group_copied[q], i + 1)

                    def turn(k):
                        pe.wait_ge(lhs_copied[q], i * GB + max(k, 1))
                        M.transpose(acc[:, (k % 2) * 512:(k % 2) * 512 + P], nat_slot[:, k, :], ident[:]).then_inc(block_turned[q], 1)

                    turn(0)
                    for k in range(GB):
                        if k + 1 < GB:
                            turn(k + 1)
                        pe.wait_ge(lhs_copied[q], i * GB + k + 2)
                        pe.wait_ge(product_read[q], i * GB + max(k, 1))
                        if wide:
                            for c in range(2):
                                last = M.matmul(acc[:, (k % 2 + 1) * R * D + c * 512:(k % 2 + 1) * R * D + (c + 1) * 512],
                                                lhs_slot[:, k % 2, :], W[:, c * 512:(c + 1) * 512], start=True, stop=True)
                        else:
                            last = M.matmul(acc[:, (2 + k % 2) * 512:(2 + k % 2) * 512 + P], lhs_slot[:, k % 2, :], W[:], start=True, stop=True)
                        last.then_inc(product_ready[q], 1)

            def weighted_quarter(q, p, n):
                _, blk = nc.values_load_multi_w_load_instructions(
                    block_row[0:1, ds(q * QU, n)], engines=[pe.engine], min_val=0, max_val=NB - 1,
                    skip_runtime_bounds_check_because="a step's block counts which of the NB - 1 others lie before it")
                pe.wait_ge(spread_hot_ready, q + 1)
                for k in range(n):
                    last = M.matmul(acc[:, p * 512 + k * D:p * 512 + (k + 1) * D], onehot_t[:, p, k * P:(k + 1) * P],
                                    X[:].rearrange("p b f -> p (b f)")[:, ds(blk[k] * D, D)], start=True, stop=True)
                last.then_inc(rows_spread, 1)
                pe.wait_ge(weighted, q + 1)
                pe.wait_ge(same_source_ready, q + 1)
                pe.wait_ge(sum_ready, q + 1)
                for k in range(n):
                    last = M.matmul(acc[:, (2 + p) * 512 + k * D:(2 + p) * 512 + (k + 1) * D], onehot[:, p, k, :], rows[:, p, k, :],
                                    start=True, stop=True)
                last.then_inc(rows_summed, 1)

            pe.wait_ge(nodes_loaded, 32)
            for _ in range(2):
                pe.nop().then_inc(rows_summed, 1)
            with pe.Fori(0, 2 * QLOOPS) as j:
                for p in range(2):
                    weighted_quarter(j * 2 + p, p, QU)
            weighted_quarter(4 * QLOOPS, 0, QU)
            weighted_quarter(4 * QLOOPS + 1, 1, QREST - QU)
            project(4, W0)
            pe.wait_ge(product_read[4], NB + 1)
            project(0, W1T, wide=True)
            pe.wait_ge(product_read[0], NB + 1)
            begin(1)
            clear()
            aggregate(1, False, side=True)
            pe.wait_ge(sums_read[1], 1)
            begin(2)
            project(1, WS1)
            pe.wait_ge(product_read[1], NB + 1)
            clear()
            aggregate(2, True)
            node_product(2, WN1)
            pe.wait_ge(sums_read[2], 1)
            begin(3)
            project(2, WS2)
            pe.wait_ge(product_read[2], NB + 1)
            clear()
            aggregate(3, True)
            node_product(3, WN2)
            pe.wait_ge(sums_read[3], 1)
            project(3, WW)
            pe.wait_ge(product_read[3], NB + 1)
            M.matmul(aux[:, 0:NB], upto[:], deg[:], start=True, stop=True)
            M.matmul(aux[:, P:P + NB], ones[:], deg[:], start=True, stop=True).then_inc(degrees_summed, 1)
            def score_half(it, p, n):
                pe.wait_ge(place_hot_ready, it + 1)
                pe.wait_ge(place_scores_read, it + 1)
                for k in range(n):
                    col = (2 * p + k // QU) * 512 + k % QU * NB * H
                    last = M.matmul(acc[:, col:col + NB * H], onehot_t[:, p, k * P:(k + 1) * P],
                                    s_src[:].rearrange("p b h -> p (b h)"), start=True, stop=True)
                last.then_inc(place_scores_ready, 1)

            pe.wait_ge(scores_ready, 1)
            with pe.Fori(0, LOOPS) as j:
                for p in range(2):
                    score_half(j * 2 + p, p, HALF)
            score_half(2 * LOOPS, 0, REST)
            pe.wait_ge(edge_scores_ready, 1)
            for h in range(H):
                for g in range(G):
                    last = M.transpose(acc[:, (g * 4 + h) * P:(g * 4 + h + 1) * P], edge_score[:, g * P:(g + 1) * P, h], ident[:])
                last.then_inc(columns_turned, 1)
            pe.wait_ge(tails_ready, 1)
            M.transpose(aux[0:H, 0:P], lane_tail[:], ident[:])
            M.transpose(aux[0:H, P:2 * P], lane_flag_h[:], ident[:]).then_inc(tails_turned, 1)
            pe.wait_ge(carry_ready, 1)
            M.transpose(aux[:, 2 * P:2 * P + H], carry[:, 0:P], ident[0:H, 0:H]).then_inc(carry_turned, 1)
            pe.wait_ge(score_rows_ready, 1)
            begin(4)
            clear()
            pe.wait_ge(self_exponent_ready, 1)

            def blocks(half):
                _, blk = nc.values_load_multi_w_load_instructions(
                    block_row[0:1, ds(half * HALF, HALF)], engines=[pe.engine], min_val=0, max_val=NB - 1,
                    skip_runtime_bounds_check_because="a step's block counts which of the NB - 1 others lie before it")
                return blk

            def expand(turn, blk, p):
                pe.wait_ge(turned_hot_ready, turn + 1)
                for k in range(HALF):
                    col = (p * HALF + k) * 6 * H
                    last = M.matmul(aux[:, col:col + 6 * H], hot_t[:, p, k * P:(k + 1) * P],
                                    node_parts[:].rearrange("p b r v -> p (b r v)")[:, ds(blk[k] * (6 * H), 6 * H)], start=True, stop=True)
                last.then_inc(expanded, 1)

            def attend(turn, blk, p):
                pe.wait_ge(onehot_ready[4], turn + 1)
                pe.wait_ge(msg_ready, turn + 1)
                for k in range(HALF):
                    M.matmul(acc[:, ds(blk[k] * D, D)], onehot[:, p, k, :], msg[:, p, k, :], start=False, stop=True, skip_group_check=True)
                pe.wait_ge(hot_ready, turn + 1)
                pe.wait_ge(parts_ready, turn + 1)
                for k in range(HALF):
                    last = M.matmul(acc[:, ds(blk[k] * (3 * H) + SIDE, 3 * H)], hot[:, p, k, :],
                                    prob_parts[:, p, k].rearrange("p r h -> p (r h)"), start=False, stop=True, skip_group_check=True)
                last.then_inc(half_done[4], 1)

            pe.nop().then_inc(expanded, 1)
            expand(0, blocks(STASHED), 0)
            with pe.Fori(0, STASHED) as j:
                ahead, now = blocks(j), blocks(j + STASHED)
                pe.wait_ge(dest_vals_read, j * 2 + 1)
                expand(j * 2 + 1, ahead, 1)
                attend(j * 2, now, 0)
                ahead, now = blocks(j + (STASHED + 1)), blocks(j)
                pe.wait_ge(dest_vals_read, j * 2 + 2)
                expand(j * 2 + 2, ahead, 0)
                attend(j * 2 + 1, now, 1)
            attend(2 * STASHED, blocks(HALVES - 1), 0)


_INS = ['x', 'src', 'dst', 'edge_type_8', 'edge_weight', 'L0_gnn_weight', 'L0_gnn_bias', 'L1_gnn_W', 'L1_gnn_b',
        'L1_gnn_gamma', 'L1_gnn_beta', 'L2_gnn_Wself1', 'L2_gnn_Wneigh1', 'L2_gnn_b1', 'L2_gnn_Wself2',
        'L2_gnn_Wneigh2', 'L2_gnn_b2', 'L3_gnn_W_w', 'L3_gnn_W_b', 'L3_gnn_a_w', 'L3_gnn_a_b']


def kernel(**inputs):
    import numpy as _np
    import concourse.bacc as _bacc
    from concourse import mybir as _mybir
    from concourse.bass_utils import run_bass_kernel_spmd as _run

    nc = _bacc.Bacc("TRN2", target_bir_lowering=False, num_devices=1)
    arrays, args = {}, []
    for name in _INS:
        a = _np.ascontiguousarray(inputs[name])
        arrays[f"in_{name}_dram"] = a
        args.append(nc.dram_tensor(f"in_{name}_dram", a.shape, _mybir.dt.from_np(a.dtype), kind="ExternalInput").ap())
    args.append(nc.dram_tensor("out_0_dram", (N, D), _mybir.dt.float32, kind="ExternalOutput").ap())
    gnn_kernel(nc, *args)
    r = _run(nc, [arrays], core_ids=[0])
    return r.results[0]["out_0_dram"]
```
